# Optimizing a Trainium2 kernel written in Bass

```python
import numpy as np
import jax
import jax.numpy as jnp

def _softmax(x, axis=-1):
    return jax.nn.softmax(x, axis=axis)

def _gelu(x):
    return jax.nn.gelu(x, approximate=True)

def _silu(x):
    return jax.nn.silu(x)

def _sigmoid(x):
    return jax.nn.sigmoid(x)

def _layernorm(x, axis=-1, eps=1e-05):
    m = jnp.mean(x, axis=axis, keepdims=True)
    v = jnp.var(x, axis=axis, keepdims=True)
    return (x - m) / jnp.sqrt(v + eps)

def _scatter_add(tgt, idx, src, axis=0):
    return tgt.at[idx].add(src)

def _segment_sum(src, seg, n):
    return jax.ops.segment_sum(src, seg, n)
kernel_name = 'mk_decoder_postln_d2_seqx_r8_1f9e40'

def setup_inputs(seed: int=0):
    np.random.seed(seed)
    _w = jnp.asarray

    def _rec_inputs():
        import jax
        import jax.numpy as jnp
        _rk = jax.random.key(seed)
        x = -7.109e-05 + 0.9999 * jax.random.normal(jax.random.fold_in(_rk, 1), (4, 256, 256), jnp.float32)
        _lenS = 256 - jax.random.randint(jax.random.fold_in(_rk, 7), (4,), 0, max(1, 256 // 4) + 1, jnp.int32)
        _lenS2 = 256 - jax.random.randint(jax.random.fold_in(_rk, 8), (4,), 0, max(1, 256 // 4) + 1, jnp.int32)
        _ctx_512P = jax.random.normal(jax.random.fold_in(_rk, 11), (4, 16, 64), jnp.float32)
        _ctx_512c = jax.random.dirichlet(jax.random.fold_in(_rk, 511), 0.3 * jnp.ones((16,), jnp.float32), (4, 256))
        _ctx_512t = jnp.einsum('bsk,bkd->bsd', _ctx_512c, _ctx_512P)
        _ctx_512t = _ctx_512t * jax.lax.rsqrt(jnp.mean(jnp.square(_ctx_512t)) + 1e-12) * 0.953939
        ctx_512 = 2.81802e-05 + 1.00001 * (_ctx_512t + 0.3 * jax.random.normal(jax.random.fold_in(_rk, 611), (4, 256, 64), jnp.float32))
        return (x, ctx_512)
    x, ctx_512 = _rec_inputs()

    def _L0_attn_setup():
        import jax, jax.numpy as jnp
        import numpy as np
        B, T, C = (1, 512, 256)
        H = 16
        D = C // H
        BLOCK = 64
        WINDOW = 128
        DILATION = 32
        GLOBAL_TOKENS = 128
        ROPE_BASE = 10000.0
        SCALE = 1.0 / np.sqrt(D)

        def _rope(x):
            t = jnp.arange(x.shape[2], dtype=jnp.float32)
            inv_freq = 1.0 / ROPE_BASE ** (jnp.arange(0, D, 2, dtype=jnp.float32) / D)
            freqs = jnp.outer(t, inv_freq)
            emb = jnp.concatenate([freqs, freqs], axis=-1)
            cos = jnp.cos(emb)[None, None].astype(x.dtype)
            sin = jnp.sin(emb)[None, None].astype(x.dtype)
            x1, x2 = jnp.split(x, 2, axis=-1)
            rot = jnp.concatenate([-x2, x1], axis=-1)
            return x * cos + rot * sin

        def _token_mask(seq_len):
            nb = (seq_len + BLOCK - 1) // BLOCK
            bp = jnp.arange(nb)
            qb, kb = (bp[:, None], bp[None, :])
            dist = qb - kb
            window_blocks = WINDOW // BLOCK
            window_mask = (dist >= 0) & (dist <= window_blocks)
            global_blocks = max(1, GLOBAL_TOKENS // BLOCK)
            global_mask = kb < global_blocks
            dilation_blocks = max(1, DILATION // BLOCK)
            dilated_mask = kb % dilation_blocks == 0
            causal_mask = kb <= qb
            block_mask = (window_mask | global_mask | dilated_mask) & causal_mask
            tok = jnp.repeat(jnp.repeat(block_mask, BLOCK, axis=0), BLOCK, axis=1)
            return tok[:seq_len, :seq_len]
        key = jax.random.key(seed)
        ks = jax.random.split(key, 5)
        x = jax.random.normal(ks[0], (B, T, C), dtype=jnp.float32)
        w_q = jax.random.normal(ks[1], (C, C), dtype=jnp.float32) * 0.02
        w_k = jax.random.normal(ks[2], (C, C), dtype=jnp.float32) * 0.02
        w_v = jax.random.normal(ks[3], (C, C), dtype=jnp.float32) * 0.02
        w_o = jax.random.normal(ks[4], (C, C), dtype=jnp.float32) * 0.02
        return {'x': x, 'w_q': w_q, 'w_k': w_k, 'w_v': w_v, 'w_o': w_o}
    _L0_attn_all = _L0_attn_setup()
    _L0_attn_in = {k: v for k, v in _L0_attn_all.items() if k in ('w_q', 'w_k', 'w_v', 'w_o')}
    del _L0_attn_all

    def _L0_xattn_setup():
        import jax, jax.numpy as jnp
        import numpy as np
        EPS = 1e-06
        IMAGE_DIMS = 256
        key = jax.random.key(seed)
        k1, k2, k3 = jax.random.split(key, 3)
        B, I, J, D = (16, 256, 256, 64)
        p = jax.random.normal(k1, (B, I, J), dtype=jnp.float32)
        k_v = jax.random.normal(k2, (B, J, D), dtype=jnp.float32)
        W_k = jax.random.normal(k3, (D, D), dtype=jnp.float32) * (1.0 / np.sqrt(D))
        b_k = jnp.zeros((D,), dtype=jnp.float32)
        ln_gamma = jnp.ones((J,), dtype=jnp.float32)
        ln_beta = jnp.zeros((J,), dtype=jnp.float32)
        return {'p': p, 'k_v': k_v, 'W_k': W_k, 'b_k': b_k, 'ln_gamma': ln_gamma, 'ln_beta': ln_beta}
    _L0_xattn_all = _L0_xattn_setup()
    _L0_xattn_in = {k: v for k, v in _L0_xattn_all.items() if k in ('W_k', 'b_k', 'ln_gamma', 'ln_beta')}
    del _L0_xattn_all

    def _L0_ffn_setup():
        import jax, jax.numpy as jnp
        import numpy as np
        from jax import lax
        E = 8
        K = 2
        H = 256
        I = 512
        B, S = (2, 256)
        SCALE = 0.02

        def _silu_and_mul(gu):
            g, u = jnp.split(gu, 2, axis=-1)
            return jax.nn.silu(g) * u
        key = jax.random.key(seed)
        ks = jax.random.split(key, 6)
        return {'hidden_states': jax.random.normal(ks[0], (B, S, H), dtype=jnp.float32), 'gate_w': jax.random.normal(ks[1], (H, E), dtype=jnp.float32) * SCALE, 'w_gate_up': jax.random.normal(ks[2], (E, H, 2 * I), dtype=jnp.float32) * SCALE, 'w_down': jax.random.normal(ks[3], (E, I, H), dtype=jnp.float32) * SCALE, 'shared_gate_up': jax.random.normal(ks[4], (H, 2 * I), dtype=jnp.float32) * SCALE, 'shared_down': jax.random.normal(ks[5], (I, H), dtype=jnp.float32) * SCALE}
    _L0_ffn_all = _L0_ffn_setup()
    _L0_ffn_in = {k: v for k, v in _L0_ffn_all.items() if k in ('gate_w', 'w_gate_up', 'w_down', 'shared_gate_up', 'shared_down')}
    del _L0_ffn_all

    def _L1_attn_setup():
        import jax, jax.numpy as jnp
        import numpy as np
        B, T, HID = (2, 128, 256)
        NKH, NVH, DK, DV, KS = (8, 16, 64, 128, 4)
        KD = NKH * DK
        VD = NVH * DV
        CD = 2 * KD + VD
        IPD = CD + VD + 2 * NVH
        EPS = 1e-06
        SCALE = DK ** (-0.5)

        def _l2norm(t):
            return t / jnp.maximum(jnp.linalg.norm(t, axis=-1, keepdims=True), 1e-12)

        def _forward(x, in_proj_w, conv_w, dt_bias, A_log, norm_weight, out_proj_w):
            Bb, Tt, _ = x.shape
            f32 = jnp.float32
            proj = x @ in_proj_w.T
            mixed = proj[..., :CD]
            z = proj[..., CD:CD + VD].reshape(Bb, Tt, NVH, DV)
            b = proj[..., CD + VD:CD + VD + NVH]
            a = proj[..., CD + VD + NVH:]
            xc = jnp.swapaxes(mixed, 1, 2)
            ci = jnp.pad(xc, ((0, 0), (0, 0), (KS, 0))).astype(f32)
            w = conv_w.astype(f32)
            Tc = Tt + 1
            acc = sum((ci[:, :, k:k + Tc] * w[:, k][None, :, None] for k in range(KS)))
            qkv = jnp.swapaxes(jax.nn.silu(acc[:, :, -Tt:]), 1, 2).astype(x.dtype)
            q = _l2norm(qkv[..., :KD].reshape(Bb, Tt, NKH, DK))
            k = _l2norm(qkv[..., KD:2 * KD].reshape(Bb, Tt, NKH, DK))
            v = qkv[..., 2 * KD:].reshape(Bb, Tt, NVH, DV)
            rep = NVH // NKH
            if rep > 1:
                q = jnp.repeat(q, rep, axis=2)
                k = jnp.repeat(k, rep, axis=2)
            beta = jax.nn.sigmoid(b).astype(f32)
            g = -jnp.exp(A_log.astype(f32)) * jax.nn.softplus(a.astype(f32) + dt_bias.astype(f32))
            seq = (jnp.swapaxes(q, 0, 1).astype(f32), jnp.swapaxes(k, 0, 1).astype(f32), jnp.swapaxes(v, 0, 1).astype(f32), jnp.swapaxes(g, 0, 1), jnp.swapaxes(beta, 0, 1))

            def step(state, inp):
                qt, kt, vt, gt, bt = inp
                state = state * jnp.exp(gt)[:, :, None, None]
                Sk = jnp.einsum('bhkv,bhk->bhv', state, kt)
                delta = bt[..., None] * (vt - Sk)
                state = state + jnp.einsum('bhk,bhv->bhkv', kt, delta)
                out = jnp.einsum('bhkv,bhk->bhv', state, qt) * SCALE
                return (state, out)
            state0 = jnp.zeros((Bb, NVH, DK, DV), f32)
            _, outs = jax.lax.scan(step, state0, seq)
            o = jnp.swapaxes(outs, 0, 1).reshape(-1, DV)
            zf = z.reshape(-1, DV).astype(f32)
            normed = norm_weight * (o * jax.lax.rsqrt(jnp.mean(o * o, axis=-1, keepdims=True) + EPS))
            gated = (normed * jax.nn.silu(zf)).astype(x.dtype)
            return gated.reshape(Bb, Tt, VD) @ out_proj_w.T
        key = jax.random.key(seed)
        k0, k1, k2, k3, k4 = jax.random.split(key, 5)
        return {'x': jax.random.normal(k0, (B, T, HID), jnp.float32), 'input_pos': jnp.arange(T, dtype=jnp.int32), 'in_proj_w': jax.random.normal(k1, (IPD, HID), jnp.float32) * 0.02, 'conv_w': jax.random.normal(k2, (CD, KS), jnp.float32) * 0.2, 'dt_bias': jnp.ones((NVH,), jnp.float32), 'A_log': jnp.log(jax.random.uniform(k3, (NVH,), jnp.float32, 0.5, 16.0)), 'norm_weight': jnp.ones((DV,), jnp.float32), 'out_proj_w': jax.random.normal(k4, (HID, VD), jnp.float32) * 0.02}
    _L1_attn_all = _L1_attn_setup()
    _L1_attn_in = {k: v for k, v in _L1_attn_all.items() if k in ('input_pos', 'in_proj_w', 'conv_w', 'dt_bias', 'A_log', 'norm_weight', 'out_proj_w')}
    del _L1_attn_all

    def _L1_xattn_setup():
        import jax, jax.numpy as jnp
        import numpy as np
        B, S, H, NH, L = (2, 256, 256, 16, 64)
        HD = H // NH
        key = jax.random.key(seed)
        k1, k2, k3, k4, k5 = jax.random.split(key, 5)
        scale = 0.02
        return {'q': jax.random.normal(k1, (B, S, H), dtype=jnp.float32), 'latent_kv': jax.random.normal(k2, (B, S, L), dtype=jnp.float32), 'Wq': jax.random.normal(k3, (H, H), dtype=jnp.float32) * scale, 'Wkv_expand': jax.random.normal(k4, (2 * H, L), dtype=jnp.float32) * scale, 'Wout': jax.random.normal(k5, (H, H), dtype=jnp.float32) * scale}
    _L1_xattn_all = _L1_xattn_setup()
    _L1_xattn_in = {k: v for k, v in _L1_xattn_all.items() if k in ('Wq', 'Wkv_expand', 'Wout')}
    del _L1_xattn_all

    def _L1_ffn_setup():
        import jax, jax.numpy as jnp
        import numpy as np
        B, S, H = (1, 128, 256)
        E, K = (32, 4)
        F, FS = (176, 704)
        CAP = 32

        def silu(x):
            return x * jax.nn.sigmoid(x)
        key = jax.random.key(seed)
        ks = jax.random.split(key, 9)
        sc = 0.02
        return {'hidden_states': jax.random.normal(ks[0], (B, S, H), jnp.float32), 'Wr': jax.random.normal(ks[1], (H, E), jnp.float32) * sc, 'Wg': jax.random.normal(ks[2], (E, H, F), jnp.float32) * sc, 'Wu': jax.random.normal(ks[3], (E, H, F), jnp.float32) * sc, 'Wd': jax.random.normal(ks[4], (E, F, H), jnp.float32) * sc, 'Wsg': jax.random.normal(ks[5], (H, FS), jnp.float32) * sc, 'Wsu': jax.random.normal(ks[6], (H, FS), jnp.float32) * sc, 'Wsd': jax.random.normal(ks[7], (FS, H), jnp.float32) * sc, 'Wse': jax.random.normal(ks[8], (H, 1), jnp.float32) * sc}
    _L1_ffn_all = _L1_ffn_setup()
    _L1_ffn_in = {k: v for k, v in _L1_ffn_all.items() if k in ('Wr', 'Wg', 'Wu', 'Wd', 'Wsg', 'Wsu', 'Wsd', 'Wse')}
    del _L1_ffn_all
    return {'x': x, 'ctx_512': ctx_512, 'L0_attn_w_q': _L0_attn_in['w_q'], 'L0_attn_w_k': _L0_attn_in['w_k'], 'L0_attn_w_v': _L0_attn_in['w_v'], 'L0_attn_w_o': _L0_attn_in['w_o'], 'L0_xattn_W_k': _L0_xattn_in['W_k'], 'L0_xattn_b_k': _L0_xattn_in['b_k'], 'L0_xattn_ln_gamma': _L0_xattn_in['ln_gamma'], 'L0_xattn_ln_beta': _L0_xattn_in['ln_beta'], 'L0_ffn_gate_w': _L0_ffn_in['gate_w'], 'L0_ffn_w_gate_up': _L0_ffn_in['w_gate_up'], 'L0_ffn_w_down': _L0_ffn_in['w_down'], 'L0_ffn_shared_gate_up': _L0_ffn_in['shared_gate_up'], 'L0_ffn_shared_down': _L0_ffn_in['shared_down'], 'L1_attn_input_pos': _L1_attn_in['input_pos'], 'L1_attn_in_proj_w': _L1_attn_in['in_proj_w'], 'L1_attn_conv_w': _L1_attn_in['conv_w'], 'L1_attn_dt_bias': _L1_attn_in['dt_bias'], 'L1_attn_A_log': _L1_attn_in['A_log'], 'L1_attn_norm_weight': _L1_attn_in['norm_weight'], 'L1_attn_out_proj_w': _L1_attn_in['out_proj_w'], 'L1_xattn_Wq': _L1_xattn_in['Wq'], 'L1_xattn_Wkv_expand': _L1_xattn_in['Wkv_expand'], 'L1_xattn_Wout': _L1_xattn_in['Wout'], 'L1_ffn_Wr': _L1_ffn_in['Wr'], 'L1_ffn_Wg': _L1_ffn_in['Wg'], 'L1_ffn_Wu': _L1_ffn_in['Wu'], 'L1_ffn_Wd': _L1_ffn_in['Wd'], 'L1_ffn_Wsg': _L1_ffn_in['Wsg'], 'L1_ffn_Wsu': _L1_ffn_in['Wsu'], 'L1_ffn_Wsd': _L1_ffn_in['Wsd'], 'L1_ffn_Wse': _L1_ffn_in['Wse']}

def reference(x, ctx_512, L0_attn_w_q, L0_attn_w_k, L0_attn_w_v, L0_attn_w_o, L0_xattn_W_k, L0_xattn_b_k, L0_xattn_ln_gamma, L0_xattn_ln_beta, L0_ffn_gate_w, L0_ffn_w_gate_up, L0_ffn_w_down, L0_ffn_shared_gate_up, L0_ffn_shared_down, L1_attn_input_pos, L1_attn_in_proj_w, L1_attn_conv_w, L1_attn_dt_bias, L1_attn_A_log, L1_attn_norm_weight, L1_attn_out_proj_w, L1_xattn_Wq, L1_xattn_Wkv_expand, L1_xattn_Wout, L1_ffn_Wr, L1_ffn_Wg, L1_ffn_Wu, L1_ffn_Wd, L1_ffn_Wsg, L1_ffn_Wsu, L1_ffn_Wsd, L1_ffn_Wse):
    import jax
    import jax.numpy as jnp

    def _L0_attn_ref(x, w_q, w_k, w_v, w_o):
        import jax, jax.numpy as jnp
        import numpy as np
        B, T, C = (1, 512, 256)
        H = 16
        D = C // H
        BLOCK = 64
        WINDOW = 128
        DILATION = 32
        GLOBAL_TOKENS = 128
        ROPE_BASE = 10000.0
        SCALE = 1.0 / np.sqrt(D)

        def _rope(x):
            t = jnp.arange(x.shape[2], dtype=jnp.float32)
            inv_freq = 1.0 / ROPE_BASE ** (jnp.arange(0, D, 2, dtype=jnp.float32) / D)
            freqs = jnp.outer(t, inv_freq)
            emb = jnp.concatenate([freqs, freqs], axis=-1)
            cos = jnp.cos(emb)[None, None].astype(x.dtype)
            sin = jnp.sin(emb)[None, None].astype(x.dtype)
            x1, x2 = jnp.split(x, 2, axis=-1)
            rot = jnp.concatenate([-x2, x1], axis=-1)
            return x * cos + rot * sin

        def _token_mask(seq_len):
            nb = (seq_len + BLOCK - 1) // BLOCK
            bp = jnp.arange(nb)
            qb, kb = (bp[:, None], bp[None, :])
            dist = qb - kb
            window_blocks = WINDOW // BLOCK
            window_mask = (dist >= 0) & (dist <= window_blocks)
            global_blocks = max(1, GLOBAL_TOKENS // BLOCK)
            global_mask = kb < global_blocks
            dilation_blocks = max(1, DILATION // BLOCK)
            dilated_mask = kb % dilation_blocks == 0
            causal_mask = kb <= qb
            block_mask = (window_mask | global_mask | dilated_mask) & causal_mask
            tok = jnp.repeat(jnp.repeat(block_mask, BLOCK, axis=0), BLOCK, axis=1)
            return tok[:seq_len, :seq_len]
        Bc, Tc, Cc = x.shape
        q = (x @ w_q.T).reshape(Bc, Tc, H, D).transpose(0, 2, 1, 3)
        k = (x @ w_k.T).reshape(Bc, Tc, H, D).transpose(0, 2, 1, 3)
        v = (x @ w_v.T).reshape(Bc, Tc, H, D).transpose(0, 2, 1, 3)
        q = _rope(q)
        k = _rope(k)
        scores = jnp.einsum('bhqd,bhkd->bhqk', q, k) * SCALE
        tok_mask = _token_mask(Tc)
        scores = jnp.where(tok_mask[None, None], scores, -jnp.inf)
        attn = jax.nn.softmax(scores, axis=-1)
        ctx = jnp.einsum('bhqk,bhkd->bhqd', attn, v)
        ctx = ctx.transpose(0, 2, 1, 3).reshape(Bc, Tc, Cc)
        return ctx @ w_o.T

    def _L0_xattn_ref(p, k_v, W_k, b_k, ln_gamma, ln_beta):
        import jax, jax.numpy as jnp
        import numpy as np
        EPS = 1e-06
        IMAGE_DIMS = 256
        kv = k_v @ W_k.T + b_k
        out = jnp.einsum('bij,bjd->bid', p, kv)
        scale = IMAGE_DIMS ** (-0.5)
        sim = jnp.einsum('bid,bjd->bij', out, kv) * scale
        mu = jnp.mean(sim, axis=-1, keepdims=True)
        var = jnp.var(sim, axis=-1, keepdims=True)
        sim = (sim - mu) * jax.lax.rsqrt(var + EPS) * ln_gamma + ln_beta
        attn = jax.nn.softmax(sim, axis=-1)
        return attn

    def _L0_ffn_ref(hidden_states, gate_w, w_gate_up, w_down, shared_gate_up, shared_down):
        import jax, jax.numpy as jnp
        import numpy as np
        from jax import lax
        E = 8
        K = 2
        H = 256
        I = 512
        B, S = (2, 256)
        SCALE = 0.02

        def _silu_and_mul(gu):
            g, u = jnp.split(gu, 2, axis=-1)
            return jax.nn.silu(g) * u
        orig_shape = hidden_states.shape
        x = hidden_states.reshape(-1, orig_shape[-1])
        shared_out = _silu_and_mul(x @ shared_gate_up) @ shared_down
        router_logits = x @ gate_w
        probs = jax.nn.softmax(router_logits, axis=-1)
        topk_w, topk_i = lax.top_k(probs, K)
        topk_w = topk_w / jnp.sum(topk_w, axis=-1, keepdims=True)
        combine = jnp.sum(jax.nn.one_hot(topk_i, E, dtype=x.dtype) * topk_w[..., None], axis=1)

        def body(acc, we):
            wg, wd, cw = we
            h = _silu_and_mul(x @ wg) @ wd
            return (acc + cw[:, None] * h, None)
        moe_out, _ = lax.scan(body, jnp.zeros_like(x), (w_gate_up, w_down, combine.T))
        return (moe_out + shared_out).reshape(orig_shape)

    def _L1_attn_ref(x, input_pos, in_proj_w, conv_w, dt_bias, A_log, norm_weight, out_proj_w):
        import jax, jax.numpy as jnp
        import numpy as np
        B, T, HID = (2, 128, 256)
        NKH, NVH, DK, DV, KS = (8, 16, 64, 128, 4)
        KD = NKH * DK
        VD = NVH * DV
        CD = 2 * KD + VD
        IPD = CD + VD + 2 * NVH
        EPS = 1e-06
        SCALE = DK ** (-0.5)

        def _l2norm(t):
            return t / jnp.maximum(jnp.linalg.norm(t, axis=-1, keepdims=True), 1e-12)

        def _forward(x, in_proj_w, conv_w, dt_bias, A_log, norm_weight, out_proj_w):
            Bb, Tt, _ = x.shape
            f32 = jnp.float32
            proj = x @ in_proj_w.T
            mixed = proj[..., :CD]
            z = proj[..., CD:CD + VD].reshape(Bb, Tt, NVH, DV)
            b = proj[..., CD + VD:CD + VD + NVH]
            a = proj[..., CD + VD + NVH:]
            xc = jnp.swapaxes(mixed, 1, 2)
            ci = jnp.pad(xc, ((0, 0), (0, 0), (KS, 0))).astype(f32)
            w = conv_w.astype(f32)
            Tc = Tt + 1
            acc = sum((ci[:, :, k:k + Tc] * w[:, k][None, :, None] for k in range(KS)))
            qkv = jnp.swapaxes(jax.nn.silu(acc[:, :, -Tt:]), 1, 2).astype(x.dtype)
            q = _l2norm(qkv[..., :KD].reshape(Bb, Tt, NKH, DK))
            k = _l2norm(qkv[..., KD:2 * KD].reshape(Bb, Tt, NKH, DK))
            v = qkv[..., 2 * KD:].reshape(Bb, Tt, NVH, DV)
            rep = NVH // NKH
            if rep > 1:
                q = jnp.repeat(q, rep, axis=2)
                k = jnp.repeat(k, rep, axis=2)
            beta = jax.nn.sigmoid(b).astype(f32)
            g = -jnp.exp(A_log.astype(f32)) * jax.nn.softplus(a.astype(f32) + dt_bias.astype(f32))
            seq = (jnp.swapaxes(q, 0, 1).astype(f32), jnp.swapaxes(k, 0, 1).astype(f32), jnp.swapaxes(v, 0, 1).astype(f32), jnp.swapaxes(g, 0, 1), jnp.swapaxes(beta, 0, 1))

            def step(state, inp):
                qt, kt, vt, gt, bt = inp
                state = state * jnp.exp(gt)[:, :, None, None]
                Sk = jnp.einsum('bhkv,bhk->bhv', state, kt)
                delta = bt[..., None] * (vt - Sk)
                state = state + jnp.einsum('bhk,bhv->bhkv', kt, delta)
                out = jnp.einsum('bhkv,bhk->bhv', state, qt) * SCALE
                return (state, out)
            state0 = jnp.zeros((Bb, NVH, DK, DV), f32)
            _, outs = jax.lax.scan(step, state0, seq)
            o = jnp.swapaxes(outs, 0, 1).reshape(-1, DV)
            zf = z.reshape(-1, DV).astype(f32)
            normed = norm_weight * (o * jax.lax.rsqrt(jnp.mean(o * o, axis=-1, keepdims=True) + EPS))
            gated = (normed * jax.nn.silu(zf)).astype(x.dtype)
            return gated.reshape(Bb, Tt, VD) @ out_proj_w.T
        return _forward(x, in_proj_w, conv_w, dt_bias, A_log, norm_weight, out_proj_w)

    def _L1_xattn_ref(q, latent_kv, Wq, Wkv_expand, Wout):
        import jax, jax.numpy as jnp
        import numpy as np
        B, S, H, NH, L = (2, 256, 256, 16, 64)
        HD = H // NH
        b, sq, _ = q.shape
        sk = latent_kv.shape[1]
        qp = q @ Wq.T
        kv = latent_kv @ Wkv_expand.T
        k, v = jnp.split(kv, 2, axis=-1)
        qh = qp.reshape(b, sq, NH, HD).transpose(0, 2, 1, 3)
        kh = k.reshape(b, sk, NH, HD).transpose(0, 2, 1, 3)
        vh = v.reshape(b, sk, NH, HD).transpose(0, 2, 1, 3)
        inv_sqrt_d = 1.0 / jnp.sqrt(jnp.float32(HD))
        scores = jnp.einsum('bhqd,bhkd->bhqk', qh, kh) * inv_sqrt_d
        causal = jnp.tril(jnp.ones((sq, sk), dtype=bool))
        scores = jnp.where(causal, scores, jnp.finfo(scores.dtype).min)
        attn = jax.nn.softmax(scores, axis=-1)
        out = jnp.einsum('bhqk,bhkd->bhqd', attn, vh)
        out = out.transpose(0, 2, 1, 3).reshape(b, sq, H)
        return out @ Wout.T

    def _L1_ffn_ref(hidden_states, Wr, Wg, Wu, Wd, Wsg, Wsu, Wsd, Wse):
        import jax, jax.numpy as jnp
        import numpy as np
        B, S, H = (1, 128, 256)
        E, K = (32, 4)
        F, FS = (176, 704)
        CAP = 32

        def silu(x):
            return x * jax.nn.sigmoid(x)
        b, s_len, h = hidden_states.shape
        x = hidden_states.reshape(-1, h)
        T = x.shape[0]
        probs = jax.nn.softmax(x @ Wr, axis=-1)
        topw, topi = jax.lax.top_k(probs, K)
        topw = topw / jnp.sum(topw, axis=-1, keepdims=True)
        shared = silu(x @ Wsg) * (x @ Wsu) @ Wsd
        shared = shared * jax.nn.sigmoid(x @ Wse)
        sel = topi.reshape(-1)
        w = topw.reshape(-1)
        tok = jnp.repeat(jnp.arange(T), K)
        oh = jax.nn.one_hot(sel, E, dtype=jnp.int32)
        pos = (jnp.cumsum(oh, axis=0) * oh).sum(-1) - 1
        valid = (pos < CAP).astype(x.dtype)
        posc = jnp.clip(pos, 0, CAP - 1)
        xe = jnp.zeros((E, CAP, h), x.dtype).at[sel, posc].add(x[tok] * valid[:, None])
        g = silu(jnp.einsum('ech,ehf->ecf', xe, Wg))
        u = jnp.einsum('ech,ehf->ecf', xe, Wu)
        ye = jnp.einsum('ecf,efh->ech', g * u, Wd)
        y_pair = ye[sel, posc] * (w * valid)[:, None]
        out = shared.at[tok].add(y_pair)
        return out.reshape(b, s_len, h)
    x = _layernorm(x + _L0_attn_ref(x, L0_attn_w_q, L0_attn_w_k, L0_attn_w_v, L0_attn_w_o), axis=-1)
    x = _layernorm(x + _L0_xattn_ref(x, ctx_512, L0_xattn_W_k, L0_xattn_b_k, L0_xattn_ln_gamma, L0_xattn_ln_beta), axis=-1)
    x = _layernorm(x + _L0_ffn_ref(x, L0_ffn_gate_w, L0_ffn_w_gate_up, L0_ffn_w_down, L0_ffn_shared_gate_up, L0_ffn_shared_down), axis=-1)
    x = _layernorm(x + _L1_attn_ref(x, L1_attn_input_pos, L1_attn_in_proj_w, L1_attn_conv_w, L1_attn_dt_bias, L1_attn_A_log, L1_attn_norm_weight, L1_attn_out_proj_w), axis=-1)
    x = _layernorm(x + _L1_xattn_ref(x, ctx_512, L1_xattn_Wq, L1_xattn_Wkv_expand, L1_xattn_Wout), axis=-1)
    x = _layernorm(x + _L1_ffn_ref(x, L1_ffn_Wr, L1_ffn_Wg, L1_ffn_Wu, L1_ffn_Wd, L1_ffn_Wsg, L1_ffn_Wsu, L1_ffn_Wsd, L1_ffn_Wse), axis=-1)
    return x

_drawn_inputs = setup_inputs


def setup_inputs(seed=0):
    import zlib

    import numpy as np

    out = dict(_drawn_inputs(seed))
    spreads = {'L0_xattn_b_k': (0.0, 0.8),
     'L0_xattn_ln_gamma': (1.0, 0.6),
     'L0_xattn_ln_beta': (0.0, 0.8),
     'L1_attn_dt_bias': (1.0, 0.6),
     'L1_attn_norm_weight': (1.0, 0.6)}
    factors = {'L0_attn_w_q': 8.0,
     'L0_attn_w_k': 8.0,
     'L0_attn_w_v': 5.933,
     'L0_attn_w_o': 6.198,
     'L0_xattn_W_k': 8.0,
     'L0_ffn_gate_w': 3.806,
     'L0_ffn_w_gate_up': 3.31,
     'L0_ffn_w_down': 3.312,
     'L1_attn_A_log': 7.96,
     'L1_xattn_Wq': 8.0,
     'L1_ffn_Wr': 8.0,
     'L1_ffn_Wg': 8.0,
     'L1_ffn_Wu': 8.0,
     'L1_ffn_Wd': 8.0,
     'L1_ffn_Wsg': 4.014,
     'L1_ffn_Wsu': 3.99,
     'L1_ffn_Wsd': 3.992,
     'L1_ffn_Wse': 8.0}
    for name, (base, spread) in spreads.items():
        noise = np.random.default_rng([zlib.crc32(name.encode()), seed]).standard_normal(out[name].shape)
        drawn = base * np.exp(spread * noise) if base else spread * noise
        out[name] = jnp.asarray(drawn.astype(out[name].dtype))
    for name, factor in factors.items():
        out[name] = (out[name] * factor).astype(out[name].dtype)
    return out
```

```python
from contextlib import ExitStack

import concourse.bass as bass
from concourse import mybir

F32 = mybir.dt.float32
BF16 = mybir.dt.bfloat16
U32 = mybir.dt.uint32

ALU = mybir.AluOpType
ACT = mybir.ActivationFunctionType
AX = mybir.AxisListType

P = 128
B, T, C = 4, 256, 256
NT = B * T // P
TPB = T // P
KC = C // P
NTOK = B * T
CTX = 64
LN_EPS = 1e-5

NH, HD, SLOT = 16, 16, 32
HPT = P // SLOT
NHT = NH // HPT
MASKED = -1e30




class Steps:

    def __init__(self, eng, sem, turn=0, per=0):
        self.eng, self.sem, self.turn, self.per, self.n = eng, sem, turn, per, 0

    def then(self, ins):
        ins.then_inc(self.sem, 1)
        self.n += 1
        return self.n

    def wait(self, n=None):
        self.eng.wait_ge(self.sem, 1 + self.turn * self.per + (self.n if n is None else n))

    def end(self):
        assert self.n == self.per, (self.n, self.per)


class LayernormSems:
    def __init__(self, sem):
        self.stats, self.mv, self.sd, self.rstd = (sem("ln_" + n) for n in ("stats", "mv", "sd", "rstd"))
        self.normed, self.turned, self.kept, self.out = (sem("ln_" + n) for n in ("normed", "turned", "kept", "out"))


class Shared:

    def __init__(self, sb, pb, sem):
        self.sem = sem
        self.bank = [pb(f"bank{i}", [P, 512], F32) for i in range(8)]
        self.X, self.XT, self.ctxT = sb("X", [P, NT, C]), sb("XT", [P, KC, NTOK]), sb("ctxT", [CTX, NTOK])
        self.ident, self.tick = sb("ident", [P, P]), sb("tick", [1, 64])
        self.eps_ln, self.eps6 = sb("eps_ln", [P, 1]), sb("eps6", [P, 1])
        self.ln_sems = LayernormSems(sem)


def layernorm(nc, g, call, spent, out=None):
    with ExitStack() as ctx:
        def sb(n, shape, dt=F32):
            return ctx.enter_context(nc.sbuf_tensor(f"ln{call}_{n}", shape, dt))

        stats = sb("stats", [P, NT, 6])
        mv = sb("mv", [P, NT, 2])
        sd = sb("sd", [P, NT])
        rstd = sb("rstd", [P, NT])
        s = g.ln_sems
        each, one, banks = call * NT, call, call * 2 * (NT // 4)

        with nc.Block() as block:
            @block.vector
            def _(dve):
                for t in range(NT):
                    dve.bn_stats(stats[:, t, :], g.X[:, t, :]).then_inc(s.stats, 1)
                for t in range(NT):
                    dve.wait_ge(s.stats, each + t + 1)
                    dve.bn_aggr(mv[:, t, :], stats[:, t, :]).then_inc(s.mv, 1)
                dve.wait_ge(s.sd, one + 1)
                dve.reciprocal(rstd[:], sd[:]).then_inc(s.rstd, 1)
                dve.wait_ge(s.rstd, one + 1)
                for t in range(NT):
                    dve.tensor_scalar(g.X[:, t, :], g.X[:, t, :], mv[:, t, 0:1], rstd[:, t:t + 1],
                                      ALU.subtract, ALU.mult).then_inc(s.normed, 1)
                if out is None:
                    for n in range(NT // 4):
                        dve.wait_ge(s.turned, banks + KC * n + 2)
                        dve.tensor_copy(g.XT[:, 1, 512 * n:512 * n + 512],
                                        g.bank[KC * n + 1][:]).then_inc(s.kept, 1)

            @block.scalar
            def _(act):
                act.wait_ge(s.mv, each + NT)
                act.activation(sd[:], mv[:, :, 1], ACT.Sqrt, bias=g.eps_ln[:, 0:1]).then_inc(s.sd, 1)
                if out is None:
                    for n in range(NT // 4):
                        act.wait_ge(s.turned, banks + KC * n + 1)
                        act.copy(g.XT[:, 0, 512 * n:512 * n + 512], g.bank[KC * n][:]).then_inc(s.kept, 1)

            @block.gpsimd
            def _(pool):
                for sem in spent:
                    pool.sem_clear(sem)
                for sem in spent:
                    pool.sem_inc(sem, 1)

            if out is None:
                @block.tensor
                def _(pe):
                    for n in range(NT // 4):
                        pe.wait_ge(s.normed, each + 4 * n + 4)
                        for k in range(KC):
                            for i in range(4):
                                last = pe.transpose(g.bank[KC * n + k][:, P * i:P * i + P],
                                                    g.X[:, 4 * n + i, P * k:P * k + P], g.ident[:])
                            last.then_inc(s.turned, 1)
            else:
                @block.sync
                def _(sp):
                    for n in range(NT // 4):
                        sp.wait_ge(s.normed, each + 4 * n + 4)
                        sp.dma_start(out[:, 4 * n:4 * n + 4, :], g.X[:, 4 * n:4 * n + 4, :]).then_inc(s.out, 16)
                    sp.wait_ge(s.out, 16 * (NT // 4))


def attention(nc, g, name, rope, a, layer):
    K = SLOT if rope else HD
    KIN = KC if rope else 1
    NP = 2 * NHT + (NHT if rope else 0) + TPB
    NIN = 1 if rope else 2
    WID = 3 * P
    with ExitStack() as ctx:
        def sb(n, shape, dt=F32):
            return ctx.enter_context(nc.sbuf_tensor(f"{name}_{n}", shape, dt))

        def sem(n):
            return g.sem(f"{name}_{n}")

        wq, wo, mask = sb("wq", [P, KC, NHT * P]), sb("wo", [P, KC, C]), sb("mask", [P, T])
        wk = sb("wk", [P if rope else CTX, KIN, NHT * P])
        wv = sb("wv", [P if rope else CTX, KIN, C])
        loads = [(wq, layer + "_wq"), (wk, layer + "_wk"), (wv, layer + "_wv"), (mask, layer + "_mask"), (wo, layer + "_wo")]
        if rope:
            table, fold = sb("table", [P, T]), sb("fold", [P, P])
            loads[1:1] = [(table, "rope"), (fold, "fold")]
        xb = sb("xb", [P, KC, T])
        cb = xb if rope else sb("cb", [CTX, 1, T])
        q = sb("q", [P, NHT, T])
        k = sb("k", [P, NHT, T])
        kparts = sb("kparts", [P, NHT, T]) if rope else k
        v = sb("v", [P, TPB, C])
        negs = sb("negs", [P, 2, WID])
        negmax = sb("negmax", [P, TPB, NH])
        sums = sb("sums", [P, TPB, NH])
        rsum = sb("rsum", [P, TPB, NH])
        probs = sb("probs", [P, 2, WID])
        probsT = sb("probsT", [P, 2, WID])
        ctxn = sb("ctxn", [P, TPB, C])
        ctxT = sb("ctxT", [P, KC, T])
        s_in, s_proj, s_kept, s_scores, s_masked = sem("in"), sem("proj"), sem("kept"), sem("scores"), sem("masked")
        s_exp, s_turned, s_back, s_pv, s_norm = sem("exp"), sem("turned"), sem("back"), sem("pv"), sem("norm")
        s_fin, s_finkept, s_rsum = sem("fin"), sem("finkept"), sem("rsum")
        proj, score, turn, mix, last_bank = g.bank[0:2], g.bank[2:4], g.bank[4:6], g.bank[6], g.bank[7]

        s_w = sem("w")
        with nc.Block() as block:
            @block.sync
            def _(sp):
                for tile, n in loads:
                    sp.dma_start(tile[:], a[n]).then_inc(s_w, 16)

            @block.tensor
            def _(pe):
                pe.wait_ge(s_w, 1 + 16 * len(loads))
                with pe.Fori(0, B) as b:
                    n = 0

                    def project(lhs, rhs, wid):
                        nonlocal n
                        pe.wait_ge(s_kept, 1 + b * NP + max(n - 1, 0))
                        for j, (l, r) in enumerate(zip(lhs, rhs)):
                            mm = pe.matmul(proj[n % 2][:, 0:wid], l, r, start=(j == 0), stop=(j == len(lhs) - 1))
                        mm.then_inc(s_proj, 1)
                        n += 1

                    pe.wait_ge(s_in, 1 + NIN * (b + 1))
                    pe.wait_ge(s_finkept, 1 + 3 * b)
                    xs, cs = [xb[:, j, :] for j in range(KC)], [cb[:, j, :] for j in range(KIN)]
                    for m in range(NHT):
                        project([wq[:, j, P * m:P * m + P] for j in range(KC)], xs, T)
                    for m in range(NHT):
                        project([wk[:, j, P * m:P * m + P] for j in range(KIN)], cs, T)
                    if rope:
                        for m in range(NHT):
                            pe.wait_ge(s_kept, 1 + b * NP + NHT + m + 1)
                            project([fold[:]], [kparts[:, m, :]], T)
                    for t in range(TPB):
                        project([c[:, P * t:P * t + P] for c in cs], [wv[:, j, :] for j in range(KIN)], C)

                    def scores(h):
                        p, m = SLOT * (h % HPT), h // HPT
                        if h == 0:
                            pe.wait_ge(s_kept, 1 + b * NP + NP)
                        pe.wait_ge(s_masked, 1 + b * NH + max(h - 1, 0))
                        pe.matmul(score[h % 2][:, 0:P], q[p:p + K, m, 0:P], k[p:p + K, m, 0:P], start=True, stop=True)
                        pe.matmul(score[h % 2][:, P:WID], q[p:p + K, m, P:T], k[p:p + K, m, :],
                                  start=True, stop=True).then_inc(s_scores, 1)

                    def transposes(h):
                        pe.wait_ge(s_exp, 1 + b * NH + h + 1)
                        pe.wait_ge(s_back, 1 + b * NH + max(h - 1, 0))
                        for i in range(3):
                            mm = pe.transpose(turn[h % 2][:, P * i:P * i + P], probs[:, h % 2, P * i:P * i + P], g.ident[:])
                        mm.then_inc(s_turned, 1)

                    def values(h):
                        pe.wait_ge(s_back, 1 + b * NH + h + 1)
                        if h == 0:
                            pe.wait_ge(s_norm, 1 + b)
                        cols = slice(HD * h, HD * h + HD)
                        pe.matmul(mix[:, HD * h:HD * h + HD], probsT[:, h % 2, 0:P], v[:, 0, cols], start=True, stop=True)
                        pe.matmul(mix[:, C + HD * h:C + HD * h + HD], probsT[:, h % 2, P:2 * P], v[:, 0, cols],
                                  start=True, stop=False)
                        pe.matmul(mix[:, C + HD * h:C + HD * h + HD], probsT[:, h % 2, 2 * P:WID], v[:, 1, cols],
                                  start=False, stop=True).then_inc(s_pv, 1)

                    for i in range(NH + 2):
                        if i < NH:
                            scores(i)
                        if 1 <= i <= NH:
                            transposes(i - 1)
                        if i >= 2:
                            values(i - 2)
                    pe.wait_ge(s_norm, 1 + b + 1)
                    for j in range(KC):
                        for t in range(TPB):
                            mm = pe.transpose(last_bank[:, T * j + P * t:T * j + P * t + P], ctxn[:, t, P * j:P * j + P], g.ident[:])
                    mm.then_inc(s_fin, 1)
                    pe.wait_ge(s_finkept, 1 + 3 * b + 1)
                    for t in range(TPB):
                        for j in range(KC):
                            mm = pe.matmul(last_bank[:, C * t:C * t + C], ctxT[:, j, P * t:P * t + P], wo[:, j, :],
                                           start=(j == 0), stop=(j == KC - 1))
                    mm.then_inc(s_fin, 1)

            @block.vector
            def _(dve):
                dve.wait_ge(s_w, 1 + 16 * len(loads))
                with dve.Fori(0, B) as b:
                    dve.tensor_copy(xb[:], g.XT[:, :, bass.ts(b, T)]).then_inc(s_in, 1)
                    if not rope:
                        dve.tensor_copy(cb[:, 0, :], g.ctxT[:, bass.ts(b, T)]).then_inc(s_in, 1)
                    n = 0

                    def keep(make):
                        nonlocal n
                        dve.wait_ge(s_proj, 1 + b * NP + n + 1)
                        make(proj[n % 2]).then_inc(s_kept, 1)
                        n += 1

                    for m in range(NHT):
                        keep(lambda ps: dve.tensor_tensor(q[:, m, :], ps[:, 0:T], table[:], ALU.mult) if rope
                             else dve.tensor_copy(q[:, m, :], ps[:, 0:T]))
                    for m in range(NHT):
                        keep(lambda ps: dve.tensor_tensor(kparts[:, m, :], ps[:, 0:T], table[:], ALU.mult) if rope
                             else dve.tensor_copy(k[:, m, :], ps[:, 0:T]))
                    if rope:
                        for m in range(NHT):
                            keep(lambda ps: dve.tensor_copy(k[:, m, :], ps[:, 0:T]))
                    for t in range(TPB):
                        keep(lambda ps: dve.tensor_copy(v[:, t, :], ps[:, 0:C]))
                    for h in range(NH):
                        dve.wait_ge(s_scores, 1 + b * NH + h + 1)
                        dve.wait_ge(s_exp, 1 + b * NH + max(h - 1, 0))
                        dve.memset(g.tick[:, h:h + 1], 0.0)
                        dve.tensor_tensor_reduce(negs[:, h % 2, 0:P], score[h % 2][:, 0:P], mask[:, P:2 * P],
                                                 -0.25, 3e38, ALU.add, ALU.min, negmax[:, 0, h:h + 1])
                        dve.tensor_tensor_reduce(negs[:, h % 2, P:WID], score[h % 2][:, P:WID], mask[:],
                                                 -0.25, 3e38, ALU.add, ALU.min, negmax[:, 1, h:h + 1]).then_inc(s_masked, 1)
                    dve.wait_ge(s_exp, 1 + b * NH + NH)
                    dve.reciprocal(rsum[:], sums[:]).then_inc(s_rsum, 1)
                    dve.wait_ge(s_rsum, 1 + b + 1)
                    dve.wait_ge(s_pv, 1 + b * NH + NH)
                    dve.tensor_tensor(ctxn[:].rearrange("p t (h d) -> p t h d", h=NH),
                                      mix[:].rearrange("p (t h d) -> p t h d", t=TPB, h=NH),
                                      rsum[:].unsqueeze(3).to_broadcast([P, TPB, NH, HD]), ALU.mult).then_inc(s_norm, 1)
                    dve.wait_ge(s_fin, 1 + 2 * b + 1)
                    dve.tensor_copy(ctxT[:].rearrange("p j t -> p (j t)"), last_bank[:]).then_inc(s_finkept, 1)
                    dve.wait_ge(s_fin, 1 + 2 * b + 2)
                    for t in range(TPB):
                        tile = g.X[:, bass.ds(b * TPB + t, 1), :]
                        dve.tensor_tensor(tile, last_bank[:, C * t:C * t + C].unsqueeze(1), tile, ALU.add).then_inc(s_finkept, 1)

            @block.scalar
            def _(act):
                with act.Fori(0, B) as b:
                    for h in range(NH + 1):
                        if h < NH:
                            act.wait_ge(s_masked, 1 + b * NH + h + 1)
                            act.wait_ge(s_turned, 1 + b * NH + max(h - 1, 0))
                            act.activation(probs[:, h % 2, 0:P], negs[:, h % 2, 0:P], ACT.Exp, bias=negmax[:, 0, h:h + 1],
                                           scale=-1.0, accum_out=sums[:, 0, h:h + 1])
                            act.activation(probs[:, h % 2, P:WID], negs[:, h % 2, P:WID], ACT.Exp, bias=negmax[:, 1, h:h + 1],
                                           scale=-1.0, accum_out=sums[:, 1, h:h + 1]).then_inc(s_exp, 1)
                        if h >= 1:
                            act.wait_ge(s_turned, 1 + b * NH + h)
                            act.wait_ge(s_pv, 1 + b * NH + max(h - 2, 0))
                            act.copy(probsT[:, (h - 1) % 2, :], turn[(h - 1) % 2][:, 0:WID]).then_inc(s_back, 1)


def context_softmax(nc, g, a):
    with ExitStack() as ctx:
        def sb(n, shape, dt=F32):
            return ctx.enter_context(nc.sbuf_tensor(f"c0_{n}", shape, dt))

        def sem(n):
            return g.sem(f"c0_{n}")

        wk = sb("wk", [CTX, CTX])
        bcol, brow = sb("bcol", [CTX, 1]), sb("brow", [P, CTX])
        gamma, beta = sb("gamma", [P, T]), sb("beta", [P, T])
        xb, cb = sb("xb", [P, KC, T]), sb("cb", [CTX, T])
        kvT, kv, outT = sb("kvT", [CTX, T]), sb("kv", [P, TPB, CTX]), sb("outT", [CTX, T])
        stats, mv = sb("stats", [P, TPB, 6]), sb("mv", [P, TPB, 2])
        sd, rstd = sb("sd", [P, TPB]), sb("rstd", [P, TPB])
        sim = sb("sim", [P, TPB, T])
        negmax, sums, rsum = sb("negmax", [P, TPB]), sb("sums", [P, TPB]), sb("rsum", [P, TPB])
        s_load, s_in, s_kv, s_kvkept, s_kvTkept = sem("load"), sem("in"), sem("kv"), sem("kvkept"), sem("kvTkept")
        s_outT, s_outTkept, s_sim, s_var, s_sd = sem("outT"), sem("outTkept"), sem("sim"), sem("var"), sem("sd")
        s_max, s_exp, s_own = sem("max"), sem("exp"), sem("own")
        PER = 12

        with nc.Block() as block:
            @block.sync
            def _(sp):
                sp.dma_start(wk[:], a["L0_Wk"]).then_inc(s_load, 16)
                sp.dma_start(bcol[:], a["L0_bk"].rearrange("(p a) -> p a", a=1)).then_inc(s_load, 16)
                sp.dma_start(brow[:], a["L0_bk"].partition_broadcast(P)).then_inc(s_load, 16)
                sp.dma_start(gamma[:], a["L0_gamma"].partition_broadcast(P)).then_inc(s_load, 16)
                sp.dma_start(beta[:], a["L0_beta"].partition_broadcast(P)).then_inc(s_load, 16)

            @block.tensor
            def _(pe):
                pe.wait_ge(s_load, 1 + 80)
                with pe.Fori(0, B) as b:
                    pe.wait_ge(s_in, 1 + 2 * b + 2)
                    for t in range(TPB):
                        pe.matmul(g.bank[1][:, CTX * t:CTX * t + CTX], cb[:, P * t:P * t + P], wk[:], start=True, stop=True)
                    mm = pe.matmul(g.bank[0][0:CTX, 0:T], wk[:], cb[:], start=True, stop=True)
                    mm.then_inc(s_kv, 1)
                    pe.wait_ge(s_kvkept, 1 + b + 1)
                    for t in range(TPB):
                        mm = pe.matmul(g.bank[2][0:CTX, 0:T], kv[:, t, :], xb[:, t, :], start=(t == 0), stop=(t == TPB - 1))
                    mm.then_inc(s_outT, 1)
                    pe.wait_ge(s_outTkept, 1 + b + 1)
                    pe.wait_ge(s_kvTkept, 1 + b + 1)
                    for t in range(TPB):
                        pe.matmul(g.bank[3 + t][:, 0:T], outT[:, P * t:P * t + P], kvT[:], start=True, stop=True).then_inc(s_sim, 1)

            @block.vector
            def _(dve):
                dve.wait_ge(s_load, 1 + 80)
                with dve.Fori(0, B) as b:
                    own = Steps(dve, s_own, b, PER)
                    dve.tensor_copy(xb[:], g.XT[:, :, bass.ts(b, T)]).then_inc(s_in, 1)
                    dve.tensor_copy(cb[:], g.ctxT[:, bass.ts(b, T)]).then_inc(s_in, 1)
                    dve.wait_ge(s_kv, 1 + b + 1)
                    dve.tensor_tensor(kv[:], g.bank[1][:, 0:TPB * CTX].rearrange("p (t d) -> p t d", t=TPB),
                                      brow[:].unsqueeze(1).to_broadcast([P, TPB, CTX]), ALU.add).then_inc(s_kvkept, 1)
                    dve.wait_ge(s_outT, 1 + b + 1)
                    dve.tensor_copy(outT[:], g.bank[2][0:CTX, 0:T]).then_inc(s_outTkept, 1)
                    for t in range(TPB):
                        dve.wait_ge(s_sim, 1 + TPB * b + t + 1)
                        own.then(dve.bn_stats(stats[:, t, :], g.bank[3 + t][:, 0:T]))
                    for t in range(TPB):
                        own.wait(1 + t)
                        dve.memset(g.tick[:, t:t + 1], 0.0)
                        dve.bn_aggr(mv[:, t, :], stats[:, t, :]).then_inc(s_var, 1)
                    dve.wait_ge(s_sd, 1 + b + 1)
                    own.then(dve.reciprocal(rstd[:], sd[:]))
                    own.wait()
                    own.then(dve.tensor_scalar(rstd[:], rstd[:], 1.0 / 16, None, ALU.mult))
                    own.wait()
                    for t in range(TPB):
                        own.then(dve.tensor_scalar(sim[:, t, :], g.bank[3 + t][:, 0:T], mv[:, t, 0:1], rstd[:, t:t + 1],
                                                   ALU.subtract, ALU.mult))
                    own.wait()
                    own.then(dve.tensor_tensor(sim[:], sim[:], gamma[:].unsqueeze(1).to_broadcast([P, TPB, T]), ALU.mult))
                    own.wait()
                    own.then(dve.tensor_tensor(sim[:], sim[:], beta[:].unsqueeze(1).to_broadcast([P, TPB, T]), ALU.add))
                    own.wait()
                    own.then(dve.tensor_reduce(negmax[:], sim[:], AX.X, ALU.max, negate=True))
                    own.wait()
                    dve.sem_inc(s_max, 1)
                    dve.wait_ge(s_exp, 1 + b + 1)
                    own.then(dve.reciprocal(rsum[:], sums[:]))
                    own.wait()
                    for t in range(TPB):
                        tile = g.X[:, bass.ds(b * TPB + t, 1), :]
                        own.then(dve.scalar_tensor_tensor(out=tile, in0=sim[:, t:t + 1, :], scalar=rsum[:, t:t + 1], in1=tile,
                                                          op0=ALU.mult, op1=ALU.add))
                    own.wait()
                    own.end()

            @block.scalar
            def _(act):
                act.wait_ge(s_load, 1 + 80)
                with act.Fori(0, B) as b:
                    act.wait_ge(s_kv, 1 + b + 1)
                    act.activation(kvT[:], g.bank[0][0:CTX, 0:T], ACT.Identity, bias=bcol[:, 0:1]).then_inc(s_kvTkept, 1)
                    act.wait_ge(s_var, 1 + TPB * (b + 1))
                    act.activation(sd[:], mv[:, :, 1], ACT.Sqrt, bias=g.eps6[:, 0:1], scale=1.0 / 256).then_inc(s_sd, 1)
                    act.wait_ge(s_max, 1 + b + 1)
                    for t in range(TPB):
                        ins = act.activation(sim[:, t, :], sim[:, t, :], ACT.Exp, bias=negmax[:, t:t + 1],
                                             accum_out=sums[:, t:t + 1])
                    ins.then_inc(s_exp, 1)


def top_weights(nc, g, name, E, TOP, wr_dram, combine, chosen=None):
    with ExitStack() as ctx:
        def sb(n, shape, dt=F32):
            return ctx.enter_context(nc.sbuf_tensor(f"{name}_{n}", shape, dt))

        def sem(n):
            return g.sem(f"{name}_{n}")

        wr = sb("wr", [P, KC, E])
        iota = sb("iota", [P, E])
        probs = sb("probs", [P, NT, E])
        peak, sums, rsum = sb("peak", [P, NT]), sb("sums", [P, NT]), sb("rsum", [P, NT])
        top = sb("top", [P, NT, 8])
        place = sb("place", [P, NT, 8], U32)
        placef = sb("placef", [P, NT, 8])
        hot = sb("hot", [P, NT, E])
        s_load, s_logits, s_shift, s_exp, s_own = sem("load"), sem("logits"), sem("shift"), sem("exp"), sem("own")

        with nc.Block() as block:
            @block.sync
            def _(sp):
                sp.dma_start(wr[:], wr_dram).then_inc(s_load, 16)

            @block.gpsimd
            def _(pool):
                pool.iota(iota[:], [[1, E]], base=0, channel_multiplier=0, allow_small_or_imprecise_dtypes=True).then_inc(s_load, 1)

            @block.tensor
            def _(pe):
                pe.wait_ge(s_load, 1 + 17)
                for t in range(NT):
                    for j in range(KC):
                        mm = pe.matmul(g.bank[0][:, E * t:E * t + E], g.XT[:, j, P * t:P * t + P], wr[:, j, :],
                                       start=(j == 0), stop=(j == KC - 1))
                mm.then_inc(s_logits, 1)

            @block.scalar
            def _(act):
                act.wait_ge(s_shift, 1 + 1)
                act.activation(probs[:], probs[:], ACT.Exp).then_inc(s_exp, 1)

            @block.vector
            def _(dve):
                own = Steps(dve, s_own)

                def step(ins):
                    own.then(ins)
                    own.wait()

                def wide(x):
                    return x.unsqueeze(2).to_broadcast([P, NT, E])

                logits = g.bank[0][:, 0:NT * E].rearrange("p (t e) -> p t e", t=NT)
                dve.wait_ge(s_logits, 1 + 1)
                step(dve.tensor_reduce(peak[:], logits, AX.X, ALU.max))
                dve.tensor_tensor(probs[:], logits, wide(peak[:]), ALU.subtract).then_inc(s_shift, 1)
                dve.wait_ge(s_exp, 1 + 1)
                step(dve.tensor_reduce(sums[:], probs[:], AX.X, ALU.add))
                step(dve.reciprocal(rsum[:], sums[:]))
                step(dve.tensor_tensor(probs[:], probs[:], wide(rsum[:]), ALU.mult))
                for t in range(NT):
                    own.then(dve.max(top[:, t, :], probs[:, t, :]))
                own.wait()
                for t in range(NT):
                    own.then(dve.max_index(place[:, t, :], top[:, t, :], probs[:, t, :]))
                own.wait()
                step(dve.tensor_copy(placef[:], place[:]))
                step(dve.tensor_reduce(sums[:], top[:, :, 0:TOP], AX.X, ALU.add))
                step(dve.reciprocal(rsum[:], sums[:]))
                step(dve.tensor_tensor(top[:], top[:], rsum[:].unsqueeze(2).to_broadcast([P, NT, 8]), ALU.mult))
                for k in range(TOP):
                    to = combine if k == 0 else hot[:]
                    step(dve.tensor_tensor(to, iota[:].unsqueeze(1).to_broadcast([P, NT, E]),
                                           wide(placef[:, :, k]), ALU.is_equal))
                    if chosen is not None:
                        step(dve.tensor_copy(chosen, to) if k == 0 else dve.tensor_tensor(chosen, chosen, to, ALU.add))
                    step(dve.tensor_tensor(to, to, wide(top[:, :, k]), ALU.mult))
                    if k:
                        step(dve.tensor_tensor(combine, combine, to, ALU.add))


E0, I0 = 8, 512


def experts0(nc, g, a):
    NE, NB, HALF = E0 + 1, 3, 512
    NF = I0 // P
    with ExitStack() as ctx:
        def sb(n, shape, dt=F32):
            return ctx.enter_context(nc.sbuf_tensor(f"e0_{n}", shape, dt))

        def sem(n):
            return g.sem(f"e0_{n}")

        combine = sb("combine", [P, NT, E0])
        cw = sb("cw", [P, NT, NE])
        wgu = [sb(f"wgu{i}", [P, KC, 2 * I0]) for i in range(NB)]
        wd = [sb(f"wd{i}", [P, NF, C]) for i in range(NB)]
        silu = sb("silu", [P, 2, HALF])
        act_ = sb("act", [P, 2, NF, HALF])
        s_cw, s_load = sem("cw"), [sem(f"load{i}") for i in range(NB)]
        s_gu, s_silu, s_act, s_down, s_added = sem("gu"), sem("silu"), sem("act"), sem("down"), sem("added")
        GU, DN = 2 * NF, NT // 2

        top_weights(nc, g, "r0", E0, 2, a["L0_gate"], combine[:])
        with nc.Block() as block:
            @block.sync
            def _(sp):
                def load(e, i):
                    sp.dma_start(wgu[i][:], a["L0_wgu"][bass.ds(e, 1)].rearrange("e p k f -> (e p) k f")).then_inc(s_load[i], 16)
                    sp.dma_start(wd[i][:], a["L0_wd"][bass.ds(e, 1)].rearrange("e p k f -> (e p) k f")).then_inc(s_load[i], 16)

                for i in range(NB):
                    load(i, i)
                with sp.Fori(0, NE // NB - 1) as r:
                    for i in range(NB):
                        sp.wait_ge(s_down, 1 + r * (NB * DN) + (i + 1) * DN)
                        load((r + 1) * NB + i, i)

            @block.tensor
            def _(pe):
                with pe.Fori(0, NE // NB) as r:
                    gu0, dn0 = r * (NB * GU), r * (NB * DN)
                    def gate_up(i, n, f):
                        u = (i * 2 + n) * NF + f
                        pe.wait_ge(s_act, 1 + gu0 + max(u - 1, 0))
                        for part in range(2):
                            for j in range(KC):
                                mm = pe.matmul(g.bank[2 * (u % 2) + part][:], wgu[i][:, j, I0 * part + P * f:I0 * part + P * f + P],
                                               g.XT[:, j, HALF * n:HALF * n + HALF], start=(j == 0), stop=(j == KC - 1))
                            mm.then_inc(s_gu, 1)

                    def down(i, n):
                        pe.wait_ge(s_act, 1 + gu0 + (i * 2 + n + 1) * NF)
                        for q in range(2):
                            d = (i * 2 + n) * 2 + q
                            pe.wait_ge(s_added, 1 + dn0 + max(d - 1, 0))
                            for t in range(2):
                                for f in range(NF):
                                    mm = pe.matmul(g.bank[4 + d % 2][:, C * t:C * t + C],
                                                   act_[:, n, f, P * (2 * q + t):P * (2 * q + t) + P], wd[i][:, f, :],
                                                   start=(f == 0), stop=(f == NF - 1))
                            mm.then_inc(s_down, 1)

                    for i in range(NB):
                        pe.wait_ge(s_load[i], 1 + 32 * r + 32)
                        for n in range(2):
                            for f in range(NF):
                                gate_up(i, n, f)
                                if f == 0 and (i or n):
                                    down(i if n else i - 1, 1 - n)
                    down(NB - 1, 1)

            @block.scalar
            def _(act):
                with act.Fori(0, NE // NB) as r:
                    for u in range(NB * GU):
                        act.wait_ge(s_gu, 1 + r * (2 * NB * GU) + 2 * u + 1)
                        act.wait_ge(s_act, 1 + r * (NB * GU) + max(u - 1, 0))
                        act.activation(silu[:, u % 2, :], g.bank[2 * (u % 2)][:], ACT.Silu).then_inc(s_silu, 1)

            @block.vector
            def _(dve):
                dve.tensor_copy(cw[:, :, 0:E0], combine[:]).then_inc(s_cw, 1)
                dve.memset(cw[:, :, E0:NE], 1.0).then_inc(s_cw, 1)
                dve.wait_ge(s_cw, 1 + 2)
                with dve.Fori(0, NE // NB) as r:
                    gu0, dn0 = r * (NB * GU), r * (NB * DN)
                    def add(i, n):
                        for q in range(2):
                            d = (i * 2 + n) * 2 + q
                            dve.wait_ge(s_down, 1 + dn0 + d + 1)
                            for t in range(2):
                                tt = 4 * n + 2 * q + t
                                ins = dve.scalar_tensor_tensor(
                                    out=g.X[:, tt, :], in0=g.bank[4 + d % 2][:, C * t:C * t + C],
                                    scalar=cw[:, tt, bass.ds(r * NB + i, 1)], in1=g.X[:, tt, :], op0=ALU.mult, op1=ALU.add)
                            ins.then_inc(s_added, 1)

                    for i in range(NB):
                        for n in range(2):
                            for f in range(NF):
                                u = (i * 2 + n) * NF + f
                                dve.wait_ge(s_gu, 1 + 2 * gu0 + 2 * u + 2)
                                dve.wait_ge(s_silu, 1 + gu0 + u + 1)
                                dve.wait_ge(s_down, 1 + dn0 + max((i * 2 + n) * 2 - 2, 0))
                                dve.tensor_tensor(act_[:, n, f, :], g.bank[2 * (u % 2) + 1][:], silu[:, u % 2, :],
                                                  ALU.mult).then_inc(s_act, 1)
                                if f == 0 and (i or n):
                                    add(i if n else i - 1, 1 - n)
                    add(NB - 1, 1)


NKH, NVH, DK, DV, TAPS = 8, 16, 64, 128, 4
REP = NVH // NKH
NQT = NKH * DK // P
NVT = NVH * DV // P
NCT = 2 * NQT + NVT
VD = NVH * DV
HG = 4
NG = NVH // HG
LEVELS = [2, 4, 8, 16, 32, 64]


def deltanet(nc, g, a):
    NP2 = NCT // 2
    with ExitStack() as ctx:
        def sb(n, shape, dt=F32):
            return ctx.enter_context(nc.sbuf_tensor(f"dn_{n}", shape, dt))

        def sem(n):
            return g.sem(f"dn_{n}")

        w = sb("w", [P, KC, NCT * P])
        wz = sb("wz", [P, KC, VD])
        wba = sb("wba", [P, KC, 2 * NVH])
        wo = sb("wo", [P, NVT, C])
        taps = sb("taps", [P, NCT, TAPS])
        dt_bias, a_exp = sb("dt_bias", [P, NVH]), sb("a_exp", [P, NVH])
        norm_w = sb("norm_w", [P, DV])
        halves = sb("halves", [P, 2])
        before, upto, after = sb("before", [P, P]), sb("upto", [P, P]), sb("after", [P, P])
        lvl = sb("lvl", [P, 2 * len(LEVELS), P], U32)
        first = sb("first", [P, P])
        xb = sb("xb", [P, KC, T])
        cT = sb("cT", [P, NCT, T])
        gT = cT[:, 0:NVT, :]
        sq = sb("sq", [P, 2 * NQT, T])
        osq = sq[:].rearrange("p m t -> p (m t)")
        ktok = sb("ktok", [P, TPB, NKH * DK])
        vtok = sb("vtok", [P, TPB, VD])
        zs = sb("zs", [P, TPB, VD])
        pre = sb("pre", [P, TPB, 2 * NVH])
        relu, gg = sb("relu", [P, TPB, NVH]), sb("gg", [P, TPB, NVH])
        beta = sb("beta", [P, TPB, NVH])
        nrm, rn = sb("nrm", [P, TPB, 2 * NKH]), sb("rn", [P, TPB, 2 * NKH])
        decay = sb("decay", [P, TPB, 2, NVH])
        bk, nbk, bks = sb("bk", [P, TPB, NVH]), sb("nbk", [P, TPB, NVH]), sb("bks", [P, TPB, NVH])
        rqs, ngam, grq = sb("rqs", [P, TPB, NVH]), sb("ngam", [P, TPB, NVH]), sb("grq", [P, TPB, NVH])
        state = sb("state", [P, NG, REP * DV])
        oss, osd, orstd = sb("oss", [P, TPB, NVH]), sb("osd", [P, TPB, NVH]), sb("orstd", [P, TPB, NVH])
        mgx = [sb(f"mgx{s}", [P, HG, P]) for s in range(2)]
        gmt = [sb(f"gmt{s}", [P, HG, P]) for s in range(2)]
        nt = [sb(f"nt{s}", [P, HG, P]) for s in range(2)]
        tri = [sb(f"tri{s}", [P, HG, P]) for s in range(2)]
        triT = [sb(f"triT{s}", [P, HG, P]) for s in range(2)]
        rhs = [sb(f"rhs{s}", [P, HG, P]) for s in range(2)]
        upd = [sb(f"upd{s}", [P, HG, P]) for s in range(2)]
        aux = [sb(f"aux{s}", [P, HG, P]) for s in range(2)]

        s_w, s_aexp, s_in = sem("w"), sem("aexp"), sem("in")
        s_ba, s_z, s_zkept, s_zw = sem("ba"), sem("z"), sem("zkept"), sem("zw")
        s_pair, s_tap0, s_tap, s_conv, s_silu = sem("pair"), sem("tap0"), sem("tap"), sem("conv"), sem("silu")
        s_sq, s_ss, s_turned, s_backA, s_backD = sem("sq"), sem("ss"), sem("turned"), sem("backA"), sem("backD")
        s_own, s_pre, s_eb, s_l1, s_gg, s_ssk, s_nrm = sem("own"), sem("pre"), sem("eb"), sem("l1"), sem("gg"), sem("ssk"), sem("nrm")
        s_cum, s_decay, s_gates, s_nv = sem("cum"), sem("decay"), sem("gates"), sem("nv")
        s_mg, s_dt, s_exp, s_gm, s_gmown, s_kkq, s_et, s_nt = (sem(x) for x in ("mg", "dt", "exp", "gm", "gmown", "kkq", "et", "nt"))
        s_tinit, s_t0, s_t0kept = sem("tinit"), sem("t0"), sem("t0kept")
        s_x, s_xkept, s_pp, s_ppkept = sem("x"), sem("xkept"), sem("pp"), sem("ppkept")
        s_ks, s_r, s_w_, s_u, s_o, s_okept, s_s, s_skept = (sem(x) for x in ("ks", "r", "w_", "u", "o", "okept", "s", "skept"))
        s_osq, s_oss, s_osd, s_on, s_og = sem("osq"), sem("oss"), sem("osd"), sem("on"), sem("og")
        s_gturned, s_gbackA, s_gbackD, s_out, s_added = sem("gturned"), sem("gbackA"), sem("gbackD"), sem("out"), sem("added")

        U = 2 * NG
        NL = len(LEVELS)
        LV = U * NL
        TG = (NQT + NVT) // 4 * TPB

        def bank(s, i):
            return g.bank[4 * s + i]

        def four(b_):
            return b_[:].rearrange("p (h i) -> p h i", h=HG)

        def at(w_, l, s):
            return (w_ * NL + l) * 2 + s

        with nc.Block() as block:
            @block.sync
            def _(sp):
                loads = [(wba, a["L1_wba"]), (wz, a["L1_wz"]), (w, a["L1_w"]), (taps, a["L1_taps"]),
                         (dt_bias, a["L1_dt"].partition_broadcast(P)), (a_exp, a["L1_alog"].partition_broadcast(P)),
                         (norm_w, a["L1_nw"].partition_broadcast(P)), (halves, a["halves"]), (before, a["before"]),
                         (upto, a["upto"]), (after, a["after"]), (lvl, a["lvl"]), (first, a["first"]), (wo, a["L1_wo2"])]
                for tile, src in loads:
                    sp.dma_start(tile[:], src).then_inc(s_w, 16)
            NLOADS = 16 * 14

            @block.tensor
            def _(pe):
                pe.wait_ge(s_w, 1 + NLOADS)
                with pe.Fori(0, B) as b:
                    pe.wait_ge(s_added, 1 + b * TPB)
                    pe.wait_ge(s_in, 1 + b + 1)
                    for t in range(TPB):
                        for j in range(KC):
                            mm = pe.matmul(g.bank[7][:, 2 * NVH * t:2 * NVH * (t + 1)], xb[:, j, P * t:P * t + P], wba[:, j, :],
                                           start=(j == 0), stop=(j == KC - 1))
                    mm.then_inc(s_ba, 1)
                    for p in range(NP2):
                        pe.wait_ge(s_conv, 1 + b * NP2 + max(p - 1, 0))
                        for i in range(2):
                            for j in range(KC):
                                mm = pe.matmul(g.bank[p % 2][:, T * i:T * i + T], w[:, j, P * (2 * p + i):P * (2 * p + i) + P],
                                               xb[:, j, :], start=(j == 0), stop=(j == KC - 1))
                        mm.then_inc(s_pair, 1)
                        if p < 2 * (VD // 512):
                            t, n = divmod(p, VD // 512)
                            pe.wait_ge(s_zkept, 1 + b * 8 + max(p - 1, 0))
                            for j in range(KC):
                                mm = pe.matmul(g.bank[5 + p % 2][:], xb[:, j, P * t:P * t + P], wz[:, j, 512 * n:512 * n + 512],
                                               start=(j == 0), stop=(j == KC - 1))
                            mm.then_inc(s_z, 1)
                    pe.wait_ge(s_sq, 1 + b + 1)
                    for t in range(TPB):
                        for m in range(2 * NQT):
                            mm = pe.matmul(g.bank[2][:, 2 * NKH * t + 2 * m:2 * NKH * t + 2 * m + 2], sq[:, m, P * t:P * t + P], halves[:],
                                           start=True, stop=True)
                    mm.then_inc(s_ss, 1)
                    pe.wait_ge(s_gg, 1 + b + 1)
                    for c in range(TPB):
                        for i, mask in enumerate((upto, after)):
                            o = NVH * (2 * c + i)
                            mm = pe.matmul(g.bank[7][:, o:o + NVH], mask[:], gg[:, c, :], start=True, stop=True)
                    mm.then_inc(s_cum, 1)
                    for n in range(TG):
                        t, m = divmod(n, TG // TPB)
                        if m == 0 and t == 0:
                            pe.wait_ge(s_silu, 1 + b * NP2 + NP2)
                        pe.wait_ge((s_backA, s_backD)[n % 2], 1 + b * (TG // 2) + n // 2)
                        for i in range(4):
                            mm = pe.transpose(g.bank[3 + n % 2][:, P * i:P * i + P], cT[:, NQT + 4 * m + i, P * t:P * t + P], g.ident[:])
                        mm.then_inc(s_turned, 1)
                    pe.wait_ge(s_backA, 1 + (b + 1) * (TG // 2))
                    pe.wait_ge(s_backD, 1 + (b + 1) * (TG // 2))
                    pe.wait_ge(s_gates, 1 + b + 1)

                    for w_ in range(U // 2):
                        c = w_ // 2
                        pair = [(s, 2 * w_ + s, (2 * w_ + s) % NG) for s in range(2)]
                        for s, u, hg in pair:
                            pe.wait_ge(s_mg, 1 + b * U + u + 1)
                            pe.wait_ge(s_okept, 1 + b * U + max(u - 1, 0))
                            for h in range(HG):
                                mm = pe.matmul(bank(s, 0)[:, P * h:P * h + P], mgx[s][:, h, :], upto[:], start=True, stop=True)
                            mm.then_inc(s_dt, 1)
                        for s, u, hg in pair:
                            if c == 0 and w_:
                                pe.wait_ge(s_skept, 1 + b * NG + hg - 1)
                            if c == 1:
                                pe.wait_ge(s_skept, 1 + b * NG + NG)
                            for k in range(2):
                                q0 = DK * k
                                for i, m in enumerate((hg, NQT + hg)):
                                    mm = pe.matmul(bank(s, 1 + k)[:, P * i:P * i + P],
                                                   cT[q0:q0 + DK, NQT + hg, P * c:P * c + P], cT[q0:q0 + DK, m, P * c:P * c + P],
                                                   start=True, stop=True)
                            mm.then_inc(s_kkq, 1)
                        for s, u, hg in pair:
                            pe.wait_ge(s_tinit, 1 + b * U + u + 1)
                            for h in range(HG):
                                mm = pe.transpose(bank(s, 0)[:, P * h:P * h + P], triT[s][:, h, :], g.ident[:])
                            mm.then_inc(s_t0, 1)
                        for l in range(NL):
                            for s, u, hg in pair:
                                n = at(w_, l, s)
                                if l == 0:
                                    pe.wait_ge(s_t0kept, 1 + b * U + u + 1)
                                else:
                                    pe.wait_ge(s_ppkept, 1 + b * LV + n - 1)
                                for h in range(HG):
                                    mm = pe.matmul(bank(s, 0)[:, P * h:P * h + P], nt[s][:, h, :], tri[s][:, h, :], start=True, stop=True)
                                mm.then_inc(s_x, 1)
                            for s, u, hg in pair:
                                n = at(w_, l, s)
                                pe.wait_ge(s_xkept, 1 + b * LV + n + 1)
                                if l < NL - 1:
                                    for h in range(HG):
                                        pe.matmul(bank(s, 1)[:, P * h:P * h + P], triT[s][:, h, :], mgx[s][:, h, :], start=True, stop=True)
                                for h in range(HG):
                                    mm = pe.matmul(bank(s, 2)[:, P * h:P * h + P], mgx[s][:, h, :], triT[s][:, h, :], start=True, stop=True)
                                mm.then_inc(s_pp, 1)
                        if c == 1:
                            for s, u, hg in pair:
                                pe.wait_ge(s_ppkept, 1 + b * LV + at(w_, NL - 1, s) + 1)
                                for k in range(2):
                                    q0 = DK * k
                                    pe.matmul(bank(s, 1 + k)[:, 0:2 * P], cT[q0:q0 + DK, NQT + hg, P * c:P * c + P],
                                              state[q0:q0 + DK, hg, :], start=True, stop=True)
                                    mm = pe.matmul(bank(s, 1 + k)[:, 2 * P:4 * P], cT[q0:q0 + DK, hg, P * c:P * c + P],
                                                   state[q0:q0 + DK, hg, :], start=True, stop=True)
                                mm.then_inc(s_ks, 1)
                        for s, u, hg in pair:
                            pe.wait_ge(s_ppkept, 1 + b * LV + at(w_, NL - 1, s) + 1)
                            if c == 1:
                                pe.wait_ge(s_r, 1 + b * NG + hg + 1)
                            else:
                                pe.wait_ge(s_nv, 1 + b + 1)
                            for h in range(HG):
                                r = vtok[:, 0, P * (HG * hg + h):P * (HG * hg + h) + P] if c == 0 else rhs[s][:, h, :]
                                mm = pe.matmul(bank(s, 0)[:, P * h:P * h + P], triT[s][:, h, :], r, start=True, stop=True)
                            mm.then_inc(s_w_, 1)
                        for s, u, hg in pair:
                            pe.wait_ge(s_u, 1 + b * U + u + 1)
                            for h in range(HG):
                                mm = pe.matmul(bank(s, 3)[:, P * h:P * h + P], gmt[s][:, h, :], upd[s][:, h, :], start=True, stop=True)
                            mm.then_inc(s_o, 1)
                            if c == 0:
                                for k in range(2):
                                    q0 = DK * k
                                    mm = pe.matmul(bank(s, 1)[q0:q0 + DK, 0:2 * P], ktok[:, 0, P * hg + q0:P * hg + q0 + DK],
                                                   aux[s][:, 2 * k:2 * k + 2, :], start=True, stop=True)
                                mm.then_inc(s_s, 1)
                    pe.wait_ge(s_okept, 1 + b * U + U)
                    for n in range(2 * NVT // 4):
                        t, m = divmod(n, NVT // 4)
                        pe.wait_ge(s_og, 1 + b * TPB + t + 1)
                        pe.wait_ge((s_gbackA, s_gbackD)[n % 2], 1 + b * 4 + n // 2)
                        for i in range(4):
                            mm = pe.transpose(g.bank[n % 2][:, P * i:P * i + P], vtok[:, t, P * (4 * m + i):P * (4 * m + i) + P], g.ident[:])
                        mm.then_inc(s_gturned, 1)
                    pe.wait_ge(s_gbackA, 1 + b * 4 + 4)
                    pe.wait_ge(s_gbackD, 1 + b * 4 + 4)
                    for t in range(TPB):
                        for m in range(NVT):
                            mm = pe.matmul(g.bank[2 + t][:, 0:C], gT[:, m, P * t:P * t + P], wo[:, m, :], start=(m == 0), stop=(m == NVT - 1))
                        mm.then_inc(s_out, 1)

            @block.scalar
            def _(act):
                act.wait_ge(s_w, 1 + NLOADS)
                act.activation(a_exp[:], a_exp[:], ACT.Exp).then_inc(s_aexp, 1)
                with act.Fori(0, B) as b:
                    act.wait_ge(s_pre, 1 + b + 1)
                    act.activation(pre[:], pre[:], ACT.Exp, scale=-1.0).then_inc(s_eb, 1)
                    act.wait_ge(s_eb, 1 + b + 1)
                    act.activation(pre[:, :, NVH:], pre[:, :, NVH:], ACT.Ln, bias=1.0).then_inc(s_l1, 1)
                    act.wait_ge(s_added, 1 + b * TPB)
                    for p in range(NP2 + 1):
                        if p < NP2:
                            act.wait_ge(s_pair, 1 + b * NP2 + p + 1)
                            for i in range(2):
                                ins = act.activation(cT[:, 2 * p + i, :], g.bank[p % 2][:, T * i:T * i + T], ACT.Copy,
                                                     scale=taps[:, 2 * p + i, TAPS - 1:TAPS])
                            ins.then_inc(s_tap0, 1)
                        if p < 8:
                            t, n = divmod(p, VD // 512)
                            act.wait_ge(s_z, 1 + b * 8 + p + 1)
                            act.activation(zs[:, t, 512 * n:512 * n + 512], g.bank[5 + p % 2][:], ACT.Silu).then_inc(s_zkept, 1)
                        if p >= 1:
                            act.wait_ge(s_conv, 1 + b * NP2 + p)
                            act.activation(cT[:, 2 * p - 2:2 * p, :], cT[:, 2 * p - 2:2 * p, :], ACT.Silu).then_inc(s_silu, 1)
                    for n in range(0, TG, 2):
                        t, m = divmod(n, TG // TPB)
                        act.wait_ge(s_turned, 1 + b * TG + n + 1)
                        to = ktok[:, t, :] if m == 0 else vtok[:, t, 512 * (m - 1):512 * m]
                        act.copy(to, g.bank[3][:]).then_inc(s_backA, 1)
                    act.wait_ge(s_ssk, 1 + b + 1)
                    act.activation(nrm[:], nrm[:], ACT.Sqrt).then_inc(s_nrm, 1)
                    act.wait_ge(s_cum, 1 + b + 1)
                    act.activation(decay[:], g.bank[7][:, 0:4 * NVH].rearrange("p (c i h) -> p c i h", c=TPB, i=2),
                                   ACT.Exp).then_inc(s_decay, 1)
                    for w_ in range(U // 2):
                        for s in range(2):
                            u = 2 * w_ + s
                            act.wait_ge(s_dt, 1 + b * U + u + 1)
                            act.activation(gmt[s][:], four(bank(s, 0)), ACT.Exp).then_inc(s_exp, 1)
                        for s in range(2):
                            u = 2 * w_ + s
                            act.wait_ge(s_t0, 1 + b * U + u + 1)
                            act.copy(tri[s][:], four(bank(s, 0))).then_inc(s_t0kept, 1)
                        for l in range(NL):
                            for s in range(2):
                                act.wait_ge(s_x, 1 + b * LV + at(w_, l, s) + 1)
                                act.copy(mgx[s][:], four(bank(s, 0))).then_inc(s_xkept, 1)
                    for t in range(TPB):
                        act.wait_ge(s_okept, 1 + b * U + NG * (t + 1))
                        act.wait_ge(s_oss, 1 + b * TPB + t)
                        act.activation(osq, vtok[:, t, :], ACT.Square).then_inc(s_osq, 1)
                    act.wait_ge(s_oss, 1 + b * TPB + TPB)
                    act.activation(osd[:], oss[:], ACT.Sqrt, scale=1.0 / DV, bias=g.eps6[:, 0:1]).then_inc(s_osd, 1)
                    for n in range(0, 8, 2):
                        t, m = divmod(n, 4)
                        act.wait_ge(s_gturned, 1 + b * 8 + n + 1)
                        act.copy(gT[:, 4 * m:4 * m + 4, P * t:P * t + P], four(g.bank[0])).then_inc(s_gbackA, 1)

            @block.gpsimd
            def _(pool):
                pool.wait_ge(s_w, 1 + NLOADS)
                with pool.Fori(0, B) as b:
                    pool.wait_ge(s_silu, 1 + b * NP2 + NQT)
                    pool.tensor_tensor(sq[:], cT[:, 0:2 * NQT, :], cT[:, 0:2 * NQT, :], ALU.mult).then_inc(s_sq, 1)
                    pool.wait_ge(s_zkept, 1 + b * 8 + 8)
                    z = zs[:].rearrange("p t (h d) -> p (t h) d", d=DV)
                    pool.tensor_tensor(z, z, norm_w[:].unsqueeze(1).to_broadcast([P, TPB * NVH, DV]), ALU.mult).then_inc(s_zw, 1)
                    pool.wait_ge(s_gates, 1 + b + 1)
                    for w_ in range(U // 2):
                        c = w_ // 2
                        for s in range(2):
                            u = 2 * w_ + s
                            hg = u % NG
                            pool.wait_ge(s_pp, 1 + b * LV + max(at(w_ - 1, NL - 1, s) + 1, 0))
                            pool.tensor_tensor(mgx[s][:], after[:].unsqueeze(1).to_broadcast([P, HG, P]),
                                               gg[:, c, HG * hg:HG * hg + HG].unsqueeze(2).to_broadcast([P, HG, P]),
                                               ALU.mult).then_inc(s_mg, 1)
                        if w_ == 0:
                            pool.wait_ge(s_backA, 1 + (b + 1) * (TG // 2))
                            pool.wait_ge(s_backD, 1 + (b + 1) * (TG // 2))
                            for t in range(TPB):
                                v = vtok[:, t, :].rearrange("p (k x) -> p k x", k=NKH)
                                ins = pool.tensor_tensor(v, v, nrm[:, t, NKH:].unsqueeze(2).to_broadcast([P, NKH, REP * DV]), ALU.mult)
                            ins.then_inc(s_nv, 1)
                        for s in range(2):
                            u = 2 * w_ + s
                            pool.wait_ge(s_exp, 1 + b * U + u + 1)
                            pool.tensor_tensor(nt[s][:], gmt[s][:], before[:].unsqueeze(1).to_broadcast([P, HG, P]), ALU.mult).then_inc(s_gmown, 1)
                            pool.wait_ge(s_gmown, 1 + b * U + u + 1)
                            pool.tensor_tensor(gmt[s][:], gmt[s][:], upto[:].unsqueeze(1).to_broadcast([P, HG, P]), ALU.mult).then_inc(s_gm, 1)
                    for t in range(TPB):
                        pool.wait_ge(s_on, 1 + b * TPB + t + 1)
                        pool.wait_ge(s_zw, 1 + b + 1)
                        pool.tensor_tensor(vtok[:, t, :], vtok[:, t, :], zs[:, t, :], ALU.mult).then_inc(s_og, 1)

            @block.vector
            def _(dve):
                dve.wait_ge(s_w, 1 + NLOADS)
                dve.wait_ge(s_aexp, 1 + 1)
                PER = 15 + 5 * NP2 + U
                with dve.Fori(0, B) as b:
                    own = Steps(dve, s_own, b, PER)

                    def step(ins):
                        own.then(ins)
                        own.wait()

                    dve.tensor_copy(xb[:], g.XT[:, :, bass.ts(b, T)]).then_inc(s_in, 1)
                    dve.wait_ge(s_ba, 1 + b + 1)
                    ba = g.bank[7][:, 0:2 * TPB * NVH].rearrange("p (t x) -> p t x", t=TPB)
                    y = pre[:, :, NVH:]
                    own.then(dve.tensor_copy(pre[:, :, 0:NVH], ba[:, :, 0:NVH]))
                    step(dve.tensor_tensor(y, ba[:, :, NVH:], dt_bias[:].unsqueeze(1).to_broadcast([P, TPB, NVH]), ALU.add))
                    step(dve.tensor_scalar(relu[:], y, 0.0, None, ALU.max))
                    step(dve.scalar_tensor_tensor(out=y, in0=relu[:], scalar=2.0, in1=y, op0=ALU.mult, op1=ALU.subtract))
                    dve.sem_inc(s_pre, 1)
                    dve.wait_ge(s_l1, 1 + b + 1)
                    step(dve.tensor_tensor(relu[:], relu[:], y, ALU.add))
                    step(dve.scalar_tensor_tensor(out=gg[:], in0=relu[:], scalar=-1.0,
                                                  in1=a_exp[:].unsqueeze(1).to_broadcast([P, TPB, NVH]), op0=ALU.mult, op1=ALU.mult))
                    dve.tensor_scalar(gg[:], gg[:], -1e30, None, ALU.max).then_inc(s_gg, 1)
                    step(dve.tensor_scalar(beta[:], pre[:, :, 0:NVH], 1.0, None, ALU.add))
                    step(dve.reciprocal(beta[:], beta[:]))
                    for p in range(NP2):
                        dve.wait_ge(s_tap0, 1 + b * NP2 + p + 1)
                        for k in range(1, TAPS):
                            for i in range(2):
                                m = 2 * p + i
                                if k > 1:
                                    own.wait(own.n - 1)
                                ins = dve.scalar_tensor_tensor(
                                    out=cT[:, m, k:T], in0=g.bank[p % 2][:, T * i:T * i + T - k],
                                    scalar=taps[:, m, TAPS - 1 - k:TAPS - k], in1=cT[:, m, k:T], op0=ALU.mult, op1=ALU.add)
                                if k < TAPS - 1 or i == 0:
                                    own.then(ins)
                                else:
                                    ins.then_inc(s_conv, 1)
                    dve.wait_ge(s_ss, 1 + b + 1)
                    dve.tensor_scalar(nrm[:], g.bank[2][:, 0:2 * TPB * NKH].rearrange("p (t x) -> p t x", t=TPB),
                                      1e-24, None, ALU.max).then_inc(s_ssk, 1)
                    for n in range(1, TG, 2):
                        t, m = divmod(n, TG // TPB)
                        dve.wait_ge(s_turned, 1 + b * TG + n + 1)
                        to = ktok[:, t, :] if m == 0 else vtok[:, t, 512 * (m - 1):512 * m]
                        dve.tensor_copy(to, g.bank[4][:]).then_inc(s_backD, 1)
                    dve.wait_ge(s_nrm, 1 + b + 1)
                    step(dve.reciprocal(rn[:], nrm[:]))

                    def by_head(x):
                        return x.unsqueeze(3).to_broadcast([P, TPB, NKH, REP])

                    def split(x):
                        return x.rearrange("p t (k r) -> p t k r", r=REP)

                    step(dve.tensor_tensor(split(bk[:]), split(beta[:]), by_head(rn[:, :, NKH:]), ALU.mult))
                    step(dve.tensor_tensor(split(bk[:]), split(bk[:]), by_head(rn[:, :, NKH:]), ALU.mult))
                    dve.wait_ge(s_decay, 1 + b + 1)
                    own.then(dve.tensor_scalar(nbk[:], bk[:], -1.0, None, ALU.mult))
                    own.then(dve.tensor_tensor(bks[:], bk[:], decay[:, :, 1, :], ALU.mult))
                    own.then(dve.tensor_scalar(ngam[:], decay[:, :, 0, :], -1.0, None, ALU.mult))
                    own.wait()
                    ins = dve.tensor_scalar(split(rqs[:]), by_head(rn[:, :, 0:NKH]), DK ** -0.5, None, ALU.mult)
                    ins.then_inc(s_gates, 1)
                    dve.wait_ge(s_gates, 1 + b + 1)
                    dve.tensor_tensor(grq[:], decay[:, :, 0, :], rqs[:], ALU.mult)

                    def wide(x, c, hg):
                        return x[:, c, HG * hg:HG * hg + HG].unsqueeze(2).to_broadcast([P, HG, P])

                    for w_ in range(U // 2):
                        c = w_ // 2
                        pair = [(s, 2 * w_ + s, (2 * w_ + s) % NG) for s in range(2)]
                        for s, u, hg in pair:
                            dve.wait_ge(s_gm, 1 + b * U + u + 1)
                            dve.wait_ge(s_kkq, 1 + b * U + u + 1)
                            for h in range(HG):
                                ins = dve.scalar_tensor_tensor(out=nt[s][:, h, :], in0=bank(s, 1 + h // 2)[:, P:2 * P],
                                                               scalar=nbk[:, c, HG * hg + h:HG * hg + h + 1], in1=nt[s][:, h, :],
                                                               op0=ALU.mult, op1=ALU.mult)
                            ins.then_inc(s_nt, 1)
                            e = gmt[s][:].rearrange("p (k r) i -> p k r i", k=2)
                            for k in range(2):
                                ins = dve.tensor_tensor(e[:, k], bank(s, 1 + k)[:, 0:P].unsqueeze(1).to_broadcast([P, REP, P]),
                                                        e[:, k], ALU.mult)
                            ins.then_inc(s_et, 1)
                            dve.wait_ge(s_nt, 1 + b * U + u + 1)
                            step(dve.tensor_tensor(triT[s][:], nt[s][:], first[:].unsqueeze(1).to_broadcast([P, HG, P]), ALU.mult))
                            dve.tensor_tensor(triT[s][:], triT[s][:], g.ident[:].unsqueeze(1).to_broadcast([P, HG, P]),
                                              ALU.add).then_inc(s_tinit, 1)
                        for l in range(NL):
                            for s, u, hg in pair:
                                dve.wait_ge(s_pp, 1 + b * LV + at(w_, l, s) + 1)
                                dve.memset(g.tick[:, at(w_, l, s):at(w_, l, s) + 1], 0.0)
                                if l < NL - 1:
                                    dve.copy_predicated(tri[s][:], lvl[:, l, :].unsqueeze(1).to_broadcast([P, HG, P]), four(bank(s, 1)))
                                dve.copy_predicated(triT[s][:], lvl[:, NL + l, :].unsqueeze(1).to_broadcast([P, HG, P]),
                                                    four(bank(s, 2))).then_inc(s_ppkept, 1)
                        if c == 1:
                            for s, u, hg in pair:
                                dve.wait_ge(s_ks, 1 + b * NG + hg + 1)
                                for h in range(HG):
                                    ins = dve.scalar_tensor_tensor(out=rhs[s][:, h, :], in0=bank(s, 1 + h // 2)[:, P * (h % 2):P * (h % 2) + P],
                                                                   scalar=ngam[:, c, HG * hg + h:HG * hg + h + 1],
                                                                   in1=vtok[:, c, P * (HG * hg + h):P * (HG * hg + h) + P],
                                                                   op0=ALU.mult, op1=ALU.add)
                                ins.then_inc(s_r, 1)
                                for k in range(2):
                                    dve.tensor_tensor(aux[s][:, 2 * k:2 * k + 2, :],
                                                      bank(s, 1 + k)[:, 2 * P:4 * P].rearrange("p (h d) -> p h d", h=2),
                                                      wide(grq, c, hg)[:, 2 * k:2 * k + 2, :], ALU.mult)
                        for s, u, hg in pair:
                            dve.wait_ge(s_w_, 1 + b * U + u + 1)
                            if c == 0:
                                dve.tensor_tensor(aux[s][:], four(bank(s, 0)), wide(bks, c, hg), ALU.mult)
                            dve.tensor_tensor(upd[s][:], four(bank(s, 0)), wide(bk, c, hg), ALU.mult).then_inc(s_u, 1)
                        for s, u, hg in pair:
                            dve.wait_ge(s_o, 1 + b * U + u + 1)
                            out = vtok[:, c, 512 * hg:512 * hg + 512].rearrange("p (h d) -> p h d", h=HG)
                            if c == 0:
                                dve.tensor_tensor(out, four(bank(s, 3)), wide(rqs, c, hg), ALU.mult).then_inc(s_okept, 1)
                                dve.wait_ge(s_s, 1 + b * NG + hg + 1)
                                dve.tensor_copy(state[:, hg, :], bank(s, 1)[:, 0:2 * P]).then_inc(s_skept, 1)
                            else:
                                for h in range(HG):
                                    ins = dve.scalar_tensor_tensor(out=out[:, h, :], in0=bank(s, 3)[:, P * h:P * h + P],
                                                                   scalar=rqs[:, c, HG * hg + h:HG * hg + h + 1], in1=aux[s][:, h, :],
                                                                   op0=ALU.mult, op1=ALU.add)
                                ins.then_inc(s_okept, 1)
                    for t in range(TPB):
                        dve.wait_ge(s_osq, 1 + b * TPB + t + 1)
                        dve.tensor_reduce(oss[:, t, :], osq.rearrange("p (h d) -> p h d", d=DV), AX.X, ALU.add).then_inc(s_oss, 1)
                    dve.wait_ge(s_osd, 1 + b + 1)
                    step(dve.reciprocal(orstd[:], osd[:]))
                    for t in range(TPB):
                        o = vtok[:, t, :].rearrange("p (h d) -> p h d", d=DV)
                        dve.tensor_tensor(o, o, orstd[:, t, :].unsqueeze(2).to_broadcast([P, NVH, DV]), ALU.mult).then_inc(s_on, 1)
                    for n in range(1, 8, 2):
                        t, m = divmod(n, 4)
                        dve.wait_ge(s_gturned, 1 + b * 8 + n + 1)
                        dve.tensor_copy(gT[:, 4 * m:4 * m + 4, P * t:P * t + P], four(g.bank[1])).then_inc(s_gbackD, 1)
                    for t in range(TPB):
                        dve.wait_ge(s_out, 1 + b * TPB + t + 1)
                        tile = g.X[:, bass.ds(b * TPB + t, 1), :]
                        dve.tensor_tensor(tile, g.bank[2 + t][:, 0:C].unsqueeze(1), tile, ALU.add).then_inc(s_added, 1)
                    own.end()


E1, TOP1, CAP = 32, 4, 32
F1, FS = 176, 704
GRP = P // CAP
NGRP = E1 // GRP
NFS = -(-FS // P)


def experts1(nc, g, a):
    HALF, FH = 512, F1 // 2
    NSLOT = E1 * CAP
    with ExitStack() as ctx:
        def sb(n, shape, dt=F32):
            return ctx.enter_context(nc.sbuf_tensor(f"e1_{n}", shape, dt))

        def sem(n):
            return g.sem(f"e1_{n}")

        combine, chosen = sb("combine", [P, NT, E1]), sb("chosen", [P, NT, E1])
        before, ones = sb("before", [P, P]), sb("ones", [P, P])
        place = sb("place", [P, NT, E1])
        iota = sb("iota", [P, CAP])
        wsgu, wsd, wse = sb("wsgu", [P, KC, 2 * FS]), sb("wsd", [P, NFS, C]), sb("wse", [P, KC, 1])
        share = sb("share", [P, NT])
        silu = sb("silu", [P, 2, HALF])
        act_ = sb("act", [P, 2, NFS, HALF])
        gate = sb("gate", [P, 2, NSLOT])
        wgate = sb("wgate", [P, 2, NSLOT])
        wgateT = sb("wgateT", [P, NGRP, NTOK])
        xeT = sb("xeT", [P, KC, NSLOT])
        wgu = [sb(f"wgu{i}", [P, GRP, KC, 2 * F1]) for i in range(2)]
        wd = [sb(f"wd{i}", [FH, GRP, 2, C]) for i in range(2)]
        xg = sb("xg", [P, 2, KC, P])
        esilu, eact = sb("esilu", [P, 2, F1]), sb("eact", [P, 2, F1])
        eactT = sb("eactT", [FH, 2, 2, P])
        X0 = sb("X0", [P, NT, C])
        ye = sb("ye", [P, NGRP, C])
        s_w, s_const, s_place, s_own, s_pos = sem("w"), sem("const"), sem("place"), sem("own"), sem("pos")
        s_ew = [sem("ew0"), sem("ew1")]
        s_share, s_sgu, s_ssilu, s_sact, s_sdown, s_sadd = sem("share"), sem("sgu"), sem("ssilu"), sem("sact"), sem("sdown"), sem("sadd")
        s_gate, s_wgate, s_disp, s_turned, s_back, s_xe = sem("gate"), sem("wgate"), sem("disp"), sem("turned"), sem("back"), sem("xe")
        s_xg, s_egu, s_esilu, s_eact = sem("xg"), sem("egu"), sem("esilu"), sem("eact")
        s_eturned, s_eback, s_edown, s_ye, s_comb, s_added = sem("eturned"), sem("eback"), sem("edown"), sem("ye"), sem("comb"), sem("added")
        widths = [min(P, FS - P * f) for f in range(NFS)]

        top_weights(nc, g, "r1", E1, TOP1, a["L1_wr"], combine[:], chosen[:])
        with nc.Block() as block:
            @block.sync
            def _(sp):
                for tile, name in ((before, "before"), (wse, "L1_wse"), (wsgu, "L1_wsgu"), (wsd, "L1_wsd")):
                    sp.dma_start(tile[:], a[name]).then_inc(s_w, 16)

                def load(e, i):
                    sp.dma_start(wgu[i][:], a["L1_wgu"][bass.ds(e, 1)].rearrange("e p g k f -> (e p) g k f")).then_inc(s_ew[i], 16)
                    sp.dma_start(wd[i][:], a["L1_wd"][bass.ds(e, 1)].rearrange("e p g k f -> (e p) g k f")).then_inc(s_ew[i], 16)

                for i in range(2):
                    load(i, i)
                with sp.Fori(0, NGRP // 2 - 1) as r:
                    for i in range(2):
                        sp.wait_ge(s_edown, 1 + 2 * r + i + 1)
                        load(2 * r + 2 + i, i)

            @block.gpsimd
            def _(pool):
                pool.iota(iota[:], [[1, CAP]], base=0, channel_multiplier=0, allow_small_or_imprecise_dtypes=True).then_inc(s_const, 1)
                pool.memset(ones[:], 1.0).then_inc(s_const, 1)
                pool.wait_ge(s_const, 1 + 2)
                pool.wait_ge(s_place, 1 + 1)
                for t in range(NT):
                    if t >= 2:
                        pool.wait_ge(s_turned, 1 + 2 * (t - 1))
                    out = wgate[:, t % 2, :].rearrange("p (e s) -> p e s", e=E1)
                    pool.wait_ge(s_gate, 1 + t + 1)
                    pool.tensor_tensor(out, gate[:, t % 2, :].rearrange("p (e s) -> p e s", e=E1),
                                       combine[:, t, :].unsqueeze(2).to_broadcast([P, E1, CAP]), ALU.mult).then_inc(s_wgate, 1)

            @block.tensor
            def _(pe):
                pe.wait_ge(s_const, 1 + 2)
                pe.wait_ge(s_w, 1 + 64)
                for t in range(NT):
                    for i in range(t + 1):
                        mm = pe.matmul(g.bank[0][:, E1 * t:E1 * t + E1], before[:] if i == t else ones[:], chosen[:, i, :],
                                       start=(i == 0), stop=(i == t))
                mm.then_inc(s_pos, 1)
                for t in range(NT):
                    for j in range(KC):
                        mm = pe.matmul(g.bank[7][:, t:t + 1], g.XT[:, j, P * t:P * t + P], wse[:, j, :], start=(j == 0), stop=(j == KC - 1))
                mm.then_inc(s_share, 1)

                def gate_up(n, f):
                    u = n * NFS + f
                    if u >= 2:
                        pe.wait_ge(s_sact, 1 + u - 1)
                    for part in range(2):
                        for j in range(KC):
                            mm = pe.matmul(g.bank[1 + 2 * (u % 2) + part][0:widths[f], :],
                                           wsgu[:, j, FS * part + P * f:FS * part + P * f + widths[f]],
                                           g.XT[:, j, HALF * n:HALF * n + HALF], start=(j == 0), stop=(j == KC - 1))
                        mm.then_inc(s_sgu, 1)

                def down(n):
                    pe.wait_ge(s_sact, 1 + (n + 1) * NFS)
                    for q in range(2):
                        d = 2 * n + q
                        if d >= 2:
                            pe.wait_ge(s_sadd, 1 + d - 1)
                        for t in range(2):
                            for f in range(NFS):
                                mm = pe.matmul(g.bank[5 + d % 2][:, C * t:C * t + C],
                                               act_[0:widths[f], n, f, P * (2 * q + t):P * (2 * q + t) + P],
                                               wsd[0:widths[f], f, :], start=(f == 0), stop=(f == NFS - 1))
                        mm.then_inc(s_sdown, 1)

                for n in range(2):
                    for f in range(NFS):
                        gate_up(n, f)
                        if f == 0 and n:
                            down(0)
                down(1)

                pe.wait_ge(s_share, 1 + 2)
                pe.wait_ge(s_place, 1 + 1)
                for t in range(NT):
                    pe.wait_ge(s_gate, 1 + t + 1)
                    for j in range(KC):
                        for n in range(2):
                            pe.matmul(g.bank[1 + 2 * j + n][:], X0[:, t, P * j:P * j + P], gate[:, t % 2, HALF * n:HALF * n + HALF],
                                      start=(t == 0), stop=(t == NT - 1)).then_inc(s_disp, 1)
                    pe.wait_ge(s_wgate, 1 + t + 1)
                    for n in range(2):
                        if t:
                            pe.wait_ge(s_back, 1 + 2 * t + n - 1)
                        for i in range(4):
                            mm = pe.transpose(g.bank[(0, 7)[n]][:, P * i:P * i + P],
                                              wgate[:, t % 2, P * (4 * n + i):P * (4 * n + i) + P], g.ident[:])
                        mm.then_inc(s_turned, 1)
                pe.wait_ge(s_xe, 1 + 4)

                with pe.Fori(0, NGRP // 2) as r:
                    def expert_down(i):
                        pe.wait_ge(s_eback, 1 + 2 * r + i + 1)
                        pe.wait_ge(s_ye, 1 + 2 * r)
                        for e in range(GRP):
                            for f in range(2):
                                mm = pe.matmul(g.bank[5 + i][CAP * e:CAP * e + CAP, 0:C], eactT[:, i, f, CAP * e:CAP * e + CAP],
                                               wd[i][:, e, f, :], start=(f == 0), stop=(f == 1), tile_position=(0, CAP * e))
                        mm.then_inc(s_edown, 1)

                    for i in range(2):
                        pe.wait_ge(s_ew[i], 1 + 32 * r + 32)
                        pe.wait_ge(s_xg, 1 + 2 * r + i + 1)
                        pe.wait_ge(s_eact, 1 + 2 * r)
                        for e in range(GRP):
                            for j in range(KC):
                                mm = pe.matmul(g.bank[1 + i][CAP * e:CAP * e + CAP, 0:2 * F1], xg[:, i, j, CAP * e:CAP * e + CAP],
                                               wgu[i][:, e, j, :], start=(j == 0), stop=(j == KC - 1), tile_position=(0, CAP * e))
                        mm.then_inc(s_egu, 1)
                    for i in range(2):
                        pe.wait_ge(s_eact, 1 + 2 * r + i + 1)
                        pe.wait_ge(s_eback, 1 + 2 * r)
                        for f in range(2):
                            mm = pe.transpose(g.bank[3 + i][0:FH, P * f:P * f + P], eact[:, i, FH * f:FH * f + FH], g.ident[:])
                        mm.then_inc(s_eturned, 1)
                    for i in range(2):
                        expert_down(i)

                pe.wait_ge(s_ye, 1 + NGRP)
                pe.wait_ge(s_back, 1 + 2 * NT)
                for t in range(NT):
                    if t >= 2:
                        pe.wait_ge(s_added, 1 + t - 1)
                    for n in range(NGRP):
                        mm = pe.matmul(g.bank[(0, 7)[t % 2]][:, 0:C], wgateT[:, n, P * t:P * t + P], ye[:, n, :],
                                       start=(n == 0), stop=(n == NGRP - 1))
                    mm.then_inc(s_comb, 1)

            @block.scalar
            def _(act):
                act.wait_ge(s_share, 1 + 1)
                act.activation(share[:], g.bank[7][:, 0:NT], ACT.Sigmoid).then_inc(s_share, 1)
                for u in range(2 * NFS):
                    w = widths[u % NFS]
                    act.wait_ge(s_sgu, 1 + 2 * u + 1)
                    if u >= 2:
                        act.wait_ge(s_sact, 1 + u - 1)
                    act.activation(silu[0:w, u % 2, :], g.bank[1 + 2 * (u % 2)][0:w, :], ACT.Silu).then_inc(s_ssilu, 1)
                for t in range(NT):
                    for n in range(2):
                        act.wait_ge(s_turned, 1 + 2 * t + n + 1)
                        act.copy(wgateT[:, 4 * n:4 * n + 4, P * t:P * t + P],
                                 g.bank[(0, 7)[n]][:].rearrange("p (i t) -> p i t", i=4)).then_inc(s_back, 1)
                with act.Fori(0, NGRP // 2) as r:
                    for i in range(2):
                        act.wait_ge(s_egu, 1 + 2 * r + i + 1)
                        act.wait_ge(s_eact, 1 + 2 * r)
                        act.activation(esilu[:, i, :], g.bank[1 + i][:, 0:F1], ACT.Silu).then_inc(s_esilu, 1)
                    for i in range(2):
                        act.wait_ge(s_edown, 1 + 2 * r + i + 1)
                        act.copy(ye[:, bass.ds(2 * r + i, 1), :], g.bank[5 + i][:, 0:C].unsqueeze(1)).then_inc(s_ye, 1)

            @block.vector
            def _(dve):
                own = Steps(dve, s_own)
                dve.wait_ge(s_pos, 1 + 1)
                own.then(dve.tensor_scalar(place[:], chosen[:], -1e4, 1e4, ALU.mult, ALU.add))
                own.wait()
                dve.tensor_tensor(place[:], place[:], g.bank[0][:, 0:NT * E1].rearrange("p (t e) -> p t e", t=NT),
                                  ALU.add).then_inc(s_place, 1)
                own.then(dve.tensor_copy(X0[:], g.X[:]))
                dve.wait_ge(s_share, 1 + 2)
                own.wait()

                def add(n):
                    for q in range(2):
                        d = 2 * n + q
                        dve.wait_ge(s_sdown, 1 + d + 1)
                        for t in range(2):
                            tt = 4 * n + 2 * q + t
                            ins = dve.scalar_tensor_tensor(out=g.X[:, tt, :], in0=g.bank[5 + d % 2][:, C * t:C * t + C],
                                                           scalar=share[:, tt:tt + 1], in1=g.X[:, tt, :], op0=ALU.mult, op1=ALU.add)
                        ins.then_inc(s_sadd, 1)

                for u in range(2 * NFS):
                    n, f = divmod(u, NFS)
                    dve.wait_ge(s_sgu, 1 + 2 * u + 2)
                    dve.wait_ge(s_ssilu, 1 + u + 1)
                    dve.tensor_tensor(act_[0:widths[f], n, f, :], g.bank[2 + 2 * (u % 2)][0:widths[f], :],
                                      silu[0:widths[f], u % 2, :], ALU.mult).then_inc(s_sact, 1)
                    if u == NFS:
                        add(0)
                add(1)
                dve.wait_ge(s_place, 1 + 1)
                dve.wait_ge(s_const, 1 + 2)
                for t in range(NT):
                    if t >= 2:
                        dve.wait_ge(s_disp, 1 + 4 * (t - 1))
                        dve.wait_ge(s_wgate, 1 + t - 1)
                    dve.tensor_tensor(gate[:, t % 2, :].rearrange("p (e s) -> p e s", e=E1),
                                      place[:, t, :].unsqueeze(2).to_broadcast([P, E1, CAP]),
                                      iota[:].unsqueeze(1).to_broadcast([P, E1, CAP]), ALU.is_equal).then_inc(s_gate, 1)
                for j in range(KC):
                    for n in range(2):
                        dve.wait_ge(s_disp, 1 + 4 * (NT - 1) + 2 * j + n + 1)
                        dve.tensor_copy(xeT[:, j, HALF * n:HALF * n + HALF], g.bank[1 + 2 * j + n][:]).then_inc(s_xe, 1)
                dve.wait_ge(s_xe, 1 + 4)
                with dve.Fori(0, NGRP // 2) as r:
                    for i in range(2):
                        dve.wait_ge(s_egu, 1 + 2 * r)
                        dve.tensor_copy(xg[:, i, :, :], xeT[:, :, bass.ds(r * (2 * P) + P * i, P)]).then_inc(s_xg, 1)
                    for i in range(2):
                        dve.wait_ge(s_esilu, 1 + 2 * r + i + 1)
                        dve.wait_ge(s_eturned, 1 + 2 * r)
                        dve.tensor_tensor(eact[:, i, :], g.bank[1 + i][:, F1:2 * F1], esilu[:, i, :], ALU.mult).then_inc(s_eact, 1)
                    for i in range(2):
                        dve.wait_ge(s_eturned, 1 + 2 * r + i + 1)
                        dve.wait_ge(s_edown, 1 + 2 * r)
                        dve.tensor_copy(eactT[:, i, :, :], g.bank[3 + i][0:FH, 0:2 * P].rearrange("p (f t) -> p f t", f=2)).then_inc(s_eback, 1)
                for t in range(NT):
                    dve.wait_ge(s_comb, 1 + t + 1)
                    dve.tensor_tensor(g.X[:, t, :], g.bank[(0, 7)[t % 2]][:, 0:C], g.X[:, t, :], ALU.add).then_inc(s_added, 1)


SEMS = 80


def program(nc, a, out, first=0, last=6):
    with ExitStack() as ctx:
        def sb(name, shape, dt=F32):
            return ctx.enter_context(nc.sbuf_tensor(name, shape, dt))

        g = Shared(sb, lambda name, shape, dt: ctx.enter_context(nc.psum_tensor(name, shape, dt)),
                   lambda name: ctx.enter_context(nc.semaphore(name)))
        order = [("ident", g.ident), ("x", g.X), ("xT", g.XT), ("ctxT", g.ctxT)]
        s_load = g.sem("load")
        pool_of_sems = [g.sem(f"shared{n}") for n in range(SEMS)]
        with nc.Block() as block:
            @block.gpsimd
            def _(pool):
                for sem in pool_of_sems:
                    pool.sem_inc(sem, 1)

            @block.sync
            def _(sp):
                for n, (name, tile) in enumerate(order):
                    sp.dma_start(tile[:], a[name]).then_inc(s_load, 16)

            @block.vector
            def _(dve):
                dve.memset(g.eps_ln[:], LN_EPS)
                dve.memset(g.eps6[:], 1e-6)
                dve.wait_ge(s_load, 16 * len(order))
        subs = [
            lambda: attention(nc, g, "a0", True, a, "L0"),
            lambda: context_softmax(nc, g, a),
            lambda: experts0(nc, g, a),
            lambda: deltanet(nc, g, a),
            lambda: attention(nc, g, "a1", False, a, "L1"),
            lambda: experts1(nc, g, a),
        ]
        for n in range(first, last):
            used = []
            g.sem = lambda name: (used.append(pool_of_sems[len(used)]), used[-1])[1]
            subs[n]()
            layernorm(nc, g, n - first, used if n < last - 1 else [], out if n == last - 1 else None)


def arrays_of(i):
    import numpy as np

    def tiled(w):
        return np.ascontiguousarray(w.reshape(-1, P, w.shape[-1]).transpose(1, 0, 2))

    def slots(wT, second=None):
        lo = wT.reshape(-1, NH, HD)
        hi = np.zeros_like(lo) if second is None else second.reshape(-1, NH, HD)
        return np.concatenate([lo, hi], axis=2).reshape(-1, NH * SLOT)

    def rotated(wT):
        h = wT.reshape(-1, NH, 2, HD // 2)
        return h[:, :, ::-1, :].reshape(wT.shape)

    f = np.float32
    x = np.asarray(i["x"])
    a = {"x": tiled(x.reshape(NTOK, C)), "xT": tiled(x.reshape(NTOK, C).T), "ident": np.eye(P, dtype=f)}
    a["ctxT"] = np.ascontiguousarray(np.asarray(i["ctx_512"]).reshape(NTOK, CTX).T)
    wq, wk, wv, wo = (np.asarray(i["L0_attn_w_" + n]).T for n in "qkvo")
    a["L0_wq"], a["L0_wk"] = (tiled(slots(w, rotated(w))) for w in (wq, wk))
    a["L0_wv"], a["L0_wo"] = tiled(wv), tiled(wo)
    inv = (f(1.0) / f(10000.0) ** (np.arange(0, HD, 2, dtype=f) / f(HD))).astype(f)
    freq = np.outer(np.arange(T, dtype=f), inv).astype(f)
    cos, sin = np.cos(freq).T.astype(f), np.sin(freq).T.astype(f)
    a["rope"] = np.ascontiguousarray(np.tile(np.concatenate([cos, cos, -sin, sin]), (HPT, 1)))
    fold = np.zeros((P, P), f)
    for s in range(0, P, SLOT):
        for r in range(HD):
            for c in (0, HD):
                fold[s + r, s + c + r] = fold[s + HD + r, s + c + r] = 1.0
    a["fold"] = fold
    qi, ki = np.arange(P)[:, None], np.arange(P)[None, :]
    zero = np.zeros((P, P), f)
    a["L0_mask"] = np.concatenate([zero, np.where(ki // 64 <= qi // 64, 0, MASKED).astype(f)], axis=1)
    a["L1_mask"] = np.concatenate([zero, np.where(ki <= qi, 0, MASKED).astype(f)], axis=1)
    a["L1_wq"] = tiled(slots(np.asarray(i["L1_xattn_Wq"]).T))
    kv = np.asarray(i["L1_xattn_Wkv_expand"]).T
    a["L1_wk"] = np.ascontiguousarray(slots(kv[:, :C]))[:, None, :]
    a["L1_wv"] = np.ascontiguousarray(kv[:, C:])[:, None, :]
    a["L1_wo"] = tiled(np.asarray(i["L1_xattn_Wout"]).T)
    a["L0_Wk"] = np.ascontiguousarray(np.asarray(i["L0_xattn_W_k"]).T)
    a["L0_bk"], a["L0_gamma"], a["L0_beta"] = (np.asarray(i["L0_xattn_" + n]) for n in ("b_k", "ln_gamma", "ln_beta"))
    a["L0_gate"] = tiled(np.asarray(i["L0_ffn_gate_w"]))

    def experts(w, shared):
        w = np.concatenate([np.asarray(w), np.asarray(shared)[None]])
        return np.ascontiguousarray(w.reshape(w.shape[0], -1, P, w.shape[2]).transpose(0, 2, 1, 3))

    a["L0_wgu"] = experts(i["L0_ffn_w_gate_up"], i["L0_ffn_shared_gate_up"])
    a["L0_wd"] = experts(i["L0_ffn_w_down"], i["L0_ffn_shared_down"])
    a["L1_wr"] = tiled(np.asarray(i["L1_ffn_Wr"]))
    a["L1_wse"] = tiled(np.asarray(i["L1_ffn_Wse"]))
    a["L1_wsgu"] = tiled(np.concatenate([np.asarray(i["L1_ffn_Wsg"]), np.asarray(i["L1_ffn_Wsu"])], axis=1))
    wsd = np.asarray(i["L1_ffn_Wsd"])
    a["L1_wsd"] = tiled(np.concatenate([wsd, np.zeros((NFS * P - FS, C), f)]))
    gu = np.concatenate([np.asarray(i["L1_ffn_Wg"]), np.asarray(i["L1_ffn_Wu"])], axis=2)
    a["L1_wgu"] = np.ascontiguousarray(gu.reshape(NGRP, GRP, KC, P, 2 * F1).transpose(0, 3, 1, 2, 4))
    a["L1_wd"] = np.ascontiguousarray(np.asarray(i["L1_ffn_Wd"]).reshape(NGRP, GRP, 2, F1 // 2, C).transpose(0, 3, 1, 2, 4))
    pw = np.asarray(i["L1_attn_in_proj_w"]).T
    n = NCT * P
    a["L1_w"], a["L1_wz"], a["L1_wba"] = tiled(pw[:, :n]), tiled(pw[:, n:n + VD]), tiled(pw[:, n + VD:])
    a["L1_taps"] = tiled(np.asarray(i["L1_attn_conv_w"]))
    a["L1_dt"], a["L1_alog"], a["L1_nw"] = (np.asarray(i["L1_attn_" + n]) for n in ("dt_bias", "A_log", "norm_weight"))
    a["L1_wo2"] = tiled(np.asarray(i["L1_attn_out_proj_w"]).T)
    a["halves"] = (np.arange(P)[:, None] // DK == np.arange(2)[None, :]).astype(f)
    r, c = np.arange(P)[:, None], np.arange(P)[None, :]
    a["upto"], a["after"] = (r <= c).astype(f), (r > c).astype(f)
    fill = [(r // (2 * s) == c // (2 * s)) & (r % (2 * s) >= s) & (c % (2 * s) < s) for s in [1] + LEVELS]
    a["first"] = np.ascontiguousarray(fill[0].T).astype(f)
    a["lvl"] = np.stack(fill[1:] + [m.T for m in fill[1:]], axis=1).astype(np.uint32)
    a["before"] = (np.arange(P)[:, None] < np.arange(P)[None, :]).astype(f)
    return a


def kernel(**inputs):
    import numpy as _np
    import concourse.bacc as _bacc
    from concourse import mybir as _mybir
    from concourse.bass_utils import run_bass_kernel_spmd as _run

    nc = _bacc.Bacc("TRN2", target_bir_lowering=False, num_devices=1)
    arrays = arrays_of(inputs)
    aps = {n: nc.dram_tensor(f"in_{n}", a.shape, _mybir.dt.from_np(a.dtype), kind="ExternalInput").ap()
           for n, a in arrays.items()}
    out = nc.dram_tensor("out", (P, NT, C), F32, kind="ExternalOutput").ap()
    program(nc, aps, out)
    r = _run(nc, [{f"in_{n}": a for n, a in arrays.items()}], core_ids=[0])
    return r.results[0]["out"].transpose(1, 0, 2).reshape(B, T, C)
```

```python
from contextlib import ExitStack

import concourse.bass as bass
from concourse import mybir

F32 = mybir.dt.float32
F16 = mybir.dt.float16
U32 = mybir.dt.uint32

ALU = mybir.AluOpType
ACT = mybir.ActivationFunctionType
AX = mybir.AxisListType

P = 128
B, T, C = 4, 256, 256
NT = B * T // P
TPB = T // P
KC = C // P
NTOK = B * T
CTX = 64
LN_EPS = 1e-5

NH, HD = 16, 16
MASKED = -1e30




class Steps:

    def __init__(self, eng, sem, turn=0, per=0):
        self.eng, self.sem, self.turn, self.per, self.n = eng, sem, turn, per, 0

    def then(self, ins):
        ins.then_inc(self.sem, 1)
        self.n += 1
        return self.n

    def wait(self, n=None):
        self.eng.wait_ge(self.sem, 1 + self.turn * self.per + (self.n if n is None else n))

    def end(self):
        assert self.n == self.per, (self.n, self.per)


class LayernormSems:
    def __init__(self, sem):
        self.stats, self.mv, self.sd, self.rstd = (sem("ln_" + n) for n in ("stats", "mv", "sd", "rstd"))
        self.normed, self.turned, self.kept, self.out = (sem("ln_" + n) for n in ("normed", "turned", "kept", "out"))


class Shared:

    def __init__(self, sb, pb, sem):
        self.sem = sem
        self.bank = [pb(f"bank{i}", [P, 512], F32) for i in range(8)]
        self.X, self.XT, self.ctxT = sb("X", [P, NT, C]), sb("XT", [P, KC, NTOK]), sb("ctxT", [CTX, NTOK])
        self.ident, self.tick = sb("ident", [P, P]), sb("tick", [1, 64])
        self.eps_ln, self.eps6 = sb("eps_ln", [P, 1]), sb("eps6", [P, 1])
        self.ln_sems = LayernormSems(sem)


def layernorm(nc, g, call, spent, out=None):
    with ExitStack() as ctx:
        def sb(n, shape, dt=F32):
            return ctx.enter_context(nc.sbuf_tensor(f"ln{call}_{n}", shape, dt))

        stats = sb("stats", [P, NT, 6])
        mv = sb("mv", [P, NT, 2])
        sd = sb("sd", [P, NT])
        rstd = sb("rstd", [P, NT])
        s = g.ln_sems
        each, one, banks = call * NT, call, call * 2 * (NT // 4)

        with nc.Block() as block:
            @block.vector
            def _(dve):
                for t in range(NT):
                    dve.bn_stats(stats[:, t, :], g.X[:, t, :]).then_inc(s.stats, 1)
                for t in range(NT):
                    dve.wait_ge(s.stats, each + t + 1)
                    dve.bn_aggr(mv[:, t, :], stats[:, t, :]).then_inc(s.mv, 1)
                dve.wait_ge(s.sd, one + 1)
                dve.reciprocal(rstd[:], sd[:]).then_inc(s.rstd, 1)
                dve.wait_ge(s.rstd, one + 1)
                for t in range(NT):
                    dve.tensor_scalar(g.X[:, t, :], g.X[:, t, :], mv[:, t, 0:1], rstd[:, t:t + 1],
                                      ALU.subtract, ALU.mult).then_inc(s.normed, 1)
                if out is None:
                    for n in range(NT // 4):
                        dve.wait_ge(s.turned, banks + KC * n + 2)
                        dve.tensor_copy(g.XT[:, 1, 512 * n:512 * n + 512],
                                        g.bank[KC * n + 1][:]).then_inc(s.kept, 1)

            @block.scalar
            def _(act):
                act.wait_ge(s.mv, each + NT)
                act.activation(sd[:], mv[:, :, 1], ACT.Sqrt, bias=g.eps_ln[:, 0:1]).then_inc(s.sd, 1)
                if out is None:
                    for n in range(NT // 4):
                        act.wait_ge(s.turned, banks + KC * n + 1)
                        act.copy(g.XT[:, 0, 512 * n:512 * n + 512], g.bank[KC * n][:]).then_inc(s.kept, 1)

            @block.gpsimd
            def _(pool):
                for sem in spent:
                    pool.sem_clear(sem)
                for sem in spent:
                    pool.sem_inc(sem, 1)

            if out is None:
                @block.tensor
                def _(pe):
                    for n in range(NT // 4):
                        pe.wait_ge(s.normed, each + 4 * n + 4)
                        for k in range(KC):
                            for i in range(4):
                                last = pe.transpose(g.bank[KC * n + k][:, P * i:P * i + P],
                                                    g.X[:, 4 * n + i, P * k:P * k + P], g.ident[:])
                            last.then_inc(s.turned, 1)
            else:
                @block.sync
                def _(sp):
                    for n in range(NT // 4):
                        sp.wait_ge(s.normed, each + 4 * n + 4)
                        sp.dma_start(out[:, 4 * n:4 * n + 4, :], g.X[:, 4 * n:4 * n + 4, :]).then_inc(s.out, 16)
                    sp.wait_ge(s.out, 16 * (NT // 4))


def attention(nc, g, name, rope, a, layer):
    KIN = KC if rope else 1
    NV = 2 if rope else 1
    WID = 3 * P
    HALF = 512
    NU = 2 * 2 * (NTOK // HALF)
    NPT = NH // 2
    SC, TB = 3, 3
    with ExitStack() as ctx:
        def sb(n, shape, dt=F32):
            return ctx.enter_context(nc.sbuf_tensor(f"{name}_{n}", shape, dt))

        def sem(n):
            return g.sem(f"{name}_{n}")

        wq, wo, mask = sb("wq", [P, KC, NV * C]), sb("wo", [P, KC, C]), sb("mask", [P, T])
        wk = sb("wk", [P if rope else CTX, KIN, NV * C])
        wv = sb("wv", [P if rope else CTX, KIN, C])
        spread32, spread = sb("spread32", [P, 4, 4, P]), sb("spread", [P, 4, 4, P], F16)
        loads = [(wq, layer + "_wq"), (wk, layer + "_wk"), (spread32, "spread"), (wv, layer + "_wv"),
                 (mask, layer + "_mask"), (wo, layer + "_wo")]
        if rope:
            table = sb("table", [P, 2, HALF])
            loads[1:1] = [(table, "rope")]
        src = g.XT if rope else g.ctxT[:].unsqueeze(1)
        parts = sb("parts", [P, 2, 2, HALF])
        whole = sb("whole", [P, 2, HALF])
        high, low = sb("high", [P, 2, HALF], F16), sb("low", [P, 2, HALF], F16)
        packs = sb("packs", [P, B, 2, NPT, T], F16)
        pack = sb("pack", [P, 2, NPT, T], F16)
        vhl = sb("vhl", [P, NT, NH, 2 * HD], F16)
        vnow = sb("vnow", [P, TPB, NH * 2 * HD], F16)
        negs = sb("negs", [P, 3, WID])
        negmax, sums, rsum = sb("negmax", [P, TPB, NH]), sb("sums", [P, TPB, NH]), sb("rsum", [P, TPB, NH])
        probs = sb("probs", [P, 3, WID])
        highT, lowT = sb("highT", [P, 3, WID], F16), sb("lowT", [P, 3, WID], F16)
        ctxs, ctxn = sb("ctxs", [P, TPB, NH, HD]), sb("ctxn", [P, NT, C])
        ctxT = sb("ctxT", [P, KC, NTOK])
        s_w, s_spread, s_proj, s_parts, s_whole = sem("w"), sem("spread"), sem("proj"), sem("parts"), sem("whole")
        s_high, s_low, s_rep, s_repA, s_repD = sem("high"), sem("low"), sem("rep"), sem("repA"), sem("repD")
        s_v, s_vhigh, s_vlow, s_pack = sem("v"), sem("vhigh"), sem("vlow"), sem("pack")
        s_scores, s_masked, s_exp, s_turned = sem("scores"), sem("masked"), sem("exp"), sem("turned")
        s_hiT, s_loT, s_pv, s_sum, s_rsum, s_norm = sem("hiT"), sem("loT"), sem("pv"), sem("sum"), sem("rsum"), sem("norm")
        s_fin, s_finkept, s_out, s_added = sem("fin"), sem("finkept"), sem("out"), sem("added")
        units = [(n, i, m) for n in range(NTOK // HALF) for i in range(2) for m in range(2)]

        with nc.Block() as block:
            @block.sync
            def _(sp):
                for tile, n in loads:
                    sp.dma_start(tile[:], a[n]).then_inc(s_w, 16)
                sp.wait_ge(s_repA, 1 + 2 * NU)
                sp.wait_ge(s_repD, 1 + 2 * NU)
                sp.wait_ge(s_vlow, 1 + NT)
                with sp.Fori(0, B) as b:
                    sp.wait_ge(s_scores, 1 + b * NH)
                    sp.dma_start(pack[:], packs[:, bass.ds(b, 1)].rearrange("p b i n t -> p (b i) n t")).then_inc(s_pack, 16)
                    sp.wait_ge(s_pv, 1 + b * NH)
                    sp.dma_start(vnow[:], vhl[:, bass.ts(b, TPB)].rearrange("p t h d -> p t (h d)")).then_inc(s_pack, 16)

            @block.tensor
            def _(pe):
                pe.wait_ge(s_w, 1 + 16 * len(loads))

                def project(u):
                    n, i, m = units[u]
                    w, x, kin = ((wq, g.XT, KC), (wk, src, KIN))[i]
                    if u >= 2:
                        pe.wait_ge(s_parts if rope else s_low, 1 + (NV if rope else 1) * (u - 1))
                    for r in range(NV):
                        for j in range(kin):
                            mm = pe.matmul(g.bank[2 * (u % 2) + r][:], w[:, j, C * r + P * m:C * r + P * m + P],
                                           x[:, j, HALF * n:HALF * n + HALF], start=(j == 0), stop=(j == kin - 1))
                        mm.then_inc(s_proj, 1)

                def replicate(u):
                    n, i, m = units[u]
                    pe.wait_ge(s_low, 1 + u + 1)
                    for j in range(4):
                        pe.wait_ge((s_repA, s_repD)[j % 2], 1 + 2 * u + j // 2)
                        pe.matmul(g.bank[4 + j % 2][:], spread[:, 2 * i, j, :], high[:, u % 2, :], start=True, stop=False)
                        pe.matmul(g.bank[4 + j % 2][:], spread[:, 2 * i + 1, j, :], low[:, u % 2, :],
                                  start=False, stop=True).then_inc(s_rep, 1)

                for u in range(NU):
                    project(u)
                    if u == 0:
                        pe.wait_ge(s_spread, 1 + 1)
                    if u >= 1:
                        replicate(u - 1)
                replicate(NU - 1)
                for t in range(NT):
                    if t >= 2:
                        pe.wait_ge(s_vlow, 1 + t - 1)
                    for j in range(KIN):
                        mm = pe.matmul(g.bank[6 + t % 2][:, 0:C], src[:, j, P * t:P * t + P], wv[:, j, :],
                                       start=(j == 0), stop=(j == KIN - 1))
                    mm.then_inc(s_v, 1)
                pe.wait_ge(s_vlow, 1 + NT)
                pe.wait_ge(s_repA, 1 + 2 * NU)
                pe.wait_ge(s_repD, 1 + 2 * NU)

                def heads(b):
                    def scores(h):
                        p, m = 64 * (h % 2), h // 2
                        if h == 0:
                            pe.wait_ge(s_pack, 1 + 32 * b + 32)
                        pe.wait_ge(s_masked, 1 + b * NH + max(h - SC + 1, 0))
                        qp, kp = pack[p:p + 64, 0, m, :], pack[p:p + 64, 1, m, :]
                        pe.matmul(g.bank[h % SC][:, 0:P], qp[:, 0:P], kp[:, 0:P], start=True, stop=True)
                        pe.matmul(g.bank[h % SC][:, P:WID], qp[:, P:T], kp, start=True, stop=True).then_inc(s_scores, 1)

                    def transposes(h):
                        pe.wait_ge(s_exp, 1 + b * NH + h + 1)
                        pe.wait_ge(s_loT, 1 + b * NH + max(h - TB + 1, 0))
                        for i in range(3):
                            mm = pe.transpose(g.bank[SC + h % TB][:, P * i:P * i + P], probs[:, h % 3, P * i:P * i + P], g.ident[:])
                        mm.then_inc(s_turned, 1)

                    def values(h):
                        pe.wait_ge(s_loT, 1 + b * NH + h + 1)
                        if h == 0:
                            pe.wait_ge(s_sum, 1 + TPB * b)
                        cols = slice(2 * HD * h, 2 * HD * h + 2 * HD)
                        for t, blocks in enumerate((((0, 0),), ((1, 0), (2, 1)))):
                            prods = [(part, i, j) for i, j in blocks for part in (highT, lowT)]
                            for n, (part, i, j) in enumerate(prods):
                                mm = pe.matmul(g.bank[6 + t][:, cols], part[:, h % 3, P * i:P * i + P], vnow[:, j, cols],
                                               start=(n == 0), stop=(n == len(prods) - 1))
                        mm.then_inc(s_pv, 1)

                    for i in range(NH + 4):
                        if i < NH:
                            scores(i)
                        if 2 <= i < NH + 2:
                            transposes(i - 2)
                        if i >= 4:
                            values(i - 4)

                with pe.Fori(0, B) as b:
                    heads(b)
                for n in range(NTOK // HALF):
                    pe.wait_ge(s_norm, 1 + 2 * (n + 1))
                    for j in range(KC):
                        for t in range(4):
                            mm = pe.transpose(g.bank[2 * n + j][:, P * t:P * t + P], ctxn[:, 4 * n + t, P * j:P * j + P], g.ident[:])
                        mm.then_inc(s_fin, 1)
                for t in range(NT):
                    pe.wait_ge(s_finkept, 1 + KC * (t // 4 + 1))
                    if t >= 2:
                        pe.wait_ge(s_added, 1 + t - 1)
                    for j in range(KC):
                        mm = pe.matmul(g.bank[4 + t % 2][:, 0:C], ctxT[:, j, P * t:P * t + P], wo[:, j, :],
                                       start=(j == 0), stop=(j == KC - 1))
                    mm.then_inc(s_out, 1)

            @block.scalar
            def _(act):
                act.wait_ge(s_w, 1 + 16 * len(loads))
                act.copy(spread[:], spread32[:]).then_inc(s_spread, 1)

                def high_part(u):
                    if u >= 2:
                        act.wait_ge(s_rep, 1 + 4 * (u - 1))
                    if rope:
                        act.wait_ge(s_whole, 1 + u + 1)
                        act.copy(high[:, u % 2, :], whole[:, u % 2, :]).then_inc(s_high, 1)
                    else:
                        act.wait_ge(s_proj, 1 + u + 1)
                        act.copy(high[:, u % 2, :], g.bank[2 * (u % 2)][:]).then_inc(s_high, 1)

                def take(u):
                    n, i, m = units[u]
                    for j in (0, 2):
                        act.wait_ge(s_rep, 1 + 4 * u + j + 1)
                        act.copy(packs[:, 2 * n:2 * n + 2, i, 4 * m + j, :],
                                 g.bank[4][:].rearrange("p (b t) -> p b t", b=2)).then_inc(s_repA, 1)

                for u in range(NU + 1):
                    if u < NU:
                        high_part(u)
                    if u >= 1:
                        take(u - 1)
                for t in range(NT):
                    act.wait_ge(s_v, 1 + t + 1)
                    act.copy(vhl[:, t, :, 0:HD], g.bank[6 + t % 2][:, 0:C].rearrange("p (h d) -> p h d", h=NH)).then_inc(s_vhigh, 1)

                with act.Fori(0, B) as b:
                    for h in range(NH + 2):
                        if h < NH:
                            act.wait_ge(s_masked, 1 + b * NH + h + 1)
                            act.wait_ge(s_turned, 1 + b * NH + max(h - 2, 0))
                            act.activation(probs[:, h % 3, 0:P], negs[:, h % 3, 0:P], ACT.Exp, bias=negmax[:, 0, h:h + 1],
                                           scale=-1.0, accum_out=sums[:, 0, h:h + 1])
                            act.activation(probs[:, h % 3, P:WID], negs[:, h % 3, P:WID], ACT.Exp, bias=negmax[:, 1, h:h + 1],
                                           scale=-1.0, accum_out=sums[:, 1, h:h + 1]).then_inc(s_exp, 1)
                        if h >= 2:
                            act.wait_ge(s_turned, 1 + b * NH + h - 1)
                            act.wait_ge(s_pv, 1 + b * NH + max(h - 4, 0))
                            act.copy(highT[:, (h - 2) % 3, :], g.bank[SC + (h - 2) % TB][:, 0:WID]).then_inc(s_hiT, 1)
                for n in range(NTOK // HALF):
                    act.wait_ge(s_fin, 1 + KC * n + 1)
                    act.copy(ctxT[:, 0, HALF * n:HALF * n + HALF], g.bank[2 * n][:]).then_inc(s_finkept, 1)
                    act.wait_ge(s_fin, 1 + KC * n + 2)
                    act.copy(ctxT[:, 1, HALF * n:HALF * n + HALF], g.bank[2 * n + 1][:]).then_inc(s_finkept, 1)

            if rope:
                @block.gpsimd
                def _(pool):
                    for u in range(NU):
                        pool.wait_ge(s_parts, 1 + 2 * u + 2)
                        if u >= 2:
                            pool.wait_ge(s_low, 1 + u - 1)
                        pool.tensor_tensor(whole[:, u % 2, :], parts[:, u % 2, 0, :], parts[:, u % 2, 1, :],
                                           ALU.add).then_inc(s_whole, 1)

            @block.vector
            def _(dve):
                dve.wait_ge(s_w, 1 + 16 * len(loads))

                def rotate(u):
                    for r in range(2):
                        dve.wait_ge(s_proj, 1 + 2 * u + r + 1)
                        if u >= 2:
                            dve.wait_ge(s_whole, 1 + u - 1)
                        dve.tensor_tensor(parts[:, u % 2, r, :], g.bank[2 * (u % 2) + r][:], table[:, r, :],
                                          ALU.mult).then_inc(s_parts, 1)

                def low_part(u):
                    dve.wait_ge(s_high, 1 + u + 1)
                    dve.tensor_tensor(low[:, u % 2, :], whole[:, u % 2, :] if rope else g.bank[2 * (u % 2)][:],
                                      high[:, u % 2, :], ALU.subtract).then_inc(s_low, 1)

                def take(u):
                    n, i, m = units[u]
                    for j in (1, 3):
                        dve.wait_ge(s_rep, 1 + 4 * u + j + 1)
                        dve.tensor_copy(packs[:, 2 * n:2 * n + 2, i, 4 * m + j, :],
                                        g.bank[5][:].rearrange("p (b t) -> p b t", b=2)).then_inc(s_repD, 1)

                for u in range(NU + 1):
                    if rope and u < NU:
                        rotate(u)
                    if not rope and u < NU:
                        low_part(u)
                    if u >= 1:
                        if rope:
                            low_part(u - 1)
                        take(u - 1)
                for t in range(NT):
                    dve.wait_ge(s_vhigh, 1 + t + 1)
                    dve.tensor_tensor(vhl[:, t, :, HD:2 * HD], g.bank[6 + t % 2][:, 0:C].rearrange("p (h d) -> p h d", h=NH),
                                      vhl[:, t, :, 0:HD], ALU.subtract).then_inc(s_vlow, 1)

                with dve.Fori(0, B) as b:
                    def mask_head(h):
                        dve.wait_ge(s_scores, 1 + b * NH + h + 1)
                        dve.wait_ge(s_exp, 1 + b * NH + max(h - 2, 0))
                        dve.memset(g.tick[:, h:h + 1], 0.0)
                        dve.tensor_tensor_reduce(negs[:, h % 3, 0:P], g.bank[h % SC][:, 0:P], mask[:, P:2 * P],
                                                 -0.25, 3e38, ALU.add, ALU.min, negmax[:, 0, h:h + 1])
                        dve.tensor_tensor_reduce(negs[:, h % 3, P:WID], g.bank[h % SC][:, P:WID], mask[:],
                                                 -0.25, 3e38, ALU.add, ALU.min, negmax[:, 1, h:h + 1]).then_inc(s_masked, 1)

                    def low_turned(h):
                        dve.wait_ge(s_hiT, 1 + b * NH + h + 1)
                        dve.tensor_tensor(lowT[:, h % 3, :], g.bank[SC + h % TB][:, 0:WID], highT[:, h % 3, :],
                                          ALU.subtract).then_inc(s_loT, 1)

                    for i in range(NH + 3):
                        if i < NH:
                            mask_head(i)
                        if i >= 3:
                            low_turned(i - 3)
                    dve.wait_ge(s_exp, 1 + b * NH + NH)
                    dve.reciprocal(rsum[:], sums[:]).then_inc(s_rsum, 1)
                    dve.wait_ge(s_pv, 1 + b * NH + NH)
                    for t in range(TPB):
                        dve.tensor_reduce(ctxs[:, t], g.bank[6 + t][:].rearrange("p (h i d) -> p h d i", h=NH, i=2),
                                          AX.X, ALU.add).then_inc(s_sum, 1)
                    dve.wait_ge(s_rsum, 1 + b + 1)
                    dve.wait_ge(s_sum, 1 + TPB * (b + 1))
                    dve.tensor_tensor(ctxn[:, bass.ts(b, TPB)].rearrange("p t (h d) -> p t h d", h=NH), ctxs[:],
                                      rsum[:].unsqueeze(3).to_broadcast([P, TPB, NH, HD]), ALU.mult).then_inc(s_norm, 1)
                for t in range(NT):
                    dve.wait_ge(s_out, 1 + t + 1)
                    dve.tensor_tensor(g.X[:, t, :], g.bank[4 + t % 2][:, 0:C], g.X[:, t, :], ALU.add).then_inc(s_added, 1)


def context_softmax(nc, g, a):
    with ExitStack() as ctx:
        def sb(n, shape, dt=F32):
            return ctx.enter_context(nc.sbuf_tensor(f"c0_{n}", shape, dt))

        def sem(n):
            return g.sem(f"c0_{n}")

        wk = sb("wk", [CTX, CTX])
        bcol, brow = sb("bcol", [CTX, 1]), sb("brow", [P, CTX])
        gamma, beta = sb("gamma", [P, T]), sb("beta", [P, T])
        xb, cb = sb("xb", [P, KC, T]), sb("cb", [CTX, T])
        kvT, kv, outT = sb("kvT", [CTX, T]), sb("kv", [P, TPB, CTX]), sb("outT", [CTX, T])
        stats, mv = sb("stats", [P, TPB, 6]), sb("mv", [P, TPB, 2])
        sd, rstd = sb("sd", [P, TPB]), sb("rstd", [P, TPB])
        sim = sb("sim", [P, TPB, T])
        negmax, sums, rsum = sb("negmax", [P, TPB]), sb("sums", [P, TPB]), sb("rsum", [P, TPB])
        s_load, s_in, s_kv, s_kvkept, s_kvTkept = sem("load"), sem("in"), sem("kv"), sem("kvkept"), sem("kvTkept")
        s_outT, s_outTkept, s_sim, s_var, s_sd = sem("outT"), sem("outTkept"), sem("sim"), sem("var"), sem("sd")
        s_max, s_exp, s_own = sem("max"), sem("exp"), sem("own")
        PER = 12

        with nc.Block() as block:
            @block.sync
            def _(sp):
                sp.dma_start(wk[:], a["L0_Wk"]).then_inc(s_load, 16)
                sp.dma_start(bcol[:], a["L0_bk"].rearrange("(p a) -> p a", a=1)).then_inc(s_load, 16)
                sp.dma_start(brow[:], a["L0_bk"].partition_broadcast(P)).then_inc(s_load, 16)
                sp.dma_start(gamma[:], a["L0_gamma"].partition_broadcast(P)).then_inc(s_load, 16)
                sp.dma_start(beta[:], a["L0_beta"].partition_broadcast(P)).then_inc(s_load, 16)

            @block.tensor
            def _(pe):
                pe.wait_ge(s_load, 1 + 80)
                with pe.Fori(0, B) as b:
                    pe.wait_ge(s_in, 1 + 2 * b + 2)
                    for t in range(TPB):
                        pe.matmul(g.bank[1][:, CTX * t:CTX * t + CTX], cb[:, P * t:P * t + P], wk[:], start=True, stop=True)
                    mm = pe.matmul(g.bank[0][0:CTX, 0:T], wk[:], cb[:], start=True, stop=True)
                    mm.then_inc(s_kv, 1)
                    pe.wait_ge(s_kvkept, 1 + b + 1)
                    for t in range(TPB):
                        mm = pe.matmul(g.bank[2][0:CTX, 0:T], kv[:, t, :], xb[:, t, :], start=(t == 0), stop=(t == TPB - 1))
                    mm.then_inc(s_outT, 1)
                    pe.wait_ge(s_outTkept, 1 + b + 1)
                    pe.wait_ge(s_kvTkept, 1 + b + 1)
                    for t in range(TPB):
                        pe.matmul(g.bank[3 + t][:, 0:T], outT[:, P * t:P * t + P], kvT[:], start=True, stop=True).then_inc(s_sim, 1)

            @block.vector
            def _(dve):
                dve.wait_ge(s_load, 1 + 80)
                with dve.Fori(0, B) as b:
                    own = Steps(dve, s_own, b, PER)
                    dve.tensor_copy(xb[:], g.XT[:, :, bass.ts(b, T)]).then_inc(s_in, 1)
                    dve.tensor_copy(cb[:], g.ctxT[:, bass.ts(b, T)]).then_inc(s_in, 1)
                    dve.wait_ge(s_kv, 1 + b + 1)
                    dve.tensor_tensor(kv[:], g.bank[1][:, 0:TPB * CTX].rearrange("p (t d) -> p t d", t=TPB),
                                      brow[:].unsqueeze(1).to_broadcast([P, TPB, CTX]), ALU.add).then_inc(s_kvkept, 1)
                    dve.wait_ge(s_outT, 1 + b + 1)
                    dve.tensor_copy(outT[:], g.bank[2][0:CTX, 0:T]).then_inc(s_outTkept, 1)
                    for t in range(TPB):
                        dve.wait_ge(s_sim, 1 + TPB * b + t + 1)
                        own.then(dve.bn_stats(stats[:, t, :], g.bank[3 + t][:, 0:T]))
                    for t in range(TPB):
                        own.wait(1 + t)
                        dve.memset(g.tick[:, t:t + 1], 0.0)
                        dve.bn_aggr(mv[:, t, :], stats[:, t, :]).then_inc(s_var, 1)
                    dve.wait_ge(s_sd, 1 + b + 1)
                    own.then(dve.reciprocal(rstd[:], sd[:]))
                    own.wait()
                    own.then(dve.tensor_scalar(rstd[:], rstd[:], 1.0 / 16, None, ALU.mult))
                    own.wait()
                    for t in range(TPB):
                        own.then(dve.tensor_scalar(sim[:, t, :], g.bank[3 + t][:, 0:T], mv[:, t, 0:1], rstd[:, t:t + 1],
                                                   ALU.subtract, ALU.mult))
                    own.wait()
                    own.then(dve.tensor_tensor(sim[:], sim[:], gamma[:].unsqueeze(1).to_broadcast([P, TPB, T]), ALU.mult))
                    own.wait()
                    own.then(dve.tensor_tensor(sim[:], sim[:], beta[:].unsqueeze(1).to_broadcast([P, TPB, T]), ALU.add))
                    own.wait()
                    own.then(dve.tensor_reduce(negmax[:], sim[:], AX.X, ALU.max, negate=True))
                    own.wait()
                    dve.sem_inc(s_max, 1)
                    dve.wait_ge(s_exp, 1 + b + 1)
                    own.then(dve.reciprocal(rsum[:], sums[:]))
                    own.wait()
                    for t in range(TPB):
                        tile = g.X[:, bass.ds(b * TPB + t, 1), :]
                        own.then(dve.scalar_tensor_tensor(out=tile, in0=sim[:, t:t + 1, :], scalar=rsum[:, t:t + 1], in1=tile,
                                                          op0=ALU.mult, op1=ALU.add))
                    own.wait()
                    own.end()

            @block.scalar
            def _(act):
                act.wait_ge(s_load, 1 + 80)
                with act.Fori(0, B) as b:
                    act.wait_ge(s_kv, 1 + b + 1)
                    act.activation(kvT[:], g.bank[0][0:CTX, 0:T], ACT.Identity, bias=bcol[:, 0:1]).then_inc(s_kvTkept, 1)
                    act.wait_ge(s_var, 1 + TPB * (b + 1))
                    act.activation(sd[:], mv[:, :, 1], ACT.Sqrt, bias=g.eps6[:, 0:1], scale=1.0 / 256).then_inc(s_sd, 1)
                    act.wait_ge(s_max, 1 + b + 1)
                    for t in range(TPB):
                        ins = act.activation(sim[:, t, :], sim[:, t, :], ACT.Exp, bias=negmax[:, t:t + 1],
                                             accum_out=sums[:, t:t + 1])
                    ins.then_inc(s_exp, 1)


def top_weights(nc, g, name, E, TOP, wr_dram, combine, chosen=None):
    with ExitStack() as ctx:
        def sb(n, shape, dt=F32):
            return ctx.enter_context(nc.sbuf_tensor(f"{name}_{n}", shape, dt))

        def sem(n):
            return g.sem(f"{name}_{n}")

        wr = sb("wr", [P, KC, E])
        iota = sb("iota", [P, E])
        probs = sb("probs", [P, NT, E])
        peak, sums, rsum = sb("peak", [P, NT]), sb("sums", [P, NT]), sb("rsum", [P, NT])
        top = sb("top", [P, NT, 8])
        place = sb("place", [P, NT, 8], U32)
        placef = sb("placef", [P, NT, 8])
        hot = sb("hot", [P, NT, E])
        s_load, s_logits, s_shift, s_exp, s_own = sem("load"), sem("logits"), sem("shift"), sem("exp"), sem("own")

        with nc.Block() as block:
            @block.sync
            def _(sp):
                sp.dma_start(wr[:], wr_dram).then_inc(s_load, 16)

            @block.gpsimd
            def _(pool):
                pool.iota(iota[:], [[1, E]], base=0, channel_multiplier=0, allow_small_or_imprecise_dtypes=True).then_inc(s_load, 1)

            @block.tensor
            def _(pe):
                pe.wait_ge(s_load, 1 + 17)
                for t in range(NT):
                    for j in range(KC):
                        mm = pe.matmul(g.bank[0][:, E * t:E * t + E], g.XT[:, j, P * t:P * t + P], wr[:, j, :],
                                       start=(j == 0), stop=(j == KC - 1))
                mm.then_inc(s_logits, 1)

            @block.scalar
            def _(act):
                act.wait_ge(s_shift, 1 + 1)
                act.activation(probs[:], probs[:], ACT.Exp).then_inc(s_exp, 1)

            @block.vector
            def _(dve):
                own = Steps(dve, s_own)

                def step(ins):
                    own.then(ins)
                    own.wait()

                def wide(x):
                    return x.unsqueeze(2).to_broadcast([P, NT, E])

                logits = g.bank[0][:, 0:NT * E].rearrange("p (t e) -> p t e", t=NT)
                dve.wait_ge(s_logits, 1 + 1)
                step(dve.tensor_reduce(peak[:], logits, AX.X, ALU.max))
                dve.tensor_tensor(probs[:], logits, wide(peak[:]), ALU.subtract).then_inc(s_shift, 1)
                dve.wait_ge(s_exp, 1 + 1)
                step(dve.tensor_reduce(sums[:], probs[:], AX.X, ALU.add))
                step(dve.reciprocal(rsum[:], sums[:]))
                step(dve.tensor_tensor(probs[:], probs[:], wide(rsum[:]), ALU.mult))
                for t in range(NT):
                    own.then(dve.max(top[:, t, :], probs[:, t, :]))
                own.wait()
                for t in range(NT):
                    own.then(dve.max_index(place[:, t, :], top[:, t, :], probs[:, t, :]))
                own.wait()
                step(dve.tensor_copy(placef[:], place[:]))
                step(dve.tensor_reduce(sums[:], top[:, :, 0:TOP], AX.X, ALU.add))
                step(dve.reciprocal(rsum[:], sums[:]))
                step(dve.tensor_tensor(top[:], top[:], rsum[:].unsqueeze(2).to_broadcast([P, NT, 8]), ALU.mult))
                for k in range(TOP):
                    to = combine if k == 0 else hot[:]
                    step(dve.tensor_tensor(to, iota[:].unsqueeze(1).to_broadcast([P, NT, E]),
                                           wide(placef[:, :, k]), ALU.is_equal))
                    if chosen is not None:
                        step(dve.tensor_copy(chosen, to) if k == 0 else dve.tensor_tensor(chosen, chosen, to, ALU.add))
                    step(dve.tensor_tensor(to, to, wide(top[:, :, k]), ALU.mult))
                    if k:
                        step(dve.tensor_tensor(combine, combine, to, ALU.add))


E0, I0 = 8, 512


def experts0(nc, g, a):
    NE, NB, HALF = E0 + 1, 3, 512
    NF = I0 // P
    with ExitStack() as ctx:
        def sb(n, shape, dt=F32):
            return ctx.enter_context(nc.sbuf_tensor(f"e0_{n}", shape, dt))

        def sem(n):
            return g.sem(f"e0_{n}")

        combine = sb("combine", [P, NT, E0])
        cw = sb("cw", [P, NT, NE])
        wgu = [sb(f"wgu{i}", [P, KC, 2 * I0]) for i in range(NB)]
        wd = [sb(f"wd{i}", [P, NF, C]) for i in range(NB)]
        silu = sb("silu", [P, 2, HALF])
        act_ = sb("act", [P, 2, NF, HALF])
        s_cw, s_load = sem("cw"), [sem(f"load{i}") for i in range(NB)]
        s_gu, s_silu, s_act, s_down, s_added = sem("gu"), sem("silu"), sem("act"), sem("down"), sem("added")
        GU, DN = 2 * NF, NT // 2

        top_weights(nc, g, "r0", E0, 2, a["L0_gate"], combine[:])
        with nc.Block() as block:
            @block.sync
            def _(sp):
                def load(e, i):
                    sp.dma_start(wgu[i][:], a["L0_wgu"][bass.ds(e, 1)].rearrange("e p k f -> (e p) k f")).then_inc(s_load[i], 16)
                    sp.dma_start(wd[i][:], a["L0_wd"][bass.ds(e, 1)].rearrange("e p k f -> (e p) k f")).then_inc(s_load[i], 16)

                for i in range(NB):
                    load(i, i)
                with sp.Fori(0, NE // NB - 1) as r:
                    for i in range(NB):
                        sp.wait_ge(s_down, 1 + r * (NB * DN) + (i + 1) * DN)
                        load((r + 1) * NB + i, i)

            @block.tensor
            def _(pe):
                with pe.Fori(0, NE // NB) as r:
                    gu0, dn0 = r * (NB * GU), r * (NB * DN)
                    def gate_up(i, n, f):
                        u = (i * 2 + n) * NF + f
                        pe.wait_ge(s_act, 1 + gu0 + max(u - 1, 0))
                        for part in range(2):
                            for j in range(KC):
                                mm = pe.matmul(g.bank[2 * (u % 2) + part][:], wgu[i][:, j, I0 * part + P * f:I0 * part + P * f + P],
                                               g.XT[:, j, HALF * n:HALF * n + HALF], start=(j == 0), stop=(j == KC - 1))
                            mm.then_inc(s_gu, 1)

                    def down(i, n):
                        pe.wait_ge(s_act, 1 + gu0 + (i * 2 + n + 1) * NF)
                        for q in range(2):
                            d = (i * 2 + n) * 2 + q
                            pe.wait_ge(s_added, 1 + dn0 + max(d - 1, 0))
                            for t in range(2):
                                for f in range(NF):
                                    mm = pe.matmul(g.bank[4 + d % 2][:, C * t:C * t + C],
                                                   act_[:, n, f, P * (2 * q + t):P * (2 * q + t) + P], wd[i][:, f, :],
                                                   start=(f == 0), stop=(f == NF - 1))
                            mm.then_inc(s_down, 1)

                    for i in range(NB):
                        pe.wait_ge(s_load[i], 1 + 32 * r + 32)
                        for n in range(2):
                            for f in range(NF):
                                gate_up(i, n, f)
                                if f == 0 and (i or n):
                                    down(i if n else i - 1, 1 - n)
                    down(NB - 1, 1)

            @block.scalar
            def _(act):
                with act.Fori(0, NE // NB) as r:
                    for u in range(NB * GU):
                        act.wait_ge(s_gu, 1 + r * (2 * NB * GU) + 2 * u + 1)
                        act.wait_ge(s_act, 1 + r * (NB * GU) + max(u - 1, 0))
                        act.activation(silu[:, u % 2, :], g.bank[2 * (u % 2)][:], ACT.Silu).then_inc(s_silu, 1)

            @block.vector
            def _(dve):
                dve.tensor_copy(cw[:, :, 0:E0], combine[:]).then_inc(s_cw, 1)
                dve.memset(cw[:, :, E0:NE], 1.0).then_inc(s_cw, 1)
                dve.wait_ge(s_cw, 1 + 2)
                with dve.Fori(0, NE // NB) as r:
                    gu0, dn0 = r * (NB * GU), r * (NB * DN)
                    def add(i, n):
                        for q in range(2):
                            d = (i * 2 + n) * 2 + q
                            dve.wait_ge(s_down, 1 + dn0 + d + 1)
                            for t in range(2):
                                tt = 4 * n + 2 * q + t
                                ins = dve.scalar_tensor_tensor(
                                    out=g.X[:, tt, :], in0=g.bank[4 + d % 2][:, C * t:C * t + C],
                                    scalar=cw[:, tt, bass.ds(r * NB + i, 1)], in1=g.X[:, tt, :], op0=ALU.mult, op1=ALU.add)
                            ins.then_inc(s_added, 1)

                    for i in range(NB):
                        for n in range(2):
                            for f in range(NF):
                                u = (i * 2 + n) * NF + f
                                dve.wait_ge(s_gu, 1 + 2 * gu0 + 2 * u + 2)
                                dve.wait_ge(s_silu, 1 + gu0 + u + 1)
                                dve.wait_ge(s_down, 1 + dn0 + max((i * 2 + n) * 2 - 2, 0))
                                dve.tensor_tensor(act_[:, n, f, :], g.bank[2 * (u % 2) + 1][:], silu[:, u % 2, :],
                                                  ALU.mult).then_inc(s_act, 1)
                                if f == 0 and (i or n):
                                    add(i if n else i - 1, 1 - n)
                    add(NB - 1, 1)


NKH, NVH, DK, DV, TAPS = 8, 16, 64, 128, 4
REP = NVH // NKH
NQT = NKH * DK // P
NVT = NVH * DV // P
NCT = 2 * NQT + NVT
VD = NVH * DV
HG = 4
NG = NVH // HG
LEVELS = [2, 4, 8, 16, 32, 64]


def deltanet(nc, g, a):
    NP2 = NCT // 2
    with ExitStack() as ctx:
        def sb(n, shape, dt=F32):
            return ctx.enter_context(nc.sbuf_tensor(f"dn_{n}", shape, dt))

        def sem(n):
            return g.sem(f"dn_{n}")

        w = sb("w", [P, KC, NCT * P])
        wz = sb("wz", [P, KC, VD])
        wba = sb("wba", [P, KC, 2 * NVH])
        wo = sb("wo", [P, NVT, C])
        taps = sb("taps", [P, NCT, TAPS])
        dt_bias, a_exp = sb("dt_bias", [P, NVH]), sb("a_exp", [P, NVH])
        norm_w = sb("norm_w", [P, DV])
        halves = sb("halves", [P, 2])
        before, upto, after = sb("before", [P, P]), sb("upto", [P, P]), sb("after", [P, P])
        lvl = sb("lvl", [P, len(LEVELS), P])
        ones2 = sb("ones2", [P, P])
        ident16, minus16 = sb("ident16", [P, P], F16), sb("minus16", [P, P], F16)
        first = sb("first", [P, P])
        xb = sb("xb", [P, KC, T])
        cT = sb("cT", [P, NCT, T])
        gT = cT[:, 0:NVT, :]
        sq = sb("sq", [P, 2 * NQT, T])
        osq = sq[:].rearrange("p m t -> p (m t)")
        ktok = sb("ktok", [P, TPB, NKH * DK])
        vtok = sb("vtok", [P, TPB, VD])
        zs = sb("zs", [P, TPB, VD])
        pre = sb("pre", [P, TPB, 2 * NVH])
        relu, gg = sb("relu", [P, TPB, NVH]), sb("gg", [P, TPB, NVH])
        beta = sb("beta", [P, TPB, NVH])
        nrm, rn = sb("nrm", [P, TPB, NKH]), sb("rn", [P, TPB, NKH])
        decay = sb("decay", [P, TPB, 2, NVH])
        nbk, bks = sb("nbk", [P, TPB, NVH]), sb("bks", [P, TPB, NVH])
        rqs, ngam, grq = sb("rqs", [P, TPB, NVH]), sb("ngam", [P, TPB, NVH]), sb("grq", [P, TPB, NVH])
        state = sb("state", [P, NG, REP * DV])
        oss, osd, orstd = sb("oss", [P, TPB, NVH]), sb("osd", [P, TPB, NVH]), sb("orstd", [P, TPB, NVH])
        mg = [sb(f"mg{s}", [P, HG, P]) for s in range(2)]
        nt = [sb(f"nt{s}", [P, HG, P]) for s in range(2)]
        gmt = [[sb(f"gmt{s}{r}", [P, HG, P]) for r in range(2)] for s in range(2)]
        ntH = [[sb(f"ntH{s}{r}", [P, HG, P], F16) for r in range(2)] for s in range(2)]
        ntL = [[sb(f"ntL{s}{r}", [P, HG, P], F16) for r in range(2)] for s in range(2)]
        tri = [[sb(f"tri{s}{r}", [P, HG, P], F16) for r in range(2)] for s in range(2)]
        triT = [[sb(f"triT{s}{r}", [P, HG, P], F16) for r in range(2)] for s in range(2)]
        xm = [sb(f"xm{s}", [P, HG, P], F16) for s in range(2)]
        fine = [sb(f"fine{s}", [P, HG, P]) for s in range(2)]
        upd = [sb(f"upd{s}", [P, HG, P]) for s in range(2)]
        aux = [sb(f"aux{s}", [P, HG, P]) for s in range(2)]

        s_w, s_aexp, s_in = sem("w"), sem("aexp"), sem("in")
        s_ba, s_z, s_zkept, s_zw = sem("ba"), sem("z"), sem("zkept"), sem("zw")
        s_pair, s_tap0, s_tap, s_conv, s_silu = sem("pair"), sem("tap0"), sem("tap"), sem("conv"), sem("silu")
        s_sq, s_ss, s_turned, s_backA, s_backD = sem("sq"), sem("ss"), sem("turned"), sem("backA"), sem("backD")
        s_own, s_pre, s_eb, s_l1, s_gg, s_ssk, s_nrm = sem("own"), sem("pre"), sem("eb"), sem("l1"), sem("gg"), sem("ssk"), sem("nrm")
        s_cum, s_decay, s_gates = sem("cum"), sem("decay"), sem("gates")
        s_mg, s_dt, s_exp, s_gm, s_gmown, s_gmu, s_kkq, s_nt = (sem(x) for x in ("mg", "dt", "exp", "gm", "gmown", "gmu", "kkq", "nt"))
        s_tinit, s_t0, s_t0kept = sem("tinit"), sem("t0"), sem("t0kept")
        s_kss, s_kmax, s_ksd, s_kn, s_nth = sem("kss"), sem("kmax"), sem("ksd"), sem("kn"), sem("nth")
        s_x, s_xkept, s_p, s_pkept, s_pt, s_ptkept = (sem(x) for x in ("x", "xkept", "p", "pkept", "pt", "ptkept"))
        s_ks, s_r, s_w_, s_u, s_o, s_okept, s_s, s_skept = (sem(x) for x in ("ks", "r", "w_", "u", "o", "okept", "s", "skept"))
        s_osq, s_oss, s_osd, s_on, s_og = sem("osq"), sem("oss"), sem("osd"), sem("on"), sem("og")
        s_gturned, s_gbackA, s_gbackD, s_out, s_added = sem("gturned"), sem("gbackA"), sem("gbackD"), sem("out"), sem("added")

        U = 2 * NG
        NL = len(LEVELS)
        NS = NL + 1
        W = U // 2
        TG = (NQT + NVT) // 4 * TPB

        def bank(s, i):
            return g.bank[4 * s + i]

        def four(b_):
            return b_[:].rearrange("p (h i) -> p h i", h=HG)

        def turn_of(n):
            return (n // (NVT // 4), 1 + n % (NVT // 4)) if n < TG - TPB else (n - (TG - TPB), 0)

        def pair_of(w_):
            return [(s, 2 * w_ + s, (2 * w_ + s) % NG) for s in range(2)]

        def at(w_, l, s):
            return (w_ * NS + l) * 2 + s

        def atp(w_, l, s):
            return (w_ * NL + l) * 2 + s

        with nc.Block() as block:
            @block.sync
            def _(sp):
                loads = [(wba, a["L1_wba"]), (wz, a["L1_wz"]), (w, a["L1_w"]), (taps, a["L1_taps"]),
                         (dt_bias, a["L1_dt"].partition_broadcast(P)), (a_exp, a["L1_alog"].partition_broadcast(P)),
                         (norm_w, a["L1_nw"].partition_broadcast(P)), (halves, a["halves"]), (ones2, a["ones2"]), (before, a["before"]),
                         (upto, a["upto"]), (after, a["after"]), (lvl, a["lvl"]), (first, a["first"]), (wo, a["L1_wo2"])]
                for tile, src in loads:
                    sp.dma_start(tile[:], src).then_inc(s_w, 16)
            NLOADS = 16 * 15

            @block.tensor
            def _(pe):
                pe.wait_ge(s_w, 1 + NLOADS)
                with pe.Fori(0, B) as b:
                    pe.wait_ge(s_added, 1 + b * TPB)
                    pe.wait_ge(s_in, 1 + b + 1)
                    for t in range(TPB):
                        for j in range(KC):
                            mm = pe.matmul(g.bank[7][:, 2 * NVH * t:2 * NVH * (t + 1)], xb[:, j, P * t:P * t + P], wba[:, j, :],
                                           start=(j == 0), stop=(j == KC - 1))
                    mm.then_inc(s_ba, 1)
                    for p in range(NP2):
                        pe.wait_ge(s_conv, 1 + b * NP2 + max(p - 1, 0))
                        for i in range(2):
                            for j in range(KC):
                                mm = pe.matmul(g.bank[p % 2][:, T * i:T * i + T], w[:, j, P * (2 * p + i):P * (2 * p + i) + P],
                                               xb[:, j, :], start=(j == 0), stop=(j == KC - 1))
                        mm.then_inc(s_pair, 1)
                        if p < 2 * (VD // 512):
                            t, n = divmod(p, VD // 512)
                            pe.wait_ge(s_zkept, 1 + b * 8 + max(p - 1, 0))
                            for j in range(KC):
                                mm = pe.matmul(g.bank[5 + p % 2][:], xb[:, j, P * t:P * t + P], wz[:, j, 512 * n:512 * n + 512],
                                               start=(j == 0), stop=(j == KC - 1))
                            mm.then_inc(s_z, 1)
                    pe.wait_ge(s_sq, 1 + b + 1)
                    for i in range(2):
                        mm = pe.matmul(g.bank[3 + i][:], ones2[:], sq[:, NQT + 2 * i:NQT + 2 * i + 2, :], start=True, stop=True)
                    mm.then_inc(s_kss, 1)
                    for t in range(TPB):
                        for m in range(NQT):
                            mm = pe.matmul(g.bank[2][:, NKH * t + 2 * m:NKH * t + 2 * m + 2], sq[:, m, P * t:P * t + P], halves[:],
                                           start=True, stop=True)
                    mm.then_inc(s_ss, 1)
                    pe.wait_ge(s_gg, 1 + b + 1)
                    for c in range(TPB):
                        for i, mask in enumerate((upto, after)):
                            o = NVH * (2 * c + i)
                            mm = pe.matmul(g.bank[7][:, o:o + NVH], mask[:], gg[:, c, :], start=True, stop=True)
                    mm.then_inc(s_cum, 1)
                    pe.wait_ge(s_kmax, 1 + b + 1)
                    for n in range(TG):
                        t, m = turn_of(n)
                        if n == 0:
                            pe.wait_ge(s_silu, 1 + b * NP2 + NP2)
                        if n == TG - TPB:
                            pe.wait_ge(s_kn, 1 + b + 1)
                        pe.wait_ge((s_backA, s_backD)[n % 2], 1 + b * (TG // 2) + n // 2)
                        for i in range(4):
                            mm = pe.transpose(g.bank[3 + n % 2][:, P * i:P * i + P], cT[:, NQT + 4 * m + i, P * t:P * t + P], g.ident[:])
                        mm.then_inc(s_turned, 1)
                    pe.wait_ge(s_backA, 1 + (b + 1) * (TG // 2))
                    pe.wait_ge(s_backD, 1 + (b + 1) * (TG // 2))
                    pe.wait_ge(s_gates, 1 + b + 1)

                    def decays(w_):
                        for s, u, hg in pair_of(w_):
                            pe.wait_ge(s_mg, 1 + b * U + u + 1)
                            for h in range(HG):
                                mm = pe.matmul(bank(s, 2)[:, P * h:P * h + P], mg[s][:, h, :], upto[:], start=True, stop=True)
                            mm.then_inc(s_dt, 1)

                    def products(w_):
                        for s, u, hg in pair_of(w_):
                            pe.wait_ge(s_exp, 1 + b * U + u + 1)
                            if u >= 4:
                                pe.wait_ge(s_skept, 1 + b * NG + u - 3)
                            c = w_ // 2
                            for k in range(2):
                                q0 = DK * k
                                for i, m in enumerate((hg, NQT + hg)):
                                    mm = pe.matmul(bank(s, 2 + k)[:, P * i:P * i + P],
                                                   cT[q0:q0 + DK, NQT + hg, P * c:P * c + P], cT[q0:q0 + DK, m, P * c:P * c + P],
                                                   start=True, stop=True)
                            mm.then_inc(s_kkq, 1)

                    def turns(w_):
                        for s, u, hg in pair_of(w_):
                            pe.wait_ge(s_tinit, 1 + b * U + u + 1)
                            for h in range(HG):
                                mm = pe.matmul(bank(s, 2)[:, P * h:P * h + P], triT[s][w_ % 2][:, h, :], ident16[:], start=True, stop=True)
                            mm.then_inc(s_t0, 1)

                    def outputs(w_):
                        for s, u, hg in pair_of(w_):
                            pe.wait_ge(s_u, 1 + b * U + u + 1)
                            for h in range(HG):
                                mm = pe.matmul(bank(s, 1)[:, P * h:P * h + P], gmt[s][w_ % 2][:, h, :], upd[s][:, h, :], start=True, stop=True)
                            mm.then_inc(s_o, 1)
                            if w_ < W // 2:
                                for k in range(2):
                                    q0 = DK * k
                                    mm = pe.matmul(bank(s, 3)[q0:q0 + DK, 0:2 * P], ktok[:, 0, P * hg + q0:P * hg + q0 + DK],
                                                   aux[s][:, 2 * k:2 * k + 2, :], start=True, stop=True)
                                mm.then_inc(s_s, 1)

                    decays(0)
                    products(0)
                    turns(0)
                    for w_ in range(W):
                        c, r = w_ // 2, w_ % 2
                        pair = pair_of(w_)
                        for l in range(NL):
                            for s, u, hg in pair:
                                if l == 0:
                                    pe.wait_ge(s_t0kept, 1 + b * U + u + 1)
                                    pe.wait_ge(s_nth, 1 + b * U + u + 1)
                                    pe.wait_ge(s_u, 1 + b * U + max(u - 1, 0))
                                else:
                                    pe.wait_ge(s_pkept, 1 + b * U * NL + atp(w_, l - 1, s) + 1)
                                for h in range(HG):
                                    mm = pe.matmul(bank(s, 0)[:, P * h:P * h + P], ntH[s][r][:, h, :], tri[s][r][:, h, :], start=True, stop=True)
                                mm.then_inc(s_x, 1)
                            if l == 0:
                                if w_:
                                    outputs(w_ - 1)
                                if w_ < W - 1:
                                    decays(w_ + 1)
                            for s, u, hg in pair:
                                if l == 0:
                                    pe.wait_ge(s_okept, 1 + b * U + max(u - 1, 0))
                                else:
                                    pe.wait_ge(s_ptkept, 1 + b * U * NS + at(w_, l - 1, s) + 1)
                                pe.wait_ge(s_xkept, 1 + b * U * NS + at(w_, l, s) + 1)
                                for h in range(HG):
                                    o = bank(s, 0)[:, P * h:P * h + P]
                                    pe.matmul(o, triT[s][r][:, h, :], ident16[:], start=True, stop=False)
                                    mm = pe.matmul(o, triT[s][r][:, h, :], xm[s][:, h, :], start=False, stop=True)
                                mm.then_inc(s_p, 1)
                                for h in range(HG):
                                    o = bank(s, 1)[:, P * h:P * h + P]
                                    pe.matmul(o, ident16[:], triT[s][r][:, h, :], start=True, stop=False)
                                    mm = pe.matmul(o, xm[s][:, h, :], triT[s][r][:, h, :], start=False, stop=True)
                                mm.then_inc(s_pt, 1)
                            if w_ < W - 1 and l == 1:
                                products(w_ + 1)
                            if w_ < W - 1 and l == NL - 1:
                                turns(w_ + 1)
                        for s, u, hg in pair:
                            pe.wait_ge(s_ptkept, 1 + b * U * NS + at(w_, NL - 1, s) + 1)
                            pe.wait_ge(s_gm, 1 + b * U + u + 1)
                            for h in range(HG):
                                o = bank(s, 0)[:, P * h:P * h + P]
                                pe.matmul(o, triT[s][r][:, h, :], minus16[:], start=True, stop=False)
                                pe.matmul(o, ident16[:], ident16[:], start=False, stop=False)
                                pe.matmul(o, ntH[s][r][:, h, :], tri[s][r][:, h, :], start=False, stop=False)
                                mm = pe.matmul(o, ntL[s][r][:, h, :], tri[s][r][:, h, :], start=False, stop=True)
                            mm.then_inc(s_x, 1)
                        for s, u, hg in pair:
                            pe.wait_ge(s_xkept, 1 + b * U * NS + at(w_, NL, s) + 1)
                            for h in range(HG):
                                o = bank(s, 1)[:, P * h:P * h + P]
                                pe.matmul(o, ident16[:], triT[s][r][:, h, :], start=True, stop=False)
                                mm = pe.matmul(o, xm[s][:, h, :], triT[s][r][:, h, :], start=False, stop=True)
                            mm.then_inc(s_pt, 1)
                        if c == 1:
                            if w_ == W // 2:
                                pe.wait_ge(s_skept, 1 + b * NG + NG)
                            for s, u, hg in pair:
                                pe.wait_ge(s_ptkept, 1 + b * U * NS + at(w_, NL, s) + 1)
                                for k in range(2):
                                    q0 = DK * k
                                    pe.matmul(bank(s, k)[:, 0:2 * P], cT[q0:q0 + DK, NQT + hg, P * c:P * c + P],
                                              state[q0:q0 + DK, hg, :], start=True, stop=True)
                                    mm = pe.matmul(bank(s, k)[:, 2 * P:4 * P], cT[q0:q0 + DK, hg, P * c:P * c + P],
                                                   state[q0:q0 + DK, hg, :], start=True, stop=True)
                                mm.then_inc(s_ks, 1)
                        for s, u, hg in pair:
                            pe.wait_ge(s_ptkept, 1 + b * U * NS + at(w_, NL, s) + 1)
                            if c == 1:
                                pe.wait_ge(s_r, 1 + b * NG + hg + 1)
                            for h in range(HG):
                                v = vtok[:, 0, P * (HG * hg + h):P * (HG * hg + h) + P] if c == 0 else upd[s][:, h, :]
                                mm = pe.matmul(bank(s, 0)[:, P * h:P * h + P], fine[s][:, h, :], v, start=True, stop=True)
                            mm.then_inc(s_w_, 1)
                    outputs(W - 1)
                    pe.wait_ge(s_okept, 1 + b * U + U)
                    for n in range(2 * NVT // 4):
                        t, m = divmod(n, NVT // 4)
                        pe.wait_ge(s_og, 1 + b * TPB + t + 1)
                        pe.wait_ge((s_gbackA, s_gbackD)[n % 2], 1 + b * 4 + n // 2)
                        for i in range(4):
                            mm = pe.transpose(g.bank[n % 2][:, P * i:P * i + P], vtok[:, t, P * (4 * m + i):P * (4 * m + i) + P], g.ident[:])
                        mm.then_inc(s_gturned, 1)
                    pe.wait_ge(s_gbackA, 1 + b * 4 + 4)
                    pe.wait_ge(s_gbackD, 1 + b * 4 + 4)
                    for t in range(TPB):
                        for m in range(NVT):
                            mm = pe.matmul(g.bank[2 + t][:, 0:C], gT[:, m, P * t:P * t + P], wo[:, m, :], start=(m == 0), stop=(m == NVT - 1))
                        mm.then_inc(s_out, 1)

            @block.scalar
            def _(act):
                act.wait_ge(s_w, 1 + NLOADS)
                act.activation(a_exp[:], a_exp[:], ACT.Exp).then_inc(s_aexp, 1)
                with act.Fori(0, B) as b:
                    act.wait_ge(s_pre, 1 + b + 1)
                    act.activation(pre[:], pre[:], ACT.Exp, scale=-1.0).then_inc(s_eb, 1)
                    act.wait_ge(s_eb, 1 + b + 1)
                    act.activation(pre[:, :, NVH:], pre[:, :, NVH:], ACT.Ln, bias=1.0).then_inc(s_l1, 1)
                    act.wait_ge(s_added, 1 + b * TPB)
                    for p in range(NP2 + 1):
                        if p < NP2:
                            act.wait_ge(s_pair, 1 + b * NP2 + p + 1)
                            for i in range(2):
                                ins = act.activation(cT[:, 2 * p + i, :], g.bank[p % 2][:, T * i:T * i + T], ACT.Copy,
                                                     scale=taps[:, 2 * p + i, TAPS - 1:TAPS])
                            ins.then_inc(s_tap0, 1)
                        if p < 8:
                            t, n = divmod(p, VD // 512)
                            act.wait_ge(s_z, 1 + b * 8 + p + 1)
                            act.activation(zs[:, t, 512 * n:512 * n + 512], g.bank[5 + p % 2][:], ACT.Silu).then_inc(s_zkept, 1)
                        if p >= 1:
                            act.wait_ge(s_conv, 1 + b * NP2 + p)
                            act.activation(cT[:, 2 * p - 2:2 * p, :], cT[:, 2 * p - 2:2 * p, :], ACT.Silu).then_inc(s_silu, 1)
                    act.wait_ge(s_kmax, 1 + b + 1)
                    act.activation(sq[:, NQT:, :], sq[:, NQT:, :], ACT.Sqrt).then_inc(s_ksd, 1)
                    for n in range(0, TG, 2):
                        t, m = turn_of(n)
                        act.wait_ge(s_turned, 1 + b * TG + n + 1)
                        to = ktok[:, t, :] if m == 0 else vtok[:, t, 512 * (m - 1):512 * m]
                        act.copy(to, g.bank[3][:]).then_inc(s_backA, 1)
                    act.wait_ge(s_ssk, 1 + b + 1)
                    act.activation(nrm[:], nrm[:], ACT.Sqrt).then_inc(s_nrm, 1)
                    act.wait_ge(s_cum, 1 + b + 1)
                    act.activation(decay[:], g.bank[7][:, 0:4 * NVH].rearrange("p (c i h) -> p c i h", c=TPB, i=2),
                                   ACT.Exp).then_inc(s_decay, 1)
                    def exps(w_):
                        for s, u, _ in pair_of(w_):
                            act.wait_ge(s_dt, 1 + b * U + u + 1)
                            act.activation(gmt[s][w_ % 2][:], four(bank(s, 2)), ACT.Exp).then_inc(s_exp, 1)

                    def rounded(w_):
                        for s, u, _ in pair_of(w_):
                            act.wait_ge(s_nt, 1 + b * U + u + 1)
                            act.copy(ntH[s][w_ % 2][:], nt[s][:]).then_inc(s_nth, 1)

                    def begun(w_):
                        for s, u, _ in pair_of(w_):
                            act.wait_ge(s_t0, 1 + b * U + u + 1)
                            act.copy(tri[s][w_ % 2][:], four(bank(s, 2))).then_inc(s_t0kept, 1)

                    exps(0)
                    rounded(0)
                    begun(0)
                    for w_ in range(W):
                        for l in range(NL):
                            for s in range(2):
                                act.wait_ge(s_p, 1 + b * U * NL + atp(w_, l, s) + 1)
                                act.copy(tri[s][w_ % 2][:], four(bank(s, 0))).then_inc(s_pkept, 1)
                                act.wait_ge(s_pt, 1 + b * U * NS + at(w_, l, s) + 1)
                                act.copy(triT[s][w_ % 2][:], four(bank(s, 1))).then_inc(s_ptkept, 1)
                            if w_ < W - 1:
                                if l == 0:
                                    exps(w_ + 1)
                                if l == 4:
                                    rounded(w_ + 1)
                                if l == NL - 1:
                                    begun(w_ + 1)
                        for s in range(2):
                            act.wait_ge(s_pt, 1 + b * U * NS + at(w_, NL, s) + 1)
                            act.copy(fine[s][:], four(bank(s, 1))).then_inc(s_ptkept, 1)
                    for t in range(TPB):
                        act.wait_ge(s_okept, 1 + b * U + NG * (t + 1))
                        act.wait_ge(s_oss, 1 + b * TPB + t)
                        act.activation(osq, vtok[:, t, :], ACT.Square).then_inc(s_osq, 1)
                    act.wait_ge(s_oss, 1 + b * TPB + TPB)
                    act.activation(osd[:], oss[:], ACT.Sqrt, scale=1.0 / DV, bias=g.eps6[:, 0:1]).then_inc(s_osd, 1)
                    for n in range(0, 8, 2):
                        t, m = divmod(n, 4)
                        act.wait_ge(s_gturned, 1 + b * 8 + n + 1)
                        act.copy(gT[:, 4 * m:4 * m + 4, P * t:P * t + P], four(g.bank[0])).then_inc(s_gbackA, 1)

            @block.gpsimd
            def _(pool):
                pool.wait_ge(s_w, 1 + NLOADS)
                with pool.Fori(0, B) as b:
                    pool.wait_ge(s_silu, 1 + b * NP2 + NQT)
                    pool.tensor_tensor(sq[:], cT[:, 0:2 * NQT, :], cT[:, 0:2 * NQT, :], ALU.mult).then_inc(s_sq, 1)
                    pool.wait_ge(s_zkept, 1 + b * 8 + 8)
                    z = zs[:].rearrange("p t (h d) -> p (t h) d", d=DV)
                    pool.tensor_tensor(z, z, norm_w[:].unsqueeze(1).to_broadcast([P, TPB * NVH, DV]), ALU.mult).then_inc(s_zw, 1)
                    pool.wait_ge(s_gates, 1 + b + 1)
                    for w_ in range(W):
                        c, r = w_ // 2, w_ % 2
                        for s, u, hg in pair_of(w_):
                            pool.wait_ge(s_dt, 1 + b * U + max(u - 1, 0))
                            pool.tensor_tensor(mg[s][:], after[:].unsqueeze(1).to_broadcast([P, HG, P]),
                                               gg[:, c, HG * hg:HG * hg + HG].unsqueeze(2).to_broadcast([P, HG, P]),
                                               ALU.mult).then_inc(s_mg, 1)
                        for s, u, hg in pair_of(w_):
                            pool.wait_ge(s_exp, 1 + b * U + u + 1)
                            pool.tensor_tensor(nt[s][:], gmt[s][r][:], before[:].unsqueeze(1).to_broadcast([P, HG, P]), ALU.mult).then_inc(s_gmown, 1)
                        for s, u, hg in pair_of(w_):
                            pool.wait_ge(s_gmown, 1 + b * U + u + 1)
                            pool.tensor_tensor(gmt[s][r][:], gmt[s][r][:], upto[:].unsqueeze(1).to_broadcast([P, HG, P]), ALU.mult).then_inc(s_gmu, 1)
                        for s, u, hg in pair_of(w_):
                            pool.wait_ge(s_nth, 1 + b * U + u + 1)
                            pool.tensor_tensor(ntL[s][r][:], nt[s][:], ntH[s][r][:], ALU.subtract).then_inc(s_gm, 1)
                    for t in range(TPB):
                        pool.wait_ge(s_on, 1 + b * TPB + t + 1)
                        pool.wait_ge(s_zw, 1 + b + 1)
                        pool.tensor_tensor(vtok[:, t, :], vtok[:, t, :], zs[:, t, :], ALU.mult).then_inc(s_og, 1)

            @block.vector
            def _(dve):
                dve.wait_ge(s_w, 1 + NLOADS)
                dve.wait_ge(s_aexp, 1 + 1)
                dve.tensor_copy(ident16[:], g.ident[:])
                dve.tensor_scalar(minus16[:], g.ident[:], -1.0, None, ALU.mult)
                PER = 14 + 5 * NP2 + U
                with dve.Fori(0, B) as b:
                    own = Steps(dve, s_own, b, PER)

                    def step(ins):
                        own.then(ins)
                        own.wait()

                    dve.tensor_copy(xb[:], g.XT[:, :, bass.ts(b, T)]).then_inc(s_in, 1)
                    dve.wait_ge(s_ba, 1 + b + 1)
                    ba = g.bank[7][:, 0:2 * TPB * NVH].rearrange("p (t x) -> p t x", t=TPB)
                    y = pre[:, :, NVH:]
                    own.then(dve.tensor_copy(pre[:, :, 0:NVH], ba[:, :, 0:NVH]))
                    step(dve.tensor_tensor(y, ba[:, :, NVH:], dt_bias[:].unsqueeze(1).to_broadcast([P, TPB, NVH]), ALU.add))
                    step(dve.tensor_scalar(relu[:], y, 0.0, None, ALU.max))
                    step(dve.scalar_tensor_tensor(out=y, in0=relu[:], scalar=2.0, in1=y, op0=ALU.mult, op1=ALU.subtract))
                    dve.sem_inc(s_pre, 1)
                    dve.wait_ge(s_l1, 1 + b + 1)
                    step(dve.tensor_tensor(relu[:], relu[:], y, ALU.add))
                    step(dve.scalar_tensor_tensor(out=gg[:], in0=relu[:], scalar=-1.0,
                                                  in1=a_exp[:].unsqueeze(1).to_broadcast([P, TPB, NVH]), op0=ALU.mult, op1=ALU.mult))
                    dve.tensor_scalar(gg[:], gg[:], -1e30, None, ALU.max).then_inc(s_gg, 1)
                    step(dve.tensor_scalar(beta[:], pre[:, :, 0:NVH], 1.0, None, ALU.add))
                    step(dve.reciprocal(beta[:], beta[:]))
                    for p in range(NP2):
                        dve.wait_ge(s_tap0, 1 + b * NP2 + p + 1)
                        for k in range(1, TAPS):
                            for i in range(2):
                                m = 2 * p + i
                                if k > 1:
                                    own.wait(own.n - 1)
                                ins = dve.scalar_tensor_tensor(
                                    out=cT[:, m, k:T], in0=g.bank[p % 2][:, T * i:T * i + T - k],
                                    scalar=taps[:, m, TAPS - 1 - k:TAPS - k], in1=cT[:, m, k:T], op0=ALU.mult, op1=ALU.add)
                                if k < TAPS - 1 or i == 0:
                                    own.then(ins)
                                else:
                                    ins.then_inc(s_conv, 1)
                    dve.wait_ge(s_kss, 1 + b + 1)
                    for i in range(2):
                        ins = dve.tensor_scalar(sq[:, NQT + 2 * i:NQT + 2 * i + 2, :], g.bank[3 + i][:].rearrange("p (m t) -> p m t", m=2),
                                                1e-24, None, ALU.max)
                    ins.then_inc(s_kmax, 1)
                    dve.wait_ge(s_ss, 1 + b + 1)
                    dve.tensor_scalar(nrm[:], g.bank[2][:, 0:TPB * NKH].rearrange("p (t x) -> p t x", t=TPB),
                                      1e-24, None, ALU.max).then_inc(s_ssk, 1)
                    dve.wait_ge(s_ksd, 1 + b + 1)
                    step(dve.reciprocal(sq[:, NQT:, :], sq[:, NQT:, :]))
                    dve.tensor_tensor(cT[:, NQT:2 * NQT, :], cT[:, NQT:2 * NQT, :], sq[:, NQT:, :], ALU.mult).then_inc(s_kn, 1)
                    for n in range(1, TG, 2):
                        t, m = turn_of(n)
                        dve.wait_ge(s_turned, 1 + b * TG + n + 1)
                        to = ktok[:, t, :] if m == 0 else vtok[:, t, 512 * (m - 1):512 * m]
                        dve.tensor_copy(to, g.bank[4][:]).then_inc(s_backD, 1)
                    dve.wait_ge(s_nrm, 1 + b + 1)
                    step(dve.reciprocal(rn[:], nrm[:]))

                    def by_head(x):
                        return x.unsqueeze(3).to_broadcast([P, TPB, NKH, REP])

                    def split(x):
                        return x.rearrange("p t (k r) -> p t k r", r=REP)

                    dve.wait_ge(s_decay, 1 + b + 1)
                    own.then(dve.tensor_scalar(nbk[:], beta[:], -1.0, None, ALU.mult))
                    own.then(dve.tensor_tensor(bks[:], beta[:], decay[:, :, 1, :], ALU.mult))
                    own.then(dve.tensor_scalar(ngam[:], decay[:, :, 0, :], -1.0, None, ALU.mult))
                    own.wait()
                    ins = dve.tensor_scalar(split(rqs[:]), by_head(rn[:]), DK ** -0.5, None, ALU.mult)
                    ins.then_inc(s_gates, 1)
                    dve.wait_ge(s_gates, 1 + b + 1)
                    dve.tensor_tensor(grq[:], decay[:, :, 0, :], rqs[:], ALU.mult)

                    def wide(x, c, hg):
                        return x[:, c, HG * hg:HG * hg + HG].unsqueeze(2).to_broadcast([P, HG, P])

                    def couplings(w_):
                        c = w_ // 2
                        for s, u, hg in pair_of(w_):
                            dve.wait_ge(s_gmown, 1 + b * U + u + 1)
                            dve.wait_ge(s_kkq, 1 + b * U + u + 1)
                            for h in range(HG):
                                ins = dve.scalar_tensor_tensor(out=nt[s][:, h, :], in0=bank(s, 2 + h // 2)[:, P:2 * P],
                                                               scalar=nbk[:, c, HG * hg + h:HG * hg + h + 1], in1=nt[s][:, h, :],
                                                               op0=ALU.mult, op1=ALU.mult)
                            ins.then_inc(s_nt, 1)

                    def scores(w_):
                        for s, u, hg in pair_of(w_):
                            dve.wait_ge(s_gmu, 1 + b * U + u + 1)
                            e = gmt[s][w_ % 2][:].rearrange("p (k r) i -> p k r i", k=2)
                            for k in range(2):
                                dve.tensor_tensor(e[:, k], bank(s, 2 + k)[:, 0:P].unsqueeze(1).to_broadcast([P, REP, P]),
                                                  e[:, k], ALU.mult)

                    def starts(w_):
                        for s, u, hg in pair_of(w_):
                            dve.wait_ge(s_nt, 1 + b * U + u + 1)
                            own.then(dve.tensor_tensor(triT[s][w_ % 2][:], nt[s][:], first[:].unsqueeze(1).to_broadcast([P, HG, P]), ALU.mult))
                        for s, u, hg in pair_of(w_):
                            own.wait(own.n - 1 + s)
                            dve.tensor_tensor(triT[s][w_ % 2][:], triT[s][w_ % 2][:], g.ident[:].unsqueeze(1).to_broadcast([P, HG, P]),
                                              ALU.add).then_inc(s_tinit, 1)

                    def kept(w_):
                        for s, u, hg in pair_of(w_):
                            c = w_ // 2
                            dve.wait_ge(s_o, 1 + b * U + u + 1)
                            out = vtok[:, c, 512 * hg:512 * hg + 512].rearrange("p (h d) -> p h d", h=HG)
                            if c == 0:
                                dve.tensor_tensor(out, four(bank(s, 1)), wide(rqs, c, hg), ALU.mult).then_inc(s_okept, 1)
                                dve.wait_ge(s_s, 1 + b * NG + hg + 1)
                                dve.tensor_copy(state[:, hg, :], bank(s, 3)[:, 0:2 * P]).then_inc(s_skept, 1)
                            else:
                                for h in range(HG):
                                    ins = dve.scalar_tensor_tensor(out=out[:, h, :], in0=bank(s, 1)[:, P * h:P * h + P],
                                                                   scalar=rqs[:, c, HG * hg + h:HG * hg + h + 1], in1=aux[s][:, h, :],
                                                                   op0=ALU.mult, op1=ALU.add)
                                ins.then_inc(s_okept, 1)

                    couplings(0)
                    scores(0)
                    starts(0)
                    for w_ in range(W):
                        c = w_ // 2
                        for l in range(NL):
                            for s in range(2):
                                dve.wait_ge(s_x, 1 + b * U * NS + at(w_, l, s) + 1)
                                dve.tensor_tensor(xm[s][:], four(bank(s, 0)), lvl[:, l, :].unsqueeze(1).to_broadcast([P, HG, P]),
                                                  ALU.mult).then_inc(s_xkept, 1)
                            if w_ and l == 0:
                                kept(w_ - 1)
                            if w_ < W - 1:
                                if l == 2:
                                    couplings(w_ + 1)
                                if l == 3:
                                    scores(w_ + 1)
                                if l == 4:
                                    starts(w_ + 1)
                        for s in range(2):
                            dve.wait_ge(s_x, 1 + b * U * NS + at(w_, NL, s) + 1)
                            dve.tensor_copy(xm[s][:], four(bank(s, 0))).then_inc(s_xkept, 1)
                        if c == 1:
                            for s, u, hg in pair_of(w_):
                                dve.wait_ge(s_ks, 1 + b * NG + hg + 1)
                                for h in range(HG):
                                    ins = dve.scalar_tensor_tensor(out=upd[s][:, h, :], in0=bank(s, h // 2)[:, P * (h % 2):P * (h % 2) + P],
                                                                   scalar=ngam[:, c, HG * hg + h:HG * hg + h + 1],
                                                                   in1=vtok[:, c, P * (HG * hg + h):P * (HG * hg + h) + P],
                                                                   op0=ALU.mult, op1=ALU.add)
                                for k in range(2):
                                    ins = dve.tensor_tensor(aux[s][:, 2 * k:2 * k + 2, :],
                                                            bank(s, k)[:, 2 * P:4 * P].rearrange("p (h d) -> p h d", h=2),
                                                            wide(grq, c, hg)[:, 2 * k:2 * k + 2, :], ALU.mult)
                                ins.then_inc(s_r, 1)
                        for s, u, hg in pair_of(w_):
                            dve.wait_ge(s_w_, 1 + b * U + u + 1)
                            if c == 0:
                                dve.tensor_tensor(aux[s][:], four(bank(s, 0)), wide(bks, c, hg), ALU.mult)
                            dve.tensor_tensor(upd[s][:], four(bank(s, 0)), wide(beta, c, hg), ALU.mult).then_inc(s_u, 1)
                    kept(W - 1)
                    for t in range(TPB):
                        dve.wait_ge(s_osq, 1 + b * TPB + t + 1)
                        dve.tensor_reduce(oss[:, t, :], osq.rearrange("p (h d) -> p h d", d=DV), AX.X, ALU.add).then_inc(s_oss, 1)
                    dve.wait_ge(s_osd, 1 + b + 1)
                    step(dve.reciprocal(orstd[:], osd[:]))
                    for t in range(TPB):
                        o = vtok[:, t, :].rearrange("p (h d) -> p h d", d=DV)
                        dve.tensor_tensor(o, o, orstd[:, t, :].unsqueeze(2).to_broadcast([P, NVH, DV]), ALU.mult).then_inc(s_on, 1)
                    for n in range(1, 8, 2):
                        t, m = divmod(n, 4)
                        dve.wait_ge(s_gturned, 1 + b * 8 + n + 1)
                        dve.tensor_copy(gT[:, 4 * m:4 * m + 4, P * t:P * t + P], four(g.bank[1])).then_inc(s_gbackD, 1)
                    for t in range(TPB):
                        dve.wait_ge(s_out, 1 + b * TPB + t + 1)
                        tile = g.X[:, bass.ds(b * TPB + t, 1), :]
                        dve.tensor_tensor(tile, g.bank[2 + t][:, 0:C].unsqueeze(1), tile, ALU.add).then_inc(s_added, 1)
                    own.end()


E1, TOP1, CAP = 32, 4, 32
F1, FS = 176, 704
GRP = P // CAP
NGRP = E1 // GRP
NFS = -(-FS // P)


def experts1(nc, g, a):
    HALF, FH = 512, F1 // 2
    NSLOT = E1 * CAP
    with ExitStack() as ctx:
        def sb(n, shape, dt=F32):
            return ctx.enter_context(nc.sbuf_tensor(f"e1_{n}", shape, dt))

        def sem(n):
            return g.sem(f"e1_{n}")

        combine, chosen = sb("combine", [P, NT, E1]), sb("chosen", [P, NT, E1])
        before, ones = sb("before", [P, P]), sb("ones", [P, P])
        place = sb("place", [P, NT, E1])
        iota = sb("iota", [P, CAP])
        wsgu, wsd, wse = sb("wsgu", [P, KC, 2 * FS]), sb("wsd", [P, NFS, C]), sb("wse", [P, KC, 1])
        share = sb("share", [P, NT])
        silu = sb("silu", [P, 2, HALF])
        act_ = sb("act", [P, 2, NFS, HALF])
        gate = sb("gate", [P, 2, NSLOT])
        wgate = sb("wgate", [P, 2, NSLOT])
        wgateT = sb("wgateT", [P, NGRP, NTOK])
        xeT = sb("xeT", [P, KC, NSLOT])
        wgu = [sb(f"wgu{i}", [P, GRP, KC, 2 * F1]) for i in range(2)]
        wd = [sb(f"wd{i}", [FH, GRP, 2, C]) for i in range(2)]
        xg = sb("xg", [P, 2, KC, P])
        esilu, eact = sb("esilu", [P, 2, F1]), sb("eact", [P, 2, F1])
        eactT = sb("eactT", [FH, 2, 2, P])
        X0 = sb("X0", [P, NT, C])
        ye = sb("ye", [P, NGRP, C])
        s_w, s_const, s_place, s_own, s_pos = sem("w"), sem("const"), sem("place"), sem("own"), sem("pos")
        s_ew = [sem("ew0"), sem("ew1")]
        s_share, s_sgu, s_ssilu, s_sact, s_sdown, s_sadd = sem("share"), sem("sgu"), sem("ssilu"), sem("sact"), sem("sdown"), sem("sadd")
        s_gate, s_wgate, s_disp, s_turned, s_back, s_xe = sem("gate"), sem("wgate"), sem("disp"), sem("turned"), sem("back"), sem("xe")
        s_xg, s_egu, s_esilu, s_eact = sem("xg"), sem("egu"), sem("esilu"), sem("eact")
        s_eturned, s_eback, s_edown, s_ye, s_comb, s_added = sem("eturned"), sem("eback"), sem("edown"), sem("ye"), sem("comb"), sem("added")
        widths = [min(P, FS - P * f) for f in range(NFS)]

        top_weights(nc, g, "r1", E1, TOP1, a["L1_wr"], combine[:], chosen[:])
        with nc.Block() as block:
            @block.sync
            def _(sp):
                for tile, name in ((before, "before"), (wse, "L1_wse"), (wsgu, "L1_wsgu"), (wsd, "L1_wsd")):
                    sp.dma_start(tile[:], a[name]).then_inc(s_w, 16)

                def load(e, i):
                    sp.dma_start(wgu[i][:], a["L1_wgu"][bass.ds(e, 1)].rearrange("e p g k f -> (e p) g k f")).then_inc(s_ew[i], 16)
                    sp.dma_start(wd[i][:], a["L1_wd"][bass.ds(e, 1)].rearrange("e p g k f -> (e p) g k f")).then_inc(s_ew[i], 16)

                for i in range(2):
                    load(i, i)
                with sp.Fori(0, NGRP // 2 - 1) as r:
                    for i in range(2):
                        sp.wait_ge(s_edown, 1 + 2 * r + i + 1)
                        load(2 * r + 2 + i, i)

            @block.gpsimd
            def _(pool):
                pool.iota(iota[:], [[1, CAP]], base=0, channel_multiplier=0, allow_small_or_imprecise_dtypes=True).then_inc(s_const, 1)
                pool.memset(ones[:], 1.0).then_inc(s_const, 1)
                pool.wait_ge(s_const, 1 + 2)
                pool.wait_ge(s_place, 1 + 1)
                for t in range(NT):
                    if t >= 2:
                        pool.wait_ge(s_turned, 1 + 2 * (t - 1))
                    out = wgate[:, t % 2, :].rearrange("p (e s) -> p e s", e=E1)
                    pool.wait_ge(s_gate, 1 + t + 1)
                    pool.tensor_tensor(out, gate[:, t % 2, :].rearrange("p (e s) -> p e s", e=E1),
                                       combine[:, t, :].unsqueeze(2).to_broadcast([P, E1, CAP]), ALU.mult).then_inc(s_wgate, 1)

            @block.tensor
            def _(pe):
                pe.wait_ge(s_const, 1 + 2)
                pe.wait_ge(s_w, 1 + 64)
                for t in range(NT):
                    for i in range(t + 1):
                        mm = pe.matmul(g.bank[0][:, E1 * t:E1 * t + E1], before[:] if i == t else ones[:], chosen[:, i, :],
                                       start=(i == 0), stop=(i == t))
                mm.then_inc(s_pos, 1)
                for t in range(NT):
                    for j in range(KC):
                        mm = pe.matmul(g.bank[7][:, t:t + 1], g.XT[:, j, P * t:P * t + P], wse[:, j, :], start=(j == 0), stop=(j == KC - 1))
                mm.then_inc(s_share, 1)

                def gate_up(n, f):
                    u = n * NFS + f
                    if u >= 2:
                        pe.wait_ge(s_sact, 1 + u - 1)
                    for part in range(2):
                        for j in range(KC):
                            mm = pe.matmul(g.bank[1 + 2 * (u % 2) + part][0:widths[f], :],
                                           wsgu[:, j, FS * part + P * f:FS * part + P * f + widths[f]],
                                           g.XT[:, j, HALF * n:HALF * n + HALF], start=(j == 0), stop=(j == KC - 1))
                        mm.then_inc(s_sgu, 1)

                def down(n):
                    pe.wait_ge(s_sact, 1 + (n + 1) * NFS)
                    for q in range(2):
                        d = 2 * n + q
                        if d >= 2:
                            pe.wait_ge(s_sadd, 1 + d - 1)
                        for t in range(2):
                            for f in range(NFS):
                                mm = pe.matmul(g.bank[5 + d % 2][:, C * t:C * t + C],
                                               act_[0:widths[f], n, f, P * (2 * q + t):P * (2 * q + t) + P],
                                               wsd[0:widths[f], f, :], start=(f == 0), stop=(f == NFS - 1))
                        mm.then_inc(s_sdown, 1)

                for n in range(2):
                    for f in range(NFS):
                        gate_up(n, f)
                        if f == 0 and n:
                            down(0)
                down(1)

                pe.wait_ge(s_share, 1 + 2)
                pe.wait_ge(s_place, 1 + 1)
                for t in range(NT):
                    pe.wait_ge(s_gate, 1 + t + 1)
                    for j in range(KC):
                        for n in range(2):
                            pe.matmul(g.bank[1 + 2 * j + n][:], X0[:, t, P * j:P * j + P], gate[:, t % 2, HALF * n:HALF * n + HALF],
                                      start=(t == 0), stop=(t == NT - 1)).then_inc(s_disp, 1)
                    pe.wait_ge(s_wgate, 1 + t + 1)
                    for n in range(2):
                        if t:
                            pe.wait_ge(s_back, 1 + 2 * t + n - 1)
                        for i in range(4):
                            mm = pe.transpose(g.bank[(0, 7)[n]][:, P * i:P * i + P],
                                              wgate[:, t % 2, P * (4 * n + i):P * (4 * n + i) + P], g.ident[:])
                        mm.then_inc(s_turned, 1)
                pe.wait_ge(s_xe, 1 + 4)

                with pe.Fori(0, NGRP // 2) as r:
                    def expert_down(i):
                        pe.wait_ge(s_eback, 1 + 2 * r + i + 1)
                        pe.wait_ge(s_ye, 1 + 2 * r)
                        for e in range(GRP):
                            for f in range(2):
                                mm = pe.matmul(g.bank[5 + i][CAP * e:CAP * e + CAP, 0:C], eactT[:, i, f, CAP * e:CAP * e + CAP],
                                               wd[i][:, e, f, :], start=(f == 0), stop=(f == 1), tile_position=(0, CAP * e))
                        mm.then_inc(s_edown, 1)

                    for i in range(2):
                        pe.wait_ge(s_ew[i], 1 + 32 * r + 32)
                        pe.wait_ge(s_xg, 1 + 2 * r + i + 1)
                        pe.wait_ge(s_eact, 1 + 2 * r)
                        for e in range(GRP):
                            for j in range(KC):
                                mm = pe.matmul(g.bank[1 + i][CAP * e:CAP * e + CAP, 0:2 * F1], xg[:, i, j, CAP * e:CAP * e + CAP],
                                               wgu[i][:, e, j, :], start=(j == 0), stop=(j == KC - 1), tile_position=(0, CAP * e))
                        mm.then_inc(s_egu, 1)
                    for i in range(2):
                        pe.wait_ge(s_eact, 1 + 2 * r + i + 1)
                        pe.wait_ge(s_eback, 1 + 2 * r)
                        for f in range(2):
                            mm = pe.transpose(g.bank[3 + i][0:FH, P * f:P * f + P], eact[:, i, FH * f:FH * f + FH], g.ident[:])
                        mm.then_inc(s_eturned, 1)
                    for i in range(2):
                        expert_down(i)

                pe.wait_ge(s_ye, 1 + NGRP)
                pe.wait_ge(s_back, 1 + 2 * NT)
                for t in range(NT):
                    if t >= 2:
                        pe.wait_ge(s_added, 1 + t - 1)
                    for n in range(NGRP):
                        mm = pe.matmul(g.bank[(0, 7)[t % 2]][:, 0:C], wgateT[:, n, P * t:P * t + P], ye[:, n, :],
                                       start=(n == 0), stop=(n == NGRP - 1))
                    mm.then_inc(s_comb, 1)

            @block.scalar
            def _(act):
                act.wait_ge(s_share, 1 + 1)
                act.activation(share[:], g.bank[7][:, 0:NT], ACT.Sigmoid).then_inc(s_share, 1)
                for u in range(2 * NFS):
                    w = widths[u % NFS]
                    act.wait_ge(s_sgu, 1 + 2 * u + 1)
                    if u >= 2:
                        act.wait_ge(s_sact, 1 + u - 1)
                    act.activation(silu[0:w, u % 2, :], g.bank[1 + 2 * (u % 2)][0:w, :], ACT.Silu).then_inc(s_ssilu, 1)
                for t in range(NT):
                    for n in range(2):
                        act.wait_ge(s_turned, 1 + 2 * t + n + 1)
                        act.copy(wgateT[:, 4 * n:4 * n + 4, P * t:P * t + P],
                                 g.bank[(0, 7)[n]][:].rearrange("p (i t) -> p i t", i=4)).then_inc(s_back, 1)
                with act.Fori(0, NGRP // 2) as r:
                    for i in range(2):
                        act.wait_ge(s_egu, 1 + 2 * r + i + 1)
                        act.wait_ge(s_eact, 1 + 2 * r)
                        act.activation(esilu[:, i, :], g.bank[1 + i][:, 0:F1], ACT.Silu).then_inc(s_esilu, 1)
                    for i in range(2):
                        act.wait_ge(s_edown, 1 + 2 * r + i + 1)
                        act.copy(ye[:, bass.ds(2 * r + i, 1), :], g.bank[5 + i][:, 0:C].unsqueeze(1)).then_inc(s_ye, 1)

            @block.vector
            def _(dve):
                own = Steps(dve, s_own)
                dve.wait_ge(s_pos, 1 + 1)
                own.then(dve.tensor_scalar(place[:], chosen[:], -1e4, 1e4, ALU.mult, ALU.add))
                own.wait()
                dve.tensor_tensor(place[:], place[:], g.bank[0][:, 0:NT * E1].rearrange("p (t e) -> p t e", t=NT),
                                  ALU.add).then_inc(s_place, 1)
                own.then(dve.tensor_copy(X0[:], g.X[:]))
                dve.wait_ge(s_share, 1 + 2)
                own.wait()

                def add(n):
                    for q in range(2):
                        d = 2 * n + q
                        dve.wait_ge(s_sdown, 1 + d + 1)
                        for t in range(2):
                            tt = 4 * n + 2 * q + t
                            ins = dve.scalar_tensor_tensor(out=g.X[:, tt, :], in0=g.bank[5 + d % 2][:, C * t:C * t + C],
                                                           scalar=share[:, tt:tt + 1], in1=g.X[:, tt, :], op0=ALU.mult, op1=ALU.add)
                        ins.then_inc(s_sadd, 1)

                for u in range(2 * NFS):
                    n, f = divmod(u, NFS)
                    dve.wait_ge(s_sgu, 1 + 2 * u + 2)
                    dve.wait_ge(s_ssilu, 1 + u + 1)
                    dve.tensor_tensor(act_[0:widths[f], n, f, :], g.bank[2 + 2 * (u % 2)][0:widths[f], :],
                                      silu[0:widths[f], u % 2, :], ALU.mult).then_inc(s_sact, 1)
                    if u == NFS:
                        add(0)
                add(1)
                dve.wait_ge(s_place, 1 + 1)
                dve.wait_ge(s_const, 1 + 2)
                for t in range(NT):
                    if t >= 2:
                        dve.wait_ge(s_disp, 1 + 4 * (t - 1))
                        dve.wait_ge(s_wgate, 1 + t - 1)
                    dve.tensor_tensor(gate[:, t % 2, :].rearrange("p (e s) -> p e s", e=E1),
                                      place[:, t, :].unsqueeze(2).to_broadcast([P, E1, CAP]),
                                      iota[:].unsqueeze(1).to_broadcast([P, E1, CAP]), ALU.is_equal).then_inc(s_gate, 1)
                for j in range(KC):
                    for n in range(2):
                        dve.wait_ge(s_disp, 1 + 4 * (NT - 1) + 2 * j + n + 1)
                        dve.tensor_copy(xeT[:, j, HALF * n:HALF * n + HALF], g.bank[1 + 2 * j + n][:]).then_inc(s_xe, 1)
                dve.wait_ge(s_xe, 1 + 4)
                with dve.Fori(0, NGRP // 2) as r:
                    for i in range(2):
                        dve.wait_ge(s_egu, 1 + 2 * r)
                        dve.tensor_copy(xg[:, i, :, :], xeT[:, :, bass.ds(r * (2 * P) + P * i, P)]).then_inc(s_xg, 1)
                    for i in range(2):
                        dve.wait_ge(s_esilu, 1 + 2 * r + i + 1)
                        dve.wait_ge(s_eturned, 1 + 2 * r)
                        dve.tensor_tensor(eact[:, i, :], g.bank[1 + i][:, F1:2 * F1], esilu[:, i, :], ALU.mult).then_inc(s_eact, 1)
                    for i in range(2):
                        dve.wait_ge(s_eturned, 1 + 2 * r + i + 1)
                        dve.wait_ge(s_edown, 1 + 2 * r)
                        dve.tensor_copy(eactT[:, i, :, :], g.bank[3 + i][0:FH, 0:2 * P].rearrange("p (f t) -> p f t", f=2)).then_inc(s_eback, 1)
                for t in range(NT):
                    dve.wait_ge(s_comb, 1 + t + 1)
                    dve.tensor_tensor(g.X[:, t, :], g.bank[(0, 7)[t % 2]][:, 0:C], g.X[:, t, :], ALU.add).then_inc(s_added, 1)


SEMS = 80


def program(nc, a, out, first=0, last=6):
    with ExitStack() as ctx:
        def sb(name, shape, dt=F32):
            return ctx.enter_context(nc.sbuf_tensor(name, shape, dt))

        g = Shared(sb, lambda name, shape, dt: ctx.enter_context(nc.psum_tensor(name, shape, dt)),
                   lambda name: ctx.enter_context(nc.semaphore(name)))
        order = [("ident", g.ident), ("x", g.X), ("xT", g.XT), ("ctxT", g.ctxT)]
        s_load = g.sem("load")
        pool_of_sems = [g.sem(f"shared{n}") for n in range(SEMS)]
        with nc.Block() as block:
            @block.gpsimd
            def _(pool):
                for sem in pool_of_sems:
                    pool.sem_inc(sem, 1)

            @block.sync
            def _(sp):
                for n, (name, tile) in enumerate(order):
                    sp.dma_start(tile[:], a[name]).then_inc(s_load, 16)

            @block.vector
            def _(dve):
                dve.memset(g.eps_ln[:], LN_EPS)
                dve.memset(g.eps6[:], 1e-6)
                dve.wait_ge(s_load, 16 * len(order))
        subs = [
            lambda: attention(nc, g, "a0", True, a, "L0"),
            lambda: context_softmax(nc, g, a),
            lambda: experts0(nc, g, a),
            lambda: deltanet(nc, g, a),
            lambda: attention(nc, g, "a1", False, a, "L1"),
            lambda: experts1(nc, g, a),
        ]
        for n in range(first, last):
            used = []
            g.sem = lambda name: (used.append(pool_of_sems[len(used)]), used[-1])[1]
            subs[n]()
            layernorm(nc, g, n - first, used if n < last - 1 else [], out if n == last - 1 else None)


def arrays_of(i):
    import numpy as np

    def tiled(w):
        return np.ascontiguousarray(w.reshape(-1, P, w.shape[-1]).transpose(1, 0, 2))

    def rotated(wT):
        h = wT.reshape(-1, NH, 2, HD // 2)
        return h[:, :, ::-1, :].reshape(wT.shape)

    f = np.float32
    x = np.asarray(i["x"])
    a = {"x": tiled(x.reshape(NTOK, C)), "xT": tiled(x.reshape(NTOK, C).T), "ident": np.eye(P, dtype=f)}
    a["ctxT"] = np.ascontiguousarray(np.asarray(i["ctx_512"]).reshape(NTOK, CTX).T)
    wq, wk, wv, wo = (np.asarray(i["L0_attn_w_" + n]).T for n in "qkvo")
    a["L0_wq"], a["L0_wk"] = (tiled(np.concatenate([w, rotated(w)], axis=1)) for w in (wq, wk))
    a["L0_wv"], a["L0_wo"] = tiled(wv), tiled(wo)
    inv = (f(1.0) / f(10000.0) ** (np.arange(0, HD, 2, dtype=f) / f(HD))).astype(f)
    freq = np.outer(np.arange(T, dtype=f), inv).astype(f)
    cos, sin = np.cos(freq).T.astype(f), np.sin(freq).T.astype(f)
    rows = [np.tile(np.tile(np.concatenate(x), (P // HD, 1)), (1, 2)) for x in ([cos, cos], [-sin, sin])]
    a["rope"] = np.ascontiguousarray(np.stack(rows, axis=1))
    spread = np.zeros((P, 4, 4, P), f)
    for part, groups in enumerate(((0, 1), (2, 3), (0, 2), (1, 3))):
        for j in range(4):
            for e in range(2):
                for r in groups:
                    for d in range(HD):
                        spread[HD * (2 * j + e) + d, part, j, 64 * e + HD * r + d] = 1.0
    a["spread"] = spread
    qi, ki = np.arange(P)[:, None], np.arange(P)[None, :]
    zero = np.zeros((P, P), f)
    a["L0_mask"] = np.concatenate([zero, np.where(ki // 64 <= qi // 64, 0, MASKED).astype(f)], axis=1)
    a["L1_mask"] = np.concatenate([zero, np.where(ki <= qi, 0, MASKED).astype(f)], axis=1)
    a["L1_wq"] = tiled(np.asarray(i["L1_xattn_Wq"]).T)
    kv = np.asarray(i["L1_xattn_Wkv_expand"]).T
    a["L1_wk"] = np.ascontiguousarray(kv[:, :C])[:, None, :]
    a["L1_wv"] = np.ascontiguousarray(kv[:, C:])[:, None, :]
    a["L1_wo"] = tiled(np.asarray(i["L1_xattn_Wout"]).T)
    a["L0_Wk"] = np.ascontiguousarray(np.asarray(i["L0_xattn_W_k"]).T)
    a["L0_bk"], a["L0_gamma"], a["L0_beta"] = (np.asarray(i["L0_xattn_" + n]) for n in ("b_k", "ln_gamma", "ln_beta"))
    a["L0_gate"] = tiled(np.asarray(i["L0_ffn_gate_w"]))

    def experts(w, shared):
        w = np.concatenate([np.asarray(w), np.asarray(shared)[None]])
        return np.ascontiguousarray(w.reshape(w.shape[0], -1, P, w.shape[2]).transpose(0, 2, 1, 3))

    a["L0_wgu"] = experts(i["L0_ffn_w_gate_up"], i["L0_ffn_shared_gate_up"])
    a["L0_wd"] = experts(i["L0_ffn_w_down"], i["L0_ffn_shared_down"])
    a["L1_wr"] = tiled(np.asarray(i["L1_ffn_Wr"]))
    a["L1_wse"] = tiled(np.asarray(i["L1_ffn_Wse"]))
    a["L1_wsgu"] = tiled(np.concatenate([np.asarray(i["L1_ffn_Wsg"]), np.asarray(i["L1_ffn_Wsu"])], axis=1))
    wsd = np.asarray(i["L1_ffn_Wsd"])
    a["L1_wsd"] = tiled(np.concatenate([wsd, np.zeros((NFS * P - FS, C), f)]))
    gu = np.concatenate([np.asarray(i["L1_ffn_Wg"]), np.asarray(i["L1_ffn_Wu"])], axis=2)
    a["L1_wgu"] = np.ascontiguousarray(gu.reshape(NGRP, GRP, KC, P, 2 * F1).transpose(0, 3, 1, 2, 4))
    a["L1_wd"] = np.ascontiguousarray(np.asarray(i["L1_ffn_Wd"]).reshape(NGRP, GRP, 2, F1 // 2, C).transpose(0, 3, 1, 2, 4))
    pw = np.asarray(i["L1_attn_in_proj_w"]).T
    n = NCT * P
    a["L1_w"], a["L1_wz"], a["L1_wba"] = tiled(pw[:, :n]), tiled(pw[:, n:n + VD]), tiled(pw[:, n + VD:])
    a["L1_taps"] = tiled(np.asarray(i["L1_attn_conv_w"]))
    a["L1_dt"], a["L1_alog"], a["L1_nw"] = (np.asarray(i["L1_attn_" + n]) for n in ("dt_bias", "A_log", "norm_weight"))
    a["L1_wo2"] = tiled(np.asarray(i["L1_attn_out_proj_w"]).T)
    a["ones2"] = (np.arange(P)[:, None] // DK == np.arange(P)[None, :] // DK).astype(f)
    a["halves"] = (np.arange(P)[:, None] // DK == np.arange(2)[None, :]).astype(f)
    r, c = np.arange(P)[:, None], np.arange(P)[None, :]
    a["upto"], a["after"] = (r <= c).astype(f), (r > c).astype(f)
    fill = [(r // (2 * s) == c // (2 * s)) & (r % (2 * s) >= s) & (c % (2 * s) < s) for s in [1] + LEVELS]
    a["first"] = np.ascontiguousarray(fill[0].T).astype(f)
    a["lvl"] = np.stack(fill[1:], axis=1).astype(f)
    a["before"] = (np.arange(P)[:, None] < np.arange(P)[None, :]).astype(f)
    return a


def kernel(**inputs):
    import numpy as _np
    import concourse.bacc as _bacc
    from concourse import mybir as _mybir
    from concourse.bass_utils import run_bass_kernel_spmd as _run

    nc = _bacc.Bacc("TRN2", target_bir_lowering=False, num_devices=1)
    arrays = arrays_of(inputs)
    aps = {n: nc.dram_tensor(f"in_{n}", a.shape, _mybir.dt.from_np(a.dtype), kind="ExternalInput").ap()
           for n, a in arrays.items()}
    out = nc.dram_tensor("out", (P, NT, C), F32, kind="ExternalOutput").ap()
    program(nc, aps, out)
    r = _run(nc, [{f"in_{n}": a for n, a in arrays.items()}], core_ids=[0])
    return r.results[0]["out"].transpose(1, 0, 2).reshape(B, T, C)
```

```python
from contextlib import ExitStack

import concourse.bass as bass
from concourse import mybir

F32 = mybir.dt.float32
F16 = mybir.dt.float16
U32 = mybir.dt.uint32

ALU = mybir.AluOpType
ACT = mybir.ActivationFunctionType
AX = mybir.AxisListType

P = 128
B, T, C = 4, 256, 256
NT = B * T // P
TPB = T // P
KC = C // P
NTOK = B * T
CTX = 64
LN_EPS = 1e-5

NH, HD = 16, 16
MASKED = -1e30




class Steps:

    def __init__(self, eng, sem, turn=0, per=0):
        self.eng, self.sem, self.turn, self.per, self.n = eng, sem, turn, per, 0

    def then(self, ins):
        ins.then_inc(self.sem, 1)
        self.n += 1
        return self.n

    def wait(self, n=None):
        self.eng.wait_ge(self.sem, 1 + self.turn * self.per + (self.n if n is None else n))

    def end(self):
        assert self.n == self.per, (self.n, self.per)


class LayernormSems:
    def __init__(self, sem):
        self.stats, self.mv, self.sd, self.rstd = (sem("ln_" + n) for n in ("stats", "mv", "sd", "rstd"))
        self.normed, self.turned, self.kept, self.out = (sem("ln_" + n) for n in ("normed", "turned", "kept", "out"))


class Shared:

    def __init__(self, sb, pb, sem):
        self.sem = sem
        self.bank = [pb(f"bank{i}", [P, 512], F32) for i in range(8)]
        self.X, self.XT, self.ctxT = sb("X", [P, NT, C]), sb("XT", [P, KC, NTOK]), sb("ctxT", [CTX, NTOK])
        self.ident, self.tick = sb("ident", [P, P]), sb("tick", [1, 64])
        self.eps_ln, self.eps6 = sb("eps_ln", [P, 1]), sb("eps6", [P, 1])
        self.ln_sems = LayernormSems(sem)


def layernorm(nc, g, call, spent, out=None):
    with ExitStack() as ctx:
        def sb(n, shape, dt=F32):
            return ctx.enter_context(nc.sbuf_tensor(f"ln{call}_{n}", shape, dt))

        stats = sb("stats", [P, NT, 6])
        mv = sb("mv", [P, NT, 2])
        sd = sb("sd", [P, NT])
        rstd = sb("rstd", [P, NT])
        s = g.ln_sems
        each, one, banks = call * NT, call, call * 2 * (NT // 4)

        with nc.Block() as block:
            @block.vector
            def _(dve):
                for t in range(NT):
                    dve.bn_stats(stats[:, t, :], g.X[:, t, :]).then_inc(s.stats, 1)
                for t in range(NT):
                    dve.wait_ge(s.stats, each + t + 1)
                    dve.bn_aggr(mv[:, t, :], stats[:, t, :]).then_inc(s.mv, 1)
                dve.wait_ge(s.sd, one + 1)
                dve.reciprocal(rstd[:], sd[:]).then_inc(s.rstd, 1)
                dve.wait_ge(s.rstd, one + 1)
                for t in range(NT):
                    dve.tensor_scalar(g.X[:, t, :], g.X[:, t, :], mv[:, t, 0:1], rstd[:, t:t + 1],
                                      ALU.subtract, ALU.mult).then_inc(s.normed, 1)
                if out is None:
                    for n in range(NT // 4):
                        dve.wait_ge(s.turned, banks + KC * n + 2)
                        dve.tensor_copy(g.XT[:, 1, 512 * n:512 * n + 512],
                                        g.bank[KC * n + 1][:]).then_inc(s.kept, 1)

            @block.scalar
            def _(act):
                act.wait_ge(s.mv, each + NT)
                act.activation(sd[:], mv[:, :, 1], ACT.Sqrt, bias=g.eps_ln[:, 0:1]).then_inc(s.sd, 1)
                if out is None:
                    for n in range(NT // 4):
                        act.wait_ge(s.turned, banks + KC * n + 1)
                        act.copy(g.XT[:, 0, 512 * n:512 * n + 512], g.bank[KC * n][:]).then_inc(s.kept, 1)

            @block.gpsimd
            def _(pool):
                for sem in spent:
                    pool.sem_clear(sem)
                for sem in spent:
                    pool.sem_inc(sem, 1)

            if out is None:
                @block.tensor
                def _(pe):
                    for n in range(NT // 4):
                        pe.wait_ge(s.normed, each + 4 * n + 4)
                        for k in range(KC):
                            for i in range(4):
                                last = pe.transpose(g.bank[KC * n + k][:, P * i:P * i + P],
                                                    g.X[:, 4 * n + i, P * k:P * k + P], g.ident[:])
                            last.then_inc(s.turned, 1)
            else:
                @block.sync
                def _(sp):
                    for n in range(NT // 4):
                        sp.wait_ge(s.normed, each + 4 * n + 4)
                        sp.dma_start(out[:, 4 * n:4 * n + 4, :], g.X[:, 4 * n:4 * n + 4, :]).then_inc(s.out, 16)
                    sp.wait_ge(s.out, 16 * (NT // 4))


def attention(nc, g, name, rope, a, layer):
    KIN = KC if rope else 1
    NV = 2 if rope else 1
    WID = 3 * P
    HALF = 512
    NU = 2 * 2 * (NTOK // HALF)
    NPT = NH // 2
    SC, TB = 3, 3
    with ExitStack() as ctx:
        def sb(n, shape, dt=F32):
            return ctx.enter_context(nc.sbuf_tensor(f"{name}_{n}", shape, dt))

        def sem(n):
            return g.sem(f"{name}_{n}")

        wq, wo, mask = sb("wq", [P, KC, NV * C]), sb("wo", [P, KC, C]), sb("mask", [P, T])
        wk = sb("wk", [P if rope else CTX, KIN, NV * C])
        wv = sb("wv", [P if rope else CTX, KIN, C])
        spread32, spread = sb("spread32", [P, 4, 4, P]), sb("spread", [P, 4, 4, P], F16)
        loads = [(wq, layer + "_wq"), (wk, layer + "_wk"), (spread32, "spread"), (wv, layer + "_wv"),
                 (mask, layer + "_mask"), (wo, layer + "_wo")]
        if rope:
            table = sb("table", [P, 2, HALF])
            loads[1:1] = [(table, "rope")]
        src = g.XT if rope else g.ctxT[:].unsqueeze(1)
        parts = sb("parts", [P, 2, 2, HALF])
        whole = sb("whole", [P, 2, HALF])
        high, low = sb("high", [P, 2, HALF], F16), sb("low", [P, 2, HALF], F16)
        packs = sb("packs", [P, B, 2, NPT, T], F16)
        pack = sb("pack", [P, 2, NPT, T], F16)
        vhl = sb("vhl", [P, NT, NH, 2 * HD], F16)
        vnow = sb("vnow", [P, TPB, NH * 2 * HD], F16)
        negs = sb("negs", [P, 3, WID])
        negmax, sums, rsum = sb("negmax", [P, TPB, NH]), sb("sums", [P, TPB, NH]), sb("rsum", [P, TPB, NH])
        probs = sb("probs", [P, 3, WID])
        highT, lowT = sb("highT", [P, 3, WID], F16), sb("lowT", [P, 3, WID], F16)
        ctxs, ctxn = sb("ctxs", [P, TPB, NH, HD]), sb("ctxn", [P, NT, C])
        ctxT = sb("ctxT", [P, KC, NTOK])
        s_w, s_spread, s_proj, s_parts, s_whole = sem("w"), sem("spread"), sem("proj"), sem("parts"), sem("whole")
        s_high, s_low, s_rep, s_repA, s_repD = sem("high"), sem("low"), sem("rep"), sem("repA"), sem("repD")
        s_v, s_vhigh, s_vlow, s_pack = sem("v"), sem("vhigh"), sem("vlow"), sem("pack")
        s_scores, s_masked, s_exp, s_turned = sem("scores"), sem("masked"), sem("exp"), sem("turned")
        s_hiT, s_loT, s_pv, s_sum, s_rsum, s_norm = sem("hiT"), sem("loT"), sem("pv"), sem("sum"), sem("rsum"), sem("norm")
        s_fin, s_finkept, s_out, s_added = sem("fin"), sem("finkept"), sem("out"), sem("added")
        units = [(n, i, m) for n in range(NTOK // HALF) for i in range(2) for m in range(2)]

        with nc.Block() as block:
            @block.sync
            def _(sp):
                for tile, n in loads:
                    sp.dma_start(tile[:], a[n]).then_inc(s_w, 16)
                sp.wait_ge(s_repA, 1 + 2 * NU)
                sp.wait_ge(s_repD, 1 + 2 * NU)
                sp.wait_ge(s_vlow, 1 + NT)
                with sp.Fori(0, B) as b:
                    sp.wait_ge(s_scores, 1 + b * NH)
                    sp.dma_start(pack[:], packs[:, bass.ds(b, 1)].rearrange("p b i n t -> p (b i) n t")).then_inc(s_pack, 16)
                    sp.wait_ge(s_pv, 1 + b * NH)
                    sp.dma_start(vnow[:], vhl[:, bass.ts(b, TPB)].rearrange("p t h d -> p t (h d)")).then_inc(s_pack, 16)

            @block.tensor
            def _(pe):
                pe.wait_ge(s_w, 1 + 16 * len(loads))

                def project(u):
                    n, i, m = units[u]
                    w, x, kin = ((wq, g.XT, KC), (wk, src, KIN))[i]
                    if u >= 2:
                        pe.wait_ge(s_parts if rope else s_low, 1 + (NV if rope else 1) * (u - 1))
                    for r in range(NV):
                        for j in range(kin):
                            mm = pe.matmul(g.bank[2 * (u % 2) + r][:], w[:, j, C * r + P * m:C * r + P * m + P],
                                           x[:, j, HALF * n:HALF * n + HALF], start=(j == 0), stop=(j == kin - 1))
                        mm.then_inc(s_proj, 1)

                def replicate(u):
                    n, i, m = units[u]
                    pe.wait_ge(s_low, 1 + u + 1)
                    for j in range(4):
                        pe.wait_ge((s_repA, s_repD)[j % 2], 1 + 2 * u + j // 2)
                        pe.matmul(g.bank[4 + j % 2][:], spread[:, 2 * i, j, :], high[:, u % 2, :], start=True, stop=False)
                        pe.matmul(g.bank[4 + j % 2][:], spread[:, 2 * i + 1, j, :], low[:, u % 2, :],
                                  start=False, stop=True).then_inc(s_rep, 1)

                for u in range(NU):
                    project(u)
                    if u == 0:
                        pe.wait_ge(s_spread, 1 + 1)
                    if u >= 1:
                        replicate(u - 1)
                replicate(NU - 1)
                for t in range(NT):
                    if t >= 2:
                        pe.wait_ge(s_vlow, 1 + t - 1)
                    for j in range(KIN):
                        mm = pe.matmul(g.bank[6 + t % 2][:, 0:C], src[:, j, P * t:P * t + P], wv[:, j, :],
                                       start=(j == 0), stop=(j == KIN - 1))
                    mm.then_inc(s_v, 1)
                pe.wait_ge(s_vlow, 1 + NT)
                pe.wait_ge(s_repA, 1 + 2 * NU)
                pe.wait_ge(s_repD, 1 + 2 * NU)

                def heads(b):
                    def scores(h):
                        p, m = 64 * (h % 2), h // 2
                        if h == 0:
                            pe.wait_ge(s_pack, 1 + 32 * b + 32)
                        pe.wait_ge(s_masked, 1 + b * NH + max(h - SC + 1, 0))
                        qp, kp = pack[p:p + 64, 0, m, :], pack[p:p + 64, 1, m, :]
                        pe.matmul(g.bank[h % SC][:, 0:P], qp[:, 0:P], kp[:, 0:P], start=True, stop=True)
                        pe.matmul(g.bank[h % SC][:, P:WID], qp[:, P:T], kp, start=True, stop=True).then_inc(s_scores, 1)

                    def transposes(h):
                        pe.wait_ge(s_exp, 1 + b * NH + h + 1)
                        pe.wait_ge(s_loT, 1 + b * NH + max(h - TB + 1, 0))
                        for i in range(3):
                            mm = pe.transpose(g.bank[SC + h % TB][:, P * i:P * i + P], probs[:, h % 3, P * i:P * i + P], g.ident[:])
                        mm.then_inc(s_turned, 1)

                    def values(h):
                        pe.wait_ge(s_loT, 1 + b * NH + h + 1)
                        if h == 0:
                            pe.wait_ge(s_sum, 1 + TPB * b)
                        cols = slice(2 * HD * h, 2 * HD * h + 2 * HD)
                        for t, blocks in enumerate((((0, 0),), ((1, 0), (2, 1)))):
                            prods = [(part, i, j) for i, j in blocks for part in (highT, lowT)]
                            for n, (part, i, j) in enumerate(prods):
                                mm = pe.matmul(g.bank[6 + t][:, cols], part[:, h % 3, P * i:P * i + P], vnow[:, j, cols],
                                               start=(n == 0), stop=(n == len(prods) - 1))
                        mm.then_inc(s_pv, 1)

                    for i in range(NH + 4):
                        if i < NH:
                            scores(i)
                        if 2 <= i < NH + 2:
                            transposes(i - 2)
                        if i >= 4:
                            values(i - 4)

                with pe.Fori(0, B) as b:
                    heads(b)
                for n in range(NTOK // HALF):
                    pe.wait_ge(s_norm, 1 + 2 * (n + 1))
                    for j in range(KC):
                        for t in range(4):
                            mm = pe.transpose(g.bank[2 * n + j][:, P * t:P * t + P], ctxn[:, 4 * n + t, P * j:P * j + P], g.ident[:])
                        mm.then_inc(s_fin, 1)
                for t in range(NT):
                    pe.wait_ge(s_finkept, 1 + KC * (t // 4 + 1))
                    if t >= 2:
                        pe.wait_ge(s_added, 1 + t - 1)
                    for j in range(KC):
                        mm = pe.matmul(g.bank[4 + t % 2][:, 0:C], ctxT[:, j, P * t:P * t + P], wo[:, j, :],
                                       start=(j == 0), stop=(j == KC - 1))
                    mm.then_inc(s_out, 1)

            @block.scalar
            def _(act):
                act.wait_ge(s_w, 1 + 16 * len(loads))
                act.copy(spread[:], spread32[:]).then_inc(s_spread, 1)

                def high_part(u):
                    if u >= 2:
                        act.wait_ge(s_rep, 1 + 4 * (u - 1))
                    if rope:
                        act.wait_ge(s_whole, 1 + u + 1)
                        act.copy(high[:, u % 2, :], whole[:, u % 2, :]).then_inc(s_high, 1)
                    else:
                        act.wait_ge(s_proj, 1 + u + 1)
                        act.copy(high[:, u % 2, :], g.bank[2 * (u % 2)][:]).then_inc(s_high, 1)

                def take(u):
                    n, i, m = units[u]
                    for j in (0, 2):
                        act.wait_ge(s_rep, 1 + 4 * u + j + 1)
                        act.copy(packs[:, 2 * n:2 * n + 2, i, 4 * m + j, :],
                                 g.bank[4][:].rearrange("p (b t) -> p b t", b=2)).then_inc(s_repA, 1)

                for u in range(NU + 1):
                    if u < NU:
                        high_part(u)
                    if u >= 1:
                        take(u - 1)
                for t in range(NT):
                    act.wait_ge(s_v, 1 + t + 1)
                    act.copy(vhl[:, t, :, 0:HD], g.bank[6 + t % 2][:, 0:C].rearrange("p (h d) -> p h d", h=NH)).then_inc(s_vhigh, 1)

                with act.Fori(0, B) as b:
                    for h in range(NH + 2):
                        if h < NH:
                            act.wait_ge(s_masked, 1 + b * NH + h + 1)
                            act.wait_ge(s_turned, 1 + b * NH + max(h - 2, 0))
                            act.activation(probs[:, h % 3, 0:P], negs[:, h % 3, 0:P], ACT.Exp, bias=negmax[:, 0, h:h + 1],
                                           scale=-1.0, accum_out=sums[:, 0, h:h + 1])
                            act.activation(probs[:, h % 3, P:WID], negs[:, h % 3, P:WID], ACT.Exp, bias=negmax[:, 1, h:h + 1],
                                           scale=-1.0, accum_out=sums[:, 1, h:h + 1]).then_inc(s_exp, 1)
                        if h >= 2:
                            act.wait_ge(s_turned, 1 + b * NH + h - 1)
                            act.wait_ge(s_pv, 1 + b * NH + max(h - 4, 0))
                            act.copy(highT[:, (h - 2) % 3, :], g.bank[SC + (h - 2) % TB][:, 0:WID]).then_inc(s_hiT, 1)
                for n in range(NTOK // HALF):
                    act.wait_ge(s_fin, 1 + KC * n + 1)
                    act.copy(ctxT[:, 0, HALF * n:HALF * n + HALF], g.bank[2 * n][:]).then_inc(s_finkept, 1)
                    act.wait_ge(s_fin, 1 + KC * n + 2)
                    act.copy(ctxT[:, 1, HALF * n:HALF * n + HALF], g.bank[2 * n + 1][:]).then_inc(s_finkept, 1)

            if rope:
                @block.gpsimd
                def _(pool):
                    for u in range(NU):
                        pool.wait_ge(s_parts, 1 + 2 * u + 2)
                        if u >= 2:
                            pool.wait_ge(s_low, 1 + u - 1)
                        pool.tensor_tensor(whole[:, u % 2, :], parts[:, u % 2, 0, :], parts[:, u % 2, 1, :],
                                           ALU.add).then_inc(s_whole, 1)

            @block.vector
            def _(dve):
                dve.wait_ge(s_w, 1 + 16 * len(loads))

                def rotate(u):
                    for r in range(2):
                        dve.wait_ge(s_proj, 1 + 2 * u + r + 1)
                        if u >= 2:
                            dve.wait_ge(s_whole, 1 + u - 1)
                        dve.tensor_tensor(parts[:, u % 2, r, :], g.bank[2 * (u % 2) + r][:], table[:, r, :],
                                          ALU.mult).then_inc(s_parts, 1)

                def low_part(u):
                    dve.wait_ge(s_high, 1 + u + 1)
                    dve.tensor_tensor(low[:, u % 2, :], whole[:, u % 2, :] if rope else g.bank[2 * (u % 2)][:],
                                      high[:, u % 2, :], ALU.subtract).then_inc(s_low, 1)

                def take(u):
                    n, i, m = units[u]
                    for j in (1, 3):
                        dve.wait_ge(s_rep, 1 + 4 * u + j + 1)
                        dve.tensor_copy(packs[:, 2 * n:2 * n + 2, i, 4 * m + j, :],
                                        g.bank[5][:].rearrange("p (b t) -> p b t", b=2)).then_inc(s_repD, 1)

                for u in range(NU + 1):
                    if rope and u < NU:
                        rotate(u)
                    if not rope and u < NU:
                        low_part(u)
                    if u >= 1:
                        if rope:
                            low_part(u - 1)
                        take(u - 1)
                for t in range(NT):
                    dve.wait_ge(s_vhigh, 1 + t + 1)
                    dve.tensor_tensor(vhl[:, t, :, HD:2 * HD], g.bank[6 + t % 2][:, 0:C].rearrange("p (h d) -> p h d", h=NH),
                                      vhl[:, t, :, 0:HD], ALU.subtract).then_inc(s_vlow, 1)

                with dve.Fori(0, B) as b:
                    def mask_head(h):
                        dve.wait_ge(s_scores, 1 + b * NH + h + 1)
                        dve.wait_ge(s_exp, 1 + b * NH + max(h - 2, 0))
                        dve.memset(g.tick[:, h:h + 1], 0.0)
                        dve.tensor_tensor_reduce(negs[:, h % 3, 0:P], g.bank[h % SC][:, 0:P], mask[:, P:2 * P],
                                                 -0.25, 3e38, ALU.add, ALU.min, negmax[:, 0, h:h + 1])
                        dve.tensor_tensor_reduce(negs[:, h % 3, P:WID], g.bank[h % SC][:, P:WID], mask[:],
                                                 -0.25, 3e38, ALU.add, ALU.min, negmax[:, 1, h:h + 1]).then_inc(s_masked, 1)

                    def low_turned(h):
                        dve.wait_ge(s_hiT, 1 + b * NH + h + 1)
                        dve.tensor_tensor(lowT[:, h % 3, :], g.bank[SC + h % TB][:, 0:WID], highT[:, h % 3, :],
                                          ALU.subtract).then_inc(s_loT, 1)

                    for i in range(NH + 3):
                        if i < NH:
                            mask_head(i)
                        if i >= 3:
                            low_turned(i - 3)
                    dve.wait_ge(s_exp, 1 + b * NH + NH)
                    dve.reciprocal(rsum[:], sums[:]).then_inc(s_rsum, 1)
                    dve.wait_ge(s_pv, 1 + b * NH + NH)
                    for t in range(TPB):
                        dve.tensor_reduce(ctxs[:, t], g.bank[6 + t][:].rearrange("p (h i d) -> p h d i", h=NH, i=2),
                                          AX.X, ALU.add).then_inc(s_sum, 1)
                    dve.wait_ge(s_rsum, 1 + b + 1)
                    dve.wait_ge(s_sum, 1 + TPB * (b + 1))
                    dve.tensor_tensor(ctxn[:, bass.ts(b, TPB)].rearrange("p t (h d) -> p t h d", h=NH), ctxs[:],
                                      rsum[:].unsqueeze(3).to_broadcast([P, TPB, NH, HD]), ALU.mult).then_inc(s_norm, 1)
                for t in range(NT):
                    dve.wait_ge(s_out, 1 + t + 1)
                    dve.tensor_tensor(g.X[:, t, :], g.bank[4 + t % 2][:, 0:C], g.X[:, t, :], ALU.add).then_inc(s_added, 1)


def context_softmax(nc, g, a):
    HALF = 512
    with ExitStack() as ctx:
        def sb(n, shape, dt=F32):
            return ctx.enter_context(nc.sbuf_tensor(f"c0_{n}", shape, dt))

        def sem(n):
            return g.sem(f"c0_{n}")

        wk = sb("wk", [CTX, CTX])
        bcol, brow = sb("bcol", [CTX, 1]), sb("brow", [P, CTX])
        gamma, beta = sb("gamma", [P, T]), sb("beta", [P, T])
        kvT, kv, outT = sb("kvT", [CTX, NTOK]), sb("kv", [P, NT, CTX]), sb("outT", [CTX, NTOK])
        stats, mv = sb("stats", [P, NT, 6]), sb("mv", [P, NT, 2])
        sd, rstd = sb("sd", [P, NT]), sb("rstd", [P, NT])
        sim = sb("sim", [P, NT, T])
        negmax, sums, rsum = sb("negmax", [P, NT]), sb("sums", [P, NT]), sb("rsum", [P, NT])
        s_load, s_kv, s_kvkept, s_kvT, s_kvTkept = sem("load"), sem("kv"), sem("kvkept"), sem("kvT"), sem("kvTkept")
        s_outT, s_outTkept, s_sim, s_var, s_sd = sem("outT"), sem("outTkept"), sem("sim"), sem("var"), sem("sd")
        s_max, s_exp, s_own = sem("max"), sem("exp"), sem("own")

        def sim_bank(n):
            return g.bank[4 + n // 2][:, T * (n % 2):T * (n % 2) + T]

        with nc.Block() as block:
            @block.sync
            def _(sp):
                sp.dma_start(wk[:], a["L0_Wk"]).then_inc(s_load, 16)
                sp.dma_start(bcol[:], a["L0_bk"].rearrange("(p a) -> p a", a=1)).then_inc(s_load, 16)
                sp.dma_start(brow[:], a["L0_bk"].partition_broadcast(P)).then_inc(s_load, 16)
                sp.dma_start(gamma[:], a["L0_gamma"].partition_broadcast(P)).then_inc(s_load, 16)
                sp.dma_start(beta[:], a["L0_beta"].partition_broadcast(P)).then_inc(s_load, 16)

            @block.tensor
            def _(pe):
                pe.wait_ge(s_load, 1 + 80)
                for n in range(NT):
                    mm = pe.matmul(g.bank[2][:, CTX * n:CTX * n + CTX], g.ctxT[:, P * n:P * n + P], wk[:], start=True, stop=True)
                mm.then_inc(s_kv, 1)
                for h in range(NTOK // HALF):
                    pe.matmul(g.bank[h][0:CTX, :], wk[:], g.ctxT[:, HALF * h:HALF * h + HALF], start=True, stop=True).then_inc(s_kvT, 1)
                pe.wait_ge(s_kvkept, 1 + 1)
                for b in range(B):
                    for t in range(TPB):
                        mm = pe.matmul(g.bank[2 + b // 2][0:CTX, T * (b % 2):T * (b % 2) + T], kv[:, TPB * b + t, :],
                                       g.XT[:, t, T * b:T * b + T], start=(t == 0), stop=(t == TPB - 1))
                    if b % 2:
                        mm.then_inc(s_outT, 1)
                pe.wait_ge(s_kvTkept, 1 + 2)
                for n in range(NT):
                    if n % 4 == 0:
                        pe.wait_ge(s_outTkept, 1 + n // 4 + 1)
                    b = n // TPB
                    mm = pe.matmul(sim_bank(n), outT[:, P * n:P * n + P], kvT[:, T * b:T * b + T], start=True, stop=True)
                    if n % 2:
                        mm.then_inc(s_sim, 1)

            @block.scalar
            def _(act):
                act.wait_ge(s_load, 1 + 80)
                for h in range(NTOK // HALF):
                    act.wait_ge(s_kvT, 1 + h + 1)
                    act.activation(kvT[:, HALF * h:HALF * h + HALF], g.bank[h][0:CTX, :], ACT.Identity,
                                   bias=bcol[:, 0:1]).then_inc(s_kvTkept, 1)
                act.wait_ge(s_var, 1 + NT)
                act.activation(sd[:], mv[:, :, 1], ACT.Sqrt, bias=g.eps6[:, 0:1], scale=1.0 / 256).then_inc(s_sd, 1)
                for n in range(NT):
                    act.wait_ge(s_max, 1 + n + 1)
                    act.activation(sim[:, n, :], sim[:, n, :], ACT.Exp, bias=negmax[:, n:n + 1],
                                   accum_out=sums[:, n:n + 1]).then_inc(s_exp, 1)

            @block.vector
            def _(dve):
                own = Steps(dve, s_own)
                dve.wait_ge(s_load, 1 + 80)
                dve.wait_ge(s_kv, 1 + 1)
                dve.tensor_tensor(kv[:], g.bank[2][:].rearrange("p (t d) -> p t d", t=NT),
                                  brow[:].unsqueeze(1).to_broadcast([P, NT, CTX]), ALU.add).then_inc(s_kvkept, 1)
                for h in range(2):
                    dve.wait_ge(s_outT, 1 + h + 1)
                    dve.tensor_copy(outT[:, HALF * h:HALF * h + HALF], g.bank[2 + h][0:CTX, :]).then_inc(s_outTkept, 1)
                for n in range(NT):
                    if n % 2 == 0:
                        dve.wait_ge(s_sim, 1 + n // 2 + 1)
                    own.then(dve.bn_stats(stats[:, n, :], sim_bank(n)))
                first = own.n
                for n in range(NT):
                    own.wait(first - NT + n + 1)
                    dve.bn_aggr(mv[:, n, :], stats[:, n, :]).then_inc(s_var, 1)
                dve.wait_ge(s_var, 1 + NT)
                for n in range(NT):
                    own.then(dve.scalar_tensor_tensor(out=sim[:, n, :], in0=sim_bank(n), scalar=mv[:, n, 0:1], in1=gamma[:],
                                                      op0=ALU.subtract, op1=ALU.mult))
                dve.wait_ge(s_sd, 1 + 1)
                own.then(dve.reciprocal(rstd[:], sd[:]))
                own.wait()
                own.then(dve.tensor_scalar(rstd[:], rstd[:], 1.0 / 16, None, ALU.mult))
                own.wait()
                for n in range(NT):
                    own.then(dve.scalar_tensor_tensor(out=sim[:, n, :], in0=sim[:, n, :], scalar=rstd[:, n:n + 1], in1=beta[:],
                                                      op0=ALU.mult, op1=ALU.add))
                    if n:
                        own.wait(own.n - 1)
                        dve.tensor_reduce(negmax[:, n - 1:n], sim[:, n - 1, :], AX.X, ALU.max, negate=True).then_inc(s_max, 1)
                own.wait()
                dve.tensor_reduce(negmax[:, NT - 1:NT], sim[:, NT - 1, :], AX.X, ALU.max, negate=True).then_inc(s_max, 1)
                for n in range(NT):
                    dve.wait_ge(s_exp, 1 + n + 1)
                    own.then(dve.reciprocal(rsum[:, n:n + 1], sums[:, n:n + 1]))
                    own.wait()
                    dve.scalar_tensor_tensor(out=g.X[:, n, :], in0=sim[:, n, :], scalar=rsum[:, n:n + 1], in1=g.X[:, n, :],
                                             op0=ALU.mult, op1=ALU.add)


def top_weights(nc, g, name, E, TOP, wr_dram, combine, chosen=None, ahead=None, split=None):
    with ExitStack() as ctx:
        def sb(n, shape, dt=F32):
            return ctx.enter_context(nc.sbuf_tensor(f"{name}_{n}", shape, dt))

        def sem(n):
            return g.sem(f"{name}_{n}")

        wr = sb("wr", [P, KC, E])
        iota = sb("iota", [P, E])
        probs = sb("probs", [P, NT, E])
        peak, sums, rsum = sb("peak", [P, NT]), sb("sums", [P, NT]), sb("rsum", [P, NT])
        top = sb("top", [P, NT, 8])
        place = sb("place", [P, NT, 8], U32)
        placef = sb("placef", [P, NT, 8])
        hot = sb("hot", [P, NT, E])
        s_load, s_logits, s_shift, s_exp, s_own = sem("load"), sem("logits"), sem("shift"), sem("exp"), sem("own")

        with nc.Block() as block:
            @block.sync
            def _(sp):
                sp.dma_start(wr[:], wr_dram).then_inc(s_load, 16)
                ahead(sp)

            @block.gpsimd
            def _(pool):
                pool.iota(iota[:], [[1, E]], base=0, channel_multiplier=0, allow_small_or_imprecise_dtypes=True).then_inc(s_load, 1)

            @block.tensor
            def _(pe):
                pe.wait_ge(s_load, 1 + 17)
                for t in range(NT):
                    for j in range(KC):
                        mm = pe.matmul(g.bank[0][:, E * t:E * t + E], g.XT[:, j, P * t:P * t + P], wr[:, j, :],
                                       start=(j == 0), stop=(j == KC - 1))
                mm.then_inc(s_logits, 1)

            @block.scalar
            def _(act):
                act.wait_ge(s_shift, 1 + 1)
                act.activation(probs[:], probs[:], ACT.Exp).then_inc(s_exp, 1)
                if split is not None:
                    split(act)

            @block.vector
            def _(dve):
                own = Steps(dve, s_own)

                def step(ins):
                    own.then(ins)
                    own.wait()

                def wide(x):
                    return x.unsqueeze(2).to_broadcast([P, NT, E])

                logits = g.bank[0][:, 0:NT * E].rearrange("p (t e) -> p t e", t=NT)
                dve.wait_ge(s_logits, 1 + 1)
                step(dve.tensor_reduce(peak[:], logits, AX.X, ALU.max))
                dve.tensor_tensor(probs[:], logits, wide(peak[:]), ALU.subtract).then_inc(s_shift, 1)
                dve.wait_ge(s_exp, 1 + 1)
                step(dve.tensor_reduce(sums[:], probs[:], AX.X, ALU.add))
                step(dve.reciprocal(rsum[:], sums[:]))
                step(dve.tensor_tensor(probs[:], probs[:], wide(rsum[:]), ALU.mult))
                for t in range(NT):
                    own.then(dve.max(top[:, t, :], probs[:, t, :]))
                own.wait()
                for t in range(NT):
                    own.then(dve.max_index(place[:, t, :], top[:, t, :], probs[:, t, :]))
                own.wait()
                step(dve.tensor_copy(placef[:], place[:]))
                step(dve.tensor_reduce(sums[:], top[:, :, 0:TOP], AX.X, ALU.add))
                step(dve.reciprocal(rsum[:], sums[:]))
                step(dve.tensor_tensor(top[:], top[:], rsum[:].unsqueeze(2).to_broadcast([P, NT, 8]), ALU.mult))
                for k in range(TOP):
                    to = combine if k == 0 else hot[:]
                    step(dve.tensor_tensor(to, iota[:].unsqueeze(1).to_broadcast([P, NT, E]),
                                           wide(placef[:, :, k]), ALU.is_equal))
                    if chosen is not None:
                        step(dve.tensor_copy(chosen, to) if k == 0 else dve.tensor_tensor(chosen, chosen, to, ALU.add))
                    step(dve.tensor_tensor(to, to, wide(top[:, :, k]), ALU.mult))
                    if k:
                        step(dve.tensor_tensor(combine, combine, to, ALU.add))


E0, I0 = 8, 512


def experts0(nc, g, a):
    NE, NB, HALF = E0 + 1, 3, 512
    NF = I0 // P
    WSCALE, ASCALE = 256.0, 16.0
    with ExitStack() as ctx:
        def sb(n, shape, dt=F32):
            return ctx.enter_context(nc.sbuf_tensor(f"e0_{n}", shape, dt))

        def sem(n):
            return g.sem(f"e0_{n}")

        def parts(n, shape):
            return [sb(f"{n}{x}", shape, F16) for x in "HL"]

        combine = sb("combine", [P, NT, E0])
        cw = sb("cw", [P, NT, NE])
        wgu = [sb(f"wgu{i}", [P, KC, 2 * I0]) for i in range(NB)]
        wd = [sb(f"wd{i}", [P, NF, C]) for i in range(NB)]
        wguP = [parts(f"wguP{i}", [P, KC, 2 * I0]) for i in range(NB)]
        wdP = [parts(f"wdP{i}", [P, NF, C]) for i in range(NB)]
        xP = parts("xP", [P, KC, NTOK])
        silu = sb("silu", [P, 2, HALF])
        full = sb("full", [P, 2, HALF])
        actP = parts("actP", [P, 2, NF, HALF])
        s_cw, s_load, s_xhi, s_xlo = sem("cw"), [sem(f"load{i}") for i in range(NB)], sem("xhi"), sem("xlo")
        s_whi, s_wlo, s_ahi, s_alo = sem("whi"), sem("wlo"), sem("ahi"), sem("alo")
        s_gu, s_silu, s_act, s_down, s_added = sem("gu"), sem("silu"), sem("act"), sem("down"), sem("added")
        GU, DN = 2 * NF, NT // 2
        UNITS = NB * GU
        PRODUCTS = ((0, 0), (0, 1), (1, 0))

        def load(sp, e, i):
            sp.dma_start(wgu[i][:], a["L0_wgu"][bass.ds(e, 1)].rearrange("e p k f -> (e p) k f")).then_inc(s_load[i], 16)
            sp.dma_start(wd[i][:], a["L0_wd"][bass.ds(e, 1)].rearrange("e p k f -> (e p) k f")).then_inc(s_load[i], 16)

        def first_loads(sp):
            for i in range(NB):
                load(sp, i, i)

        def high_parts(act, r, i):
            act.wait_ge(s_load[i], 1 + 32 * r + 32)
            act.activation(wguP[i][0][:], wgu[i][:], ACT.Copy, scale=WSCALE)
            act.activation(wdP[i][0][:], wd[i][:], ACT.Copy, scale=WSCALE).then_inc(s_whi, 1)

        def first_highs(act):
            act.copy(xP[0][:], g.XT[:]).then_inc(s_xhi, 1)
            high_parts(act, 0, 0)

        def turns(eng, body):
            with eng.Fori(0, NE // NB - 1) as r:
                body(r, False)
            body(NE // NB - 1, True)

        top_weights(nc, g, "r0", E0, 2, a["L0_gate"], combine[:], ahead=first_loads,
                    split=first_highs)
        with nc.Block() as block:
            @block.sync
            def _(sp):
                with sp.Fori(0, NE // NB - 1) as r:
                    for i in range(NB):
                        sp.wait_ge(s_wlo, 1 + r * NB + i + 1)
                        load(sp, (r + 1) * NB + i, i)

            @block.tensor
            def _(pe):
                pe.wait_ge(s_xlo, 1 + 1)

                def body(r, last):
                    gu0, dn0 = r * UNITS, r * (NB * DN)

                    def gate_up(i, n, f):
                        u = (i * 2 + n) * NF + f
                        pe.wait_ge(s_act, 1 + gu0 + max(u - 1, 0))
                        for part in range(2):
                            terms = [(j, wp, xp) for j in range(KC) for wp, xp in PRODUCTS]
                            for k, (j, wp, xp) in enumerate(terms):
                                mm = pe.matmul(g.bank[2 * (u % 2) + part][:], wguP[i][wp][:, j, I0 * part + P * f:I0 * part + P * f + P],
                                               xP[xp][:, j, HALF * n:HALF * n + HALF], start=(k == 0), stop=(k == len(terms) - 1))
                            mm.then_inc(s_gu, 1)

                    def down(i, n):
                        pe.wait_ge(s_alo, 1 + gu0 + (i * 2 + n + 1) * NF)
                        for q in range(2):
                            d = (i * 2 + n) * 2 + q
                            pe.wait_ge(s_added, 1 + dn0 + max(d - 1, 0))
                            for t in range(2):
                                terms = [(f, ap, wp) for f in range(NF) for ap, wp in PRODUCTS]
                                for k, (f, ap, wp) in enumerate(terms):
                                    mm = pe.matmul(g.bank[4 + d % 2][:, C * t:C * t + C],
                                                   actP[ap][:, n, f, P * (2 * q + t):P * (2 * q + t) + P], wdP[i][wp][:, f, :],
                                                   start=(k == 0), stop=(k == len(terms) - 1))
                            mm.then_inc(s_down, 1)

                    for i in range(NB):
                        pe.wait_ge(s_wlo, 1 + r * NB + i + 1)
                        for n in range(2):
                            for f in range(NF):
                                gate_up(i, n, f)
                                if f == 1 and (i or n):
                                    down(i if n else i - 1, 1 - n)
                    down(NB - 1, 1)

                turns(pe, body)

            @block.scalar
            def _(act):
                def body(r, last):
                    gu0 = r * UNITS

                    def high(u):
                        k, f = divmod(u, NF)
                        act.wait_ge(s_act, 1 + gu0 + u + 1)
                        act.wait_ge(s_down, 1 + r * (NB * DN) + max(k * 2 - 2, 0))
                        act.copy(actP[0][:, k % 2, f, :], full[:, u % 2, :]).then_inc(s_ahi, 1)

                    for u in range(UNITS):
                        act.wait_ge(s_gu, 1 + 2 * gu0 + 2 * u + 1)
                        act.wait_ge(s_act, 1 + gu0 + max(u - 1, 0))
                        act.activation(silu[:, u % 2, :], g.bank[2 * (u % 2)][:], ACT.Silu, scale=1.0 / WSCALE).then_inc(s_silu, 1)
                        if u:
                            high(u - 1)
                        i, v = divmod(u, GU)
                        if v == 3 and not (last and i == NB - 1):
                            high_parts(act, r + (i + 1) // NB, (i + 1) % NB)
                    high(UNITS - 1)

                turns(act, body)

            @block.vector
            def _(dve):
                dve.tensor_scalar(cw[:, :, 0:E0], combine[:], 1.0 / (WSCALE * ASCALE), None, ALU.mult).then_inc(s_cw, 1)
                dve.memset(cw[:, :, E0:NE], 1.0 / (WSCALE * ASCALE)).then_inc(s_cw, 1)

                def split(r, i):
                    dve.wait_ge(s_whi, 1 + r * NB + i + 1)
                    dve.scalar_tensor_tensor(out=wguP[i][1][:], in0=wgu[i][:], scalar=WSCALE, in1=wguP[i][0][:],
                                             op0=ALU.mult, op1=ALU.subtract)
                    dve.scalar_tensor_tensor(out=wdP[i][1][:], in0=wd[i][:], scalar=WSCALE, in1=wdP[i][0][:],
                                             op0=ALU.mult, op1=ALU.subtract).then_inc(s_wlo, 1)

                dve.wait_ge(s_xhi, 1 + 1)
                dve.tensor_tensor(xP[1][:], g.XT[:], xP[0][:], ALU.subtract).then_inc(s_xlo, 1)
                split(0, 0)
                dve.wait_ge(s_cw, 1 + 2)

                def body(r, last):
                    gu0, dn0 = r * UNITS, r * (NB * DN)

                    def low(u):
                        k, f = divmod(u, NF)
                        dve.wait_ge(s_ahi, 1 + gu0 + u + 1)
                        dve.tensor_tensor(actP[1][:, k % 2, f, :], full[:, u % 2, :], actP[0][:, k % 2, f, :],
                                          ALU.subtract).then_inc(s_alo, 1)

                    def add(i, n):
                        for q in range(2):
                            d = (i * 2 + n) * 2 + q
                            dve.wait_ge(s_down, 1 + dn0 + d + 1)
                            for t in range(2):
                                tt = 4 * n + 2 * q + t
                                ins = dve.scalar_tensor_tensor(
                                    out=g.X[:, tt, :], in0=g.bank[4 + d % 2][:, C * t:C * t + C],
                                    scalar=cw[:, tt, bass.ds(r * NB + i, 1)], in1=g.X[:, tt, :], op0=ALU.mult, op1=ALU.add)
                            ins.then_inc(s_added, 1)

                    for u in range(UNITS):
                        i, v = divmod(u, GU)
                        n, f = divmod(v, NF)
                        dve.wait_ge(s_gu, 1 + 2 * gu0 + 2 * u + 2)
                        dve.wait_ge(s_silu, 1 + gu0 + u + 1)
                        dve.wait_ge(s_alo, 1 + gu0 + max(u - 1, 0))
                        dve.scalar_tensor_tensor(out=full[:, u % 2, :], in0=g.bank[2 * (u % 2) + 1][:], scalar=ASCALE / WSCALE,
                                                 in1=silu[:, u % 2, :], op0=ALU.mult, op1=ALU.mult).then_inc(s_act, 1)
                        if u:
                            low(u - 1)
                        if f == 1 and (i or n):
                            add(i if n else i - 1, 1 - n)
                        if v == 3 and not (last and i == NB - 1):
                            split(r + (i + 1) // NB, (i + 1) % NB)
                    low(UNITS - 1)
                    add(NB - 1, 1)

                turns(dve, body)


NKH, NVH, DK, DV, TAPS = 8, 16, 64, 128, 4
REP = NVH // NKH
NQT = NKH * DK // P
NVT = NVH * DV // P
NCT = 2 * NQT + NVT
VD = NVH * DV
HG = 4
NG = NVH // HG
LEVELS = [2, 4, 8, 16, 32, 64]


def deltanet(nc, g, a):
    NP2 = NCT // 2
    with ExitStack() as ctx:
        def sb(n, shape, dt=F32):
            return ctx.enter_context(nc.sbuf_tensor(f"dn_{n}", shape, dt))

        def sem(n):
            return g.sem(f"dn_{n}")

        w = sb("w", [P, KC, NCT * P])
        wz = sb("wz", [P, KC, VD])
        wba = sb("wba", [P, KC, 2 * NVH])
        wo = sb("wo", [P, NVT, C])
        taps = sb("taps", [P, NCT, TAPS])
        dt_bias, a_exp = sb("dt_bias", [P, NVH]), sb("a_exp", [P, NVH])
        norm_w = sb("norm_w", [P, 1])
        halves = sb("halves", [P, 2])
        before, upto, after = sb("before", [P, P]), sb("upto", [P, P]), sb("after", [P, P])
        lvl = sb("lvl", [P, len(LEVELS), P])
        ident16, minus16 = sb("ident16", [P, P], F16), sb("minus16", [P, P], F16)
        ident4 = sb("ident4", [P, HG, P], F16)
        first = sb("first", [P, P])
        xb = sb("xb", [P, KC, T])
        cT = sb("cT", [P, NCT, T])
        gT = cT[:, 2 * NQT:, :]
        sq = sb("sq", [P, 2 * NQT, T])
        osq = sq[:].rearrange("p (r m) t -> p r (m t)", r=2)
        ktok = sb("ktok", [P, TPB, NKH * DK])
        vtok = sb("vtok", [P, TPB, VD])
        zs = sb("zs", [P, TPB, VD])
        pre = sb("pre", [P, TPB, 2 * NVH])
        relu, gg = sb("relu", [P, TPB, NVH]), sb("gg", [P, TPB, NVH])
        beta = sb("beta", [P, TPB, NVH])
        nrm, rn = sb("nrm", [P, TPB, 2 * NKH]), sb("rn", [P, TPB, 2 * NKH])
        decay = sb("decay", [P, TPB, 2, NVH])
        nbk, bks = sb("nbk", [P, TPB, NVH]), sb("bks", [P, TPB, NVH])
        rqs, ngam, grq = sb("rqs", [P, TPB, NVH]), sb("ngam", [P, TPB, NVH]), sb("grq", [P, TPB, NVH])
        state = sb("state", [P, NG, REP * DV])
        oss, osd, orstd = sb("oss", [P, TPB, NVH]), sb("osd", [P, TPB, NVH]), sb("orstd", [P, TPB, NVH])
        mg = [sb(f"mg{s}", [P, HG, P]) for s in range(2)]
        nt = [sb(f"nt{s}", [P, HG, P]) for s in range(2)]
        gmt = [[sb(f"gmt{s}{r}", [P, HG, P])[:] for r in range(2)] for s in range(2)]
        gmt[0].append(xb[:].rearrange("p k (i t) -> p (k i) t", t=P))
        gmt[1].append(ktok[:, 1, :].rearrange("p (h i) -> p h i", h=HG))
        ntH = [[sb(f"ntH{s}{r}", [P, HG, P], F16) for r in range(2)] for s in range(2)]
        ntL = [[sb(f"ntL{s}{r}", [P, HG, P], F16) for r in range(2)] for s in range(2)]
        tri = [[sb(f"tri{s}{r}", [P, HG, P], F16) for r in range(2)] for s in range(2)]
        triT = [[sb(f"triT{s}{r}", [P, HG, P], F16) for r in range(2)] for s in range(2)]
        xm = [sb(f"xm{s}", [P, HG, P], F16) for s in range(2)]
        fine = [sb(f"fine{s}", [P, HG, P]) for s in range(2)]
        upd = [sb(f"upd{s}", [P, HG, P]) for s in range(2)]
        aux = [sb(f"aux{s}", [P, HG, P]) for s in range(2)]

        s_w, s_wz, s_wr, s_aexp, s_in = sem("w"), sem("wz"), sem("wr"), sem("aexp"), sem("in")
        s_ba, s_z, s_zkept = sem("ba"), sem("z"), sem("zkept")
        s_pair, s_tap0, s_tap, s_conv, s_silu = sem("pair"), sem("tap0"), sem("tap"), sem("conv"), sem("silu")
        s_sq, s_ss, s_turned, s_backA, s_backD = sem("sq"), sem("ss"), sem("turned"), sem("backA"), sem("backD")
        s_own, s_pre, s_eb, s_l1, s_gg, s_ssk, s_nrm = sem("own"), sem("pre"), sem("eb"), sem("l1"), sem("gg"), sem("ssk"), sem("nrm")
        s_cum, s_decay = sem("cum"), sem("decay")
        s_mg, s_dt, s_exp, s_gm, s_gmown, s_gmu, s_kkq, s_nt = (sem(x) for x in ("mg", "dt", "exp", "gm", "gmown", "gmu", "kkq", "nt"))
        s_tinit, s_t0, s_t0kept = sem("tinit"), sem("t0"), sem("t0kept")
        s_nth = sem("nth")
        s_x, s_xkept, s_p, s_pkept, s_pt, s_ptkept = (sem(x) for x in ("x", "xkept", "p", "pkept", "pt", "ptkept"))
        s_ks, s_r, s_w_, s_u, s_o, s_okept, s_s, s_skept = (sem(x) for x in ("ks", "r", "w_", "u", "o", "okept", "s", "skept"))
        s_osq, s_oss, s_osd, s_rstd, s_on, s_og, s_og1 = (sem(x) for x in ("osq", "oss", "osd", "rstd", "on", "og", "og1"))
        s_gturned, s_gbackA, s_gbackD, s_out, s_added = sem("gturned"), sem("gbackA"), sem("gbackD"), sem("out"), sem("added")

        U = 2 * NG
        NL = len(LEVELS)
        NS = NL + 1
        W = U // 2
        NZ = TPB * VD // 512
        TURNS = [("k", 0, "D"), ("k", 1, "D"), (0, 0, "A"), (0, 1, "A"), ("back", 0, "A"), ("back", 1, "A"),
                 (1, 0, "A"), (1, 1, "D"), (2, 0, "A"), (2, 1, "D"), (3, 0, "A"), (3, 1, "D")]
        GTURNS = [(m, 0, "A") for m in range(4)] + [(m, 1, "AD"[m % 2]) for m in range(4)]

        def bank(s, i):
            return g.bank[4 * s + i]

        def four(b_):
            return b_[:].rearrange("p (h i) -> p h i", h=HG)

        NA = [e for _, _, e in TURNS].count("A")

        def emptied(eng, turns, sems, b, n):
            by = [e for _, _, e in turns]
            eng.wait_ge(sems["AD".index(by[n])], 1 + b * by.count(by[n]) + by[:n + 1].count(by[n]))

        def pair_of(w_):
            return [(s, 2 * w_ + s, (2 * w_ + s) % NG) for s in range(2)]

        def at(w_, l, s):
            return (w_ * NS + l) * 2 + s

        def atp(w_, l, s):
            return (w_ * NL + l) * 2 + s

        def first_loads(a):
            return [(wba, a["L1_wba"]), (taps, a["L1_taps"]), (dt_bias, a["L1_dt"].partition_broadcast(P)),
                    (a_exp, a["L1_alog"].partition_broadcast(P)), (upto, a["upto"]), (after, a["after"]), (w, a["L1_w"])]

        N1, N2, N3 = 16 * 7, 16 * 3, 16 * 4

        with nc.Block() as block:
            @block.sync
            def _(sp):
                for sem_, loads in ((s_w, first_loads(a)), (s_wz, [(wz, a["L1_wz"]), (halves, a["halves"]), (before, a["before"])]),
                                    (s_wr, [(first, a["first"]), (lvl, a["lvl"]), (norm_w, a["L1_nw"]), (wo, a["L1_wo2"])])):
                    for tile, src in loads:
                        sp.dma_start(tile[:], src).then_inc(sem_, 16)

            @block.tensor
            def _(pe):
                pe.wait_ge(s_w, 1 + N1)
                with pe.Fori(0, B) as b:
                    pe.wait_ge(s_added, 1 + b * TPB)
                    pe.wait_ge(s_in, 1 + b + 1)
                    for t in range(TPB):
                        for j in range(KC):
                            mm = pe.matmul(g.bank[7][:, 2 * NVH * t:2 * NVH * (t + 1)], xb[:, j, P * t:P * t + P], wba[:, j, :],
                                           start=(j == 0), stop=(j == KC - 1))
                    mm.then_inc(s_ba, 1)

                    def decays(w_):
                        for s, u, hg in pair_of(w_):
                            pe.wait_ge(s_mg, 1 + b * U + u + 1)
                            for h in range(HG):
                                mm = pe.matmul(bank(s, 2)[:, P * h:P * h + P], mg[s][:, h, :], upto[:], start=True, stop=True)
                            mm.then_inc(s_dt, 1)

                    def turn(n):
                        what, t, _ = TURNS[n]
                        if n >= 2:
                            emptied(pe, TURNS, (s_backA, s_backD), b, n - 2)
                        if what == "back":
                            emptied(pe, TURNS, (s_backA, s_backD), b, t)
                        elif n % 2 == 0:
                            pe.wait_ge(s_silu, 1 + b * NP2 + (NQT if what == "k" else NQT + 2 * what + 2))
                        for i in range(4):
                            if what == "back":
                                src = ktok[:, t, P * i:P * i + P]
                            else:
                                src = cT[:, (NQT if what == "k" else 2 * NQT + 4 * what) + i, P * t:P * t + P]
                            mm = pe.transpose(g.bank[4 + n % 2][:, P * i:P * i + P], src, g.ident[:])
                        mm.then_inc(s_turned, 1)

                    for p in range(NP2):
                        pe.wait_ge(s_conv, 1 + b * NP2 + max(p - 1, 0))
                        for i in range(2):
                            for j in range(KC):
                                mm = pe.matmul(g.bank[p % 2][:, T * i:T * i + T], w[:, j, P * (2 * p + i):P * (2 * p + i) + P],
                                               xb[:, j, :], start=(j == 0), stop=(j == KC - 1))
                        mm.then_inc(s_pair, 1)
                        if p == 0:
                            pe.wait_ge(s_gg, 1 + b + 1)
                            for c in range(TPB):
                                for i, mask in enumerate((upto, after)):
                                    o = NVH * (2 * c + i)
                                    mm = pe.matmul(g.bank[7][:, o:o + NVH], mask[:], gg[:, c, :], start=True, stop=True)
                            mm.then_inc(s_cum, 1)
                        if p == 2:
                            decays(0)
                        if p >= NP2 - NZ:
                            if p == NP2 - NZ:
                                pe.wait_ge(s_exp, 1 + b * U + 2)
                            n = p - (NP2 - NZ)
                            t, m = divmod(n, VD // 512)
                            pe.wait_ge(s_wz, 1 + N2)
                            pe.wait_ge(s_zkept, 1 + b * NZ + max(n - 1, 0))
                            for j in range(KC):
                                mm = pe.matmul(g.bank[6 + n % 2][:], xb[:, j, P * t:P * t + P], wz[:, j, 512 * m:512 * m + 512],
                                               start=(j == 0), stop=(j == KC - 1))
                            mm.then_inc(s_z, 1)
                        if p == 7:
                            pe.wait_ge(s_sq, 1 + b + 1)
                            for t in range(TPB):
                                for m in range(2 * NQT):
                                    mm = pe.matmul(g.bank[2][:, 2 * NKH * t + 2 * m:2 * NKH * t + 2 * m + 2], sq[:, m, P * t:P * t + P],
                                                   halves[:], start=True, stop=True)
                            mm.then_inc(s_ss, 1)
                        if p >= 8:
                            turn(2 * (p - 8))
                            turn(2 * (p - 8) + 1)

                    def products(w_):
                        for s, u, hg in pair_of(w_):
                            pe.wait_ge(s_exp, 1 + b * U + u + 1)
                            c = w_ // 2
                            for k in range(2):
                                q0 = DK * k
                                for i, m in enumerate((hg, NQT + hg)):
                                    mm = pe.matmul(bank(s, 2 + k)[:, P * i:P * i + P],
                                                   cT[q0:q0 + DK, NQT + hg, P * c:P * c + P], cT[q0:q0 + DK, m, P * c:P * c + P],
                                                   start=True, stop=True)
                            mm.then_inc(s_kkq, 1)

                    def turns(w_):
                        for s, u, hg in pair_of(w_):
                            pe.wait_ge(s_tinit, 1 + b * U + u + 1)
                            for h in range(HG):
                                mm = pe.matmul(bank(s, 2)[:, P * h:P * h + P], triT[s][w_ % 2][:, h, :], ident16[:], start=True, stop=True)
                            mm.then_inc(s_t0, 1)

                    def states(w_):
                        for s, u, hg in pair_of(w_):
                            pe.wait_ge(s_ptkept, 1 + b * U * NS + at(w_, NL, s) + 1)
                            pe.wait_ge(s_skept, 1 + b * NG + hg + 1)
                            for k in range(2):
                                q0 = DK * k
                                pe.matmul(bank(s, 2 + k)[:, 0:2 * P], cT[q0:q0 + DK, NQT + hg, P:2 * P],
                                          state[q0:q0 + DK, hg, :], start=True, stop=True)
                                mm = pe.matmul(bank(s, 2 + k)[:, 2 * P:4 * P], cT[q0:q0 + DK, hg, P:2 * P],
                                               state[q0:q0 + DK, hg, :], start=True, stop=True)
                            mm.then_inc(s_ks, 1)

                    def solutions(w_, which=(0, 1)):
                        for s, u, hg in (pair_of(w_)[n] for n in which):
                            pe.wait_ge(s_ptkept, 1 + b * U * NS + at(w_, NL, s) + 1)
                            if w_ >= W // 2:
                                pe.wait_ge(s_r, 1 + b * NG + hg + 1)
                            for h in range(HG):
                                v = vtok[:, 0, P * (HG * hg + h):P * (HG * hg + h) + P] if w_ < W // 2 else upd[s][:, h, :]
                                mm = pe.matmul(bank(s, 2)[:, P * h:P * h + P], fine[s][:, h, :], v, start=True, stop=True)
                            mm.then_inc(s_w_, 1)

                    def outputs(w_, which=(0, 1)):
                        for s, u, hg in (pair_of(w_)[n] for n in which):
                            pe.wait_ge(s_u, 1 + b * U + u + 1)
                            for h in range(HG):
                                mm = pe.matmul(bank(s, 3)[:, P * h:P * h + P], gmt[s][w_ % 3][:, h, :], upd[s][:, h, :], start=True, stop=True)
                            mm.then_inc(s_o, 1)
                            if w_ < W // 2:
                                for k in range(2):
                                    q0 = DK * k
                                    mm = pe.matmul(bank(s, 2)[q0:q0 + DK, 0:2 * P], ktok[:, 0, P * hg + q0:P * hg + q0 + DK],
                                                   aux[s][:, 2 * k:2 * k + 2, :], start=True, stop=True)
                                mm.then_inc(s_s, 1)

                    def after_x(w_, l):
                        late = 1 if w_ > W // 2 else 0
                        if w_ and l == 1:
                            pe.wait_ge(s_exp, 1 + b * U + min(2 * w_ + 4, U))
                            if late:
                                states(w_ - 1)
                        if w_ and l == 1 + late:
                            solutions(w_ - 1, (0,))
                        if w_ and l == 2 + late:
                            outputs(w_ - 1, (0,))
                        if l == 4 and w_ < W - 1:
                            pe.wait_ge(s_okept, 1 + b * U + 2 * w_)
                            pe.wait_ge(s_skept, 1 + b * NG + min(2 * w_, NG))
                            products(w_ + 1)

                    def after_p(w_, l):
                        late = 1 if w_ > W // 2 else 0
                        if w_ and l == 1 + late:
                            solutions(w_ - 1, (1,))
                        if w_ and l == 2 + late:
                            outputs(w_ - 1, (1,))

                    def gturn(n):
                        m, t, _ = GTURNS[n]
                        if n == 0:
                            pe.wait_ge(s_og, 1 + b + 1)
                        if n >= 2:
                            emptied(pe, GTURNS, (s_gbackA, s_gbackD), b, n - 2)
                        if t == 1:
                            pe.wait_ge(s_og1, 1 + b * 4 + m + 1)
                        for i in range(4):
                            mm = pe.transpose(g.bank[n % 2][:, P * i:P * i + P], vtok[:, t, P * (4 * m + i):P * (4 * m + i) + P], g.ident[:])
                        mm.then_inc(s_gturned, 1)

                    def project(t):
                        for n in (4 * t + 2, 4 * t + 3):
                            emptied(pe, GTURNS, (s_gbackA, s_gbackD), b, n)
                        for k in range(NVT):
                            mm = pe.matmul(g.bank[4 + t][:, 0:C], gT[:, k, P * t:P * t + P], wo[:, k, :], start=(k == 0), stop=(k == NVT - 1))
                        mm.then_inc(s_out, 1)

                    pe.wait_ge(s_backA, 1 + b * NA + 4)
                    pe.wait_ge(s_zkept, 1 + b * NZ + NZ)
                    products(0)
                    for n in range(8, len(TURNS)):
                        turn(n)
                    turns(0)
                    for n in (len(TURNS) - 2, len(TURNS) - 1):
                        emptied(pe, TURNS, (s_backA, s_backD), b, n)
                    pe.wait_ge(s_wr, 1 + N3)
                    for w_ in range(W):
                        r = w_ % 2
                        pair = pair_of(w_)
                        for l in range(NL):
                            for s, u, hg in pair:
                                if l == 0:
                                    pe.wait_ge(s_t0kept, 1 + b * U + u + 1)
                                    pe.wait_ge(s_nth, 1 + b * U + u + 1)
                                else:
                                    pe.wait_ge(s_pkept, 1 + b * U * NL + atp(w_, l - 1, s) + 1)
                                pe.matmul(bank(s, 0)[:], ident16[:], ident4[:], start=True, stop=False)
                                for h in range(HG):
                                    mm = pe.matmul(bank(s, 0)[:, P * h:P * h + P], ntH[s][r][:, h, :], tri[s][r][:, h, :],
                                                   start=False, stop=(h == HG - 1))
                                mm.then_inc(s_x, 1)
                            if l == 0 and w_ < W - 1:
                                decays(w_ + 1)
                            after_x(w_, l)
                            for s, u, hg in pair:
                                if l == 0:
                                    if w_:
                                        pe.wait_ge(s_ptkept, 1 + b * U * NS + at(w_ - 1, NL, s) + 1)
                                else:
                                    pe.wait_ge(s_ptkept, 1 + b * U * NS + at(w_, l - 1, s) + 1)
                                pe.wait_ge(s_xkept, 1 + b * U * NS + at(w_, l, s) + 1)
                                for h in range(HG):
                                    mm = pe.matmul(bank(s, 0)[:, P * h:P * h + P], triT[s][r][:, h, :], xm[s][:, h, :], start=True, stop=True)
                                mm.then_inc(s_p, 1)
                                for h in range(HG):
                                    mm = pe.matmul(bank(s, 1)[:, P * h:P * h + P], xm[s][:, h, :], triT[s][r][:, h, :], start=True, stop=True)
                                mm.then_inc(s_pt, 1)
                            after_p(w_, l)
                        for s, u, hg in pair:
                            pe.wait_ge(s_ptkept, 1 + b * U * NS + at(w_, NL - 1, s) + 1)
                            pe.wait_ge(s_gm, 1 + b * U + u + 1)
                            for h in range(HG):
                                o = bank(s, 0)[:, P * h:P * h + P]
                                pe.matmul(o, triT[s][r][:, h, :], minus16[:], start=True, stop=False)
                                pe.matmul(o, ident16[:], ident16[:], start=False, stop=False)
                                pe.matmul(o, ntH[s][r][:, h, :], tri[s][r][:, h, :], start=False, stop=False)
                                mm = pe.matmul(o, ntL[s][r][:, h, :], tri[s][r][:, h, :], start=False, stop=True)
                            mm.then_inc(s_x, 1)
                        if w_ < W - 1:
                            turns(w_ + 1)
                        for s, u, hg in pair:
                            pe.wait_ge(s_xkept, 1 + b * U * NS + at(w_, NL, s) + 1)
                            for h in range(HG):
                                o = bank(s, 1)[:, P * h:P * h + P]
                                pe.matmul(o, ident16[:], triT[s][r][:, h, :], start=True, stop=False)
                                mm = pe.matmul(o, xm[s][:, h, :], triT[s][r][:, h, :], start=False, stop=True)
                            mm.then_inc(s_pt, 1)
                    states(W - 1)
                    gturn(0)
                    gturn(1)
                    solutions(W - 1)
                    gturn(2)
                    gturn(3)
                    outputs(W - 1)
                    project(0)
                    for n in range(4, 8):
                        gturn(n)
                    project(1)

            @block.scalar
            def _(act):
                act.wait_ge(s_w, 1 + N1)
                act.activation(a_exp[:], a_exp[:], ACT.Exp).then_inc(s_aexp, 1)
                with act.Fori(0, B) as b:
                    act.wait_ge(s_pre, 1 + b + 1)
                    act.activation(pre[:], pre[:], ACT.Exp, scale=-1.0).then_inc(s_eb, 1)
                    act.wait_ge(s_eb, 1 + b + 1)
                    act.activation(pre[:, :, NVH:], pre[:, :, NVH:], ACT.Ln, bias=1.0).then_inc(s_l1, 1)
                    act.wait_ge(s_added, 1 + b * TPB)

                    def exps(w_):
                        for s, u, _ in pair_of(w_):
                            act.wait_ge(s_dt, 1 + b * U + u + 1)
                            act.activation(gmt[s][w_ % 3], four(bank(s, 2)), ACT.Exp).then_inc(s_exp, 1)

                    def empty(n):
                        what, t, _ = TURNS[n]
                        act.wait_ge(s_turned, 1 + b * len(TURNS) + n + 1)
                        if what == "back":
                            act.copy(cT[:, NQT:2 * NQT, P * t:P * t + P], four(g.bank[4 + n % 2])).then_inc(s_backA, 1)
                        else:
                            act.copy(vtok[:, t, 512 * what:512 * what + 512], g.bank[4 + n % 2][:]).then_inc(s_backA, 1)

                    for p in range(NP2 + 1):
                        if p < NP2:
                            act.wait_ge(s_pair, 1 + b * NP2 + p + 1)
                            for i in range(2):
                                ins = act.activation(cT[:, 2 * p + i, :], g.bank[p % 2][:, T * i:T * i + T], ACT.Copy,
                                                     scale=taps[:, 2 * p + i, TAPS - 1:TAPS])
                            ins.then_inc(s_tap0, 1)
                        if p >= 1:
                            act.wait_ge(s_conv, 1 + b * NP2 + p)
                            act.activation(cT[:, 2 * p - 2:2 * p, :], cT[:, 2 * p - 2:2 * p, :], ACT.Silu).then_inc(s_silu, 1)
                        if NP2 - NZ <= p < NP2:
                            n = p - (NP2 - NZ)
                            t, m = divmod(n, VD // 512)
                            act.wait_ge(s_z, 1 + b * NZ + n + 1)
                            act.activation(zs[:, t, 512 * m:512 * m + 512], g.bank[6 + n % 2][:], ACT.Silu).then_inc(s_zkept, 1)
                        if p == 3:
                            act.wait_ge(s_cum, 1 + b + 1)
                            act.activation(decay[:], g.bank[7][:, 0:4 * NVH].rearrange("p (c i h) -> p c i h", c=TPB, i=2),
                                           ACT.Exp).then_inc(s_decay, 1)
                            exps(0)
                        if p == 8:
                            act.wait_ge(s_ssk, 1 + b + 1)
                            act.activation(nrm[:], nrm[:], ACT.Sqrt).then_inc(s_nrm, 1)
                        if p == 9:
                            empty(2)
                            empty(3)
                        if p == 10:
                            empty(4)
                            empty(5)
                        if p == 11:
                            empty(6)

                    def rounded(w_):
                        for s, u, _ in pair_of(w_):
                            act.wait_ge(s_nt, 1 + b * U + u + 1)
                            act.copy(ntH[s][w_ % 2][:], nt[s][:]).then_inc(s_nth, 1)

                    def begun(w_):
                        for s, u, _ in pair_of(w_):
                            act.wait_ge(s_t0, 1 + b * U + u + 1)
                            act.copy(tri[s][w_ % 2][:], four(bank(s, 2))).then_inc(s_t0kept, 1)

                    def squares(w_):
                        t, r = divmod(w_, 2)
                        act.wait_ge(s_okept, 1 + b * U + 2 * w_ + 2)
                        act.wait_ge(s_oss, 1 + b * W + max(w_ - 1, 0))
                        act.activation(osq[:, r, :], vtok[:, t, 1024 * r:1024 * r + 1024], ACT.Square).then_inc(s_osq, 1)

                    def gempty(n):
                        m, t, _ = GTURNS[n]
                        act.wait_ge(s_gturned, 1 + b * len(GTURNS) + n + 1)
                        act.activation(gT[:, 4 * m:4 * m + 4, P * t:P * t + P], four(g.bank[n % 2]), ACT.Copy, scale=norm_w[:, 0:1]).then_inc(s_gbackA, 1)

                    empty(8)
                    rounded(0)
                    empty(10)
                    begun(0)
                    for w_ in range(W):
                        for l in range(NL):
                            for s in range(2):
                                act.wait_ge(s_p, 1 + b * U * NL + atp(w_, l, s) + 1)
                                act.copy(tri[s][w_ % 2][:], four(bank(s, 0))).then_inc(s_pkept, 1)
                                act.wait_ge(s_pt, 1 + b * U * NS + at(w_, l, s) + 1)
                                act.copy(triT[s][w_ % 2][:], four(bank(s, 1))).then_inc(s_ptkept, 1)
                            if w_ < W - 1 and l == 0:
                                exps(w_ + 1)
                            if w_ < W - 1 and l == NL - 1:
                                rounded(w_ + 1)
                            if w_ and l == 4:
                                squares(w_ - 1)
                            if w_ == W - 1 and l == 0:
                                act.wait_ge(s_oss, 1 + b * W + W // 2)
                                act.activation(osd[:, 0, :], oss[:, 0, :], ACT.Sqrt, scale=1.0 / DV, bias=g.eps6[:, 0:1]).then_inc(s_osd, 1)
                        if w_ < W - 1:
                            begun(w_ + 1)
                        for s in range(2):
                            act.wait_ge(s_pt, 1 + b * U * NS + at(w_, NL, s) + 1)
                            act.copy(fine[s][:], four(bank(s, 1))).then_inc(s_ptkept, 1)
                    for n in range(4):
                        gempty(n)
                    squares(W - 1)
                    act.wait_ge(s_oss, 1 + b * W + W)
                    act.activation(osd[:, 1, :], oss[:, 1, :], ACT.Sqrt, scale=1.0 / DV, bias=g.eps6[:, 0:1]).then_inc(s_osd, 1)
                    for n in (4, 6):
                        gempty(n)

            @block.gpsimd
            def _(pool):
                pool.wait_ge(s_wz, 1 + N2)
                with pool.Fori(0, B) as b:
                    for w_ in range(W):
                        c, r = w_ // 2, w_ % 2
                        if w_ == 0:
                            pool.wait_ge(s_gg, 1 + b + 1)
                        for s, u, hg in pair_of(w_):
                            pool.wait_ge(s_dt, 1 + b * U + max(u - 1, 0))
                            pool.tensor_tensor(mg[s][:], after[:].unsqueeze(1).to_broadcast([P, HG, P]),
                                               gg[:, c, HG * hg:HG * hg + HG].unsqueeze(2).to_broadcast([P, HG, P]),
                                               ALU.mult).then_inc(s_mg, 1)
                        for s, u, hg in pair_of(w_):
                            pool.wait_ge(s_exp, 1 + b * U + u + 1)
                            pool.tensor_tensor(nt[s][:], gmt[s][w_ % 3], before[:].unsqueeze(1).to_broadcast([P, HG, P]), ALU.mult).then_inc(s_gmown, 1)
                        if w_ == 0:
                            pool.wait_ge(s_silu, 1 + b * NP2 + NQT)
                            pool.tensor_tensor(sq[:], cT[:, 0:2 * NQT, :], cT[:, 0:2 * NQT, :], ALU.mult).then_inc(s_sq, 1)
                        for s, u, hg in pair_of(w_):
                            pool.wait_ge(s_gmown, 1 + b * U + u + 1)
                            pool.tensor_tensor(gmt[s][w_ % 3], gmt[s][w_ % 3], upto[:].unsqueeze(1).to_broadcast([P, HG, P]), ALU.mult).then_inc(s_gmu, 1)
                        for s, u, hg in pair_of(w_):
                            pool.wait_ge(s_nth, 1 + b * U + u + 1)
                            pool.tensor_tensor(ntL[s][r][:], nt[s][:], ntH[s][r][:], ALU.subtract).then_inc(s_gm, 1)
                    o = vtok[:, 0, :].rearrange("p (h d) -> p h d", d=DV)
                    pool.wait_ge(s_rstd, 1 + b + 1)
                    pool.tensor_tensor(o, o, orstd[:, 0, :].unsqueeze(2).to_broadcast([P, NVH, DV]), ALU.mult).then_inc(s_on, 1)
                    pool.wait_ge(s_on, 1 + b + 1)
                    pool.tensor_tensor(vtok[:, 0, :], vtok[:, 0, :], zs[:, 0, :], ALU.mult).then_inc(s_og, 1)

            @block.vector
            def _(dve):
                dve.wait_ge(s_w, 1 + N1)
                dve.wait_ge(s_aexp, 1 + 1)
                dve.tensor_copy(ident16[:], g.ident[:])
                dve.tensor_copy(ident4[:], g.ident[:].unsqueeze(1).to_broadcast([P, HG, P]))
                dve.tensor_scalar(minus16[:], g.ident[:], -1.0, None, ALU.mult)
                PER = 15 + 5 * NP2 + U
                with dve.Fori(0, B) as b:
                    own = Steps(dve, s_own, b, PER)

                    def step(ins):
                        own.then(ins)
                        own.wait()

                    dve.tensor_copy(xb[:], g.XT[:, :, bass.ts(b, T)]).then_inc(s_in, 1)
                    dve.wait_ge(s_ba, 1 + b + 1)
                    ba = g.bank[7][:, 0:2 * TPB * NVH].rearrange("p (t x) -> p t x", t=TPB)
                    y = pre[:, :, NVH:]
                    own.then(dve.tensor_copy(pre[:, :, 0:NVH], ba[:, :, 0:NVH]))
                    step(dve.tensor_tensor(y, ba[:, :, NVH:], dt_bias[:].unsqueeze(1).to_broadcast([P, TPB, NVH]), ALU.add))
                    step(dve.tensor_scalar(relu[:], y, 0.0, None, ALU.max))
                    step(dve.scalar_tensor_tensor(out=y, in0=relu[:], scalar=2.0, in1=y, op0=ALU.mult, op1=ALU.subtract))
                    dve.sem_inc(s_pre, 1)
                    dve.wait_ge(s_l1, 1 + b + 1)
                    step(dve.tensor_tensor(relu[:], relu[:], y, ALU.add))
                    step(dve.scalar_tensor_tensor(out=gg[:], in0=relu[:], scalar=-1.0,
                                                  in1=a_exp[:].unsqueeze(1).to_broadcast([P, TPB, NVH]), op0=ALU.mult, op1=ALU.mult))
                    dve.tensor_scalar(gg[:], gg[:], -1e30, None, ALU.max).then_inc(s_gg, 1)
                    step(dve.tensor_scalar(beta[:], pre[:, :, 0:NVH], 1.0, None, ALU.add))
                    step(dve.reciprocal(beta[:], beta[:]))
                    def by_head(x):
                        return x.unsqueeze(3).to_broadcast([P, TPB, NKH, REP])

                    def split(x):
                        return x.rearrange("p t (k r) -> p t k r", r=REP)

                    def empty(n):
                        what, t, _ = TURNS[n]
                        dve.wait_ge(s_turned, 1 + b * len(TURNS) + n + 1)
                        if what == "k":
                            dve.tensor_tensor(ktok[:, t, :].rearrange("p (k d) -> p k d", d=DK),
                                              g.bank[4 + n % 2][:].rearrange("p (k d) -> p k d", d=DK),
                                              rn[:, t, NKH:].unsqueeze(2).to_broadcast([P, NKH, DK]), ALU.mult).then_inc(s_backD, 1)
                        else:
                            dve.tensor_copy(vtok[:, t, 512 * what:512 * what + 512], g.bank[4 + n % 2][:]).then_inc(s_backD, 1)

                    for p in range(NP2):
                        dve.wait_ge(s_tap0, 1 + b * NP2 + p + 1)
                        for k in range(1, TAPS):
                            for i in range(2):
                                m = 2 * p + i
                                if k > 1:
                                    own.wait(own.n - 1)
                                ins = dve.scalar_tensor_tensor(
                                    out=cT[:, m, k:T], in0=g.bank[p % 2][:, T * i:T * i + T - k],
                                    scalar=taps[:, m, TAPS - 1 - k:TAPS - k], in1=cT[:, m, k:T], op0=ALU.mult, op1=ALU.add)
                                if k < TAPS - 1 or i == 0:
                                    own.then(ins)
                                else:
                                    ins.then_inc(s_conv, 1)
                        if p == 7:
                            dve.wait_ge(s_ss, 1 + b + 1)
                            dve.tensor_scalar(nrm[:], g.bank[2][:, 0:2 * TPB * NKH].rearrange("p (t x) -> p t x", t=TPB),
                                              1e-24, None, ALU.max).then_inc(s_ssk, 1)
                        if p == 8:
                            dve.wait_ge(s_nrm, 1 + b + 1)
                            step(dve.reciprocal(rn[:], nrm[:]))
                            empty(0)
                            empty(1)
                    empty(7)
                    dve.wait_ge(s_decay, 1 + b + 1)
                    own.then(dve.tensor_scalar(nbk[:], beta[:], -1.0, None, ALU.mult))
                    own.then(dve.tensor_tensor(bks[:], beta[:], decay[:, :, 1, :], ALU.mult))
                    own.then(dve.tensor_scalar(ngam[:], decay[:, :, 0, :], -1.0, None, ALU.mult))
                    step(dve.tensor_scalar(split(rqs[:]), by_head(rn[:, :, 0:NKH]), DK ** -0.5, None, ALU.mult))
                    own.then(dve.tensor_tensor(grq[:], decay[:, :, 0, :], rqs[:], ALU.mult))
                    own.wait()

                    def wide(x, c, hg):
                        return x[:, c, HG * hg:HG * hg + HG].unsqueeze(2).to_broadcast([P, HG, P])

                    def couplings(w_):
                        c = w_ // 2
                        for s, u, hg in pair_of(w_):
                            dve.wait_ge(s_gmown, 1 + b * U + u + 1)
                            dve.wait_ge(s_kkq, 1 + b * U + u + 1)
                            for h in range(HG):
                                ins = dve.scalar_tensor_tensor(out=nt[s][:, h, :], in0=bank(s, 2 + h // 2)[:, P:2 * P],
                                                               scalar=nbk[:, c, HG * hg + h:HG * hg + h + 1], in1=nt[s][:, h, :],
                                                               op0=ALU.mult, op1=ALU.mult)
                            ins.then_inc(s_nt, 1)

                    def scores(w_):
                        for s, u, hg in pair_of(w_):
                            dve.wait_ge(s_gmu, 1 + b * U + u + 1)
                            e = gmt[s][w_ % 3].rearrange("p (k r) i -> p k r i", k=2)
                            for k in range(2):
                                dve.tensor_tensor(e[:, k], bank(s, 2 + k)[:, 0:P].unsqueeze(1).to_broadcast([P, REP, P]),
                                                  e[:, k], ALU.mult)

                    def starts(w_):
                        for s, u, hg in pair_of(w_):
                            dve.wait_ge(s_nt, 1 + b * U + u + 1)
                            own.then(dve.tensor_tensor(triT[s][w_ % 2][:], nt[s][:], first[:].unsqueeze(1).to_broadcast([P, HG, P]), ALU.mult))
                        for s, u, hg in pair_of(w_):
                            own.wait(own.n - 1 + s)
                            dve.tensor_tensor(triT[s][w_ % 2][:], triT[s][w_ % 2][:], g.ident[:].unsqueeze(1).to_broadcast([P, HG, P]),
                                              ALU.add).then_inc(s_tinit, 1)

                    def kept(w_, which=(0, 1)):
                        for s, u, hg in (pair_of(w_)[n] for n in which):
                            c = w_ // 2
                            dve.wait_ge(s_o, 1 + b * U + u + 1)
                            out = vtok[:, c, 512 * hg:512 * hg + 512].rearrange("p (h d) -> p h d", h=HG)
                            if c == 0:
                                dve.tensor_tensor(out, four(bank(s, 3)), wide(rqs, c, hg), ALU.mult).then_inc(s_okept, 1)
                                dve.wait_ge(s_s, 1 + b * NG + hg + 1)
                                dve.tensor_copy(state[:, hg, :], bank(s, 2)[:, 0:2 * P]).then_inc(s_skept, 1)
                            else:
                                for h in range(HG):
                                    ins = dve.scalar_tensor_tensor(out=out[:, h, :], in0=bank(s, 3)[:, P * h:P * h + P],
                                                                   scalar=rqs[:, c, HG * hg + h:HG * hg + h + 1], in1=aux[s][:, h, :],
                                                                   op0=ALU.mult, op1=ALU.add)
                                ins.then_inc(s_okept, 1)

                    def sums(w_):
                        t, r = divmod(w_, 2)
                        dve.wait_ge(s_osq, 1 + b * W + w_ + 1)
                        dve.tensor_reduce(oss[:, t, 8 * r:8 * r + 8], osq[:, r, :].rearrange("p (h d) -> p h d", d=DV), AX.X,
                                          ALU.add).then_inc(s_oss, 1)

                    def differences(w_):
                        for s, u, hg in pair_of(w_):
                            dve.wait_ge(s_ks, 1 + b * NG + hg + 1)
                            for h in range(HG):
                                ins = dve.scalar_tensor_tensor(out=upd[s][:, h, :], in0=bank(s, 2 + h // 2)[:, P * (h % 2):P * (h % 2) + P],
                                                               scalar=ngam[:, 1, HG * hg + h:HG * hg + h + 1],
                                                               in1=vtok[:, 1, P * (HG * hg + h):P * (HG * hg + h) + P],
                                                               op0=ALU.mult, op1=ALU.add)
                            for k in range(2):
                                ins = dve.tensor_tensor(aux[s][:, 2 * k:2 * k + 2, :],
                                                        bank(s, 2 + k)[:, 2 * P:4 * P].rearrange("p (h d) -> p h d", h=2),
                                                        wide(grq, 1, hg)[:, 2 * k:2 * k + 2, :], ALU.mult)
                            ins.then_inc(s_r, 1)

                    def updates(w_, which=(0, 1)):
                        c = w_ // 2
                        for s, u, hg in (pair_of(w_)[n] for n in which):
                            dve.wait_ge(s_w_, 1 + b * U + u + 1)
                            if c == 0:
                                dve.tensor_tensor(aux[s][:], four(bank(s, 2)), wide(bks, c, hg), ALU.mult)
                            dve.tensor_tensor(upd[s][:], four(bank(s, 2)), wide(beta, c, hg), ALU.mult).then_inc(s_u, 1)

                    couplings(0)
                    empty(9)
                    dve.wait_ge(s_wr, 1 + N3)
                    scores(0)
                    starts(0)
                    empty(11)
                    for w_ in range(W):
                        for l in range(NL):
                            for s in range(2):
                                dve.wait_ge(s_x, 1 + b * U * NS + at(w_, l, s) + 1)
                                dve.tensor_tensor(xm[s][:], four(bank(s, 0)), lvl[:, l, :].unsqueeze(1).to_broadcast([P, HG, P]),
                                                  ALU.mult).then_inc(s_xkept, 1)
                            late = 1 if w_ > W // 2 else 0
                            if w_:
                                if late and l == 1:
                                    differences(w_ - 1)
                                if l == 1 + late:
                                    updates(w_ - 1, (0,))
                                if l == 2 + late:
                                    updates(w_ - 1, (1,))
                                    kept(w_ - 1, (0,))
                                if l == 3 + late:
                                    kept(w_ - 1, (1,))
                            if w_ == W - 1 and l == 1:
                                dve.wait_ge(s_osd, 1 + b * TPB + 1)
                                dve.reciprocal(orstd[:, 0, :], osd[:, 0, :]).then_inc(s_rstd, 1)
                            if w_ < W - 1:
                                if l == 4:
                                    couplings(w_ + 1)
                                    scores(w_ + 1)
                                if l == NL - 1:
                                    starts(w_ + 1)
                        for s in range(2):
                            dve.wait_ge(s_x, 1 + b * U * NS + at(w_, NL, s) + 1)
                            dve.tensor_copy(xm[s][:], four(bank(s, 0))).then_inc(s_xkept, 1)
                        if w_:
                            sums(w_ - 1)
                    differences(W - 1)
                    updates(W - 1)
                    kept(W - 1)
                    sums(W - 1)
                    dve.wait_ge(s_osd, 1 + b * TPB + 2)
                    step(dve.reciprocal(orstd[:, 1, :], osd[:, 1, :]))
                    for h in range(NVH):
                        o = vtok[:, 1, DV * h:DV * h + DV]
                        ins = dve.scalar_tensor_tensor(out=o, in0=o, scalar=orstd[:, 1, h:h + 1], in1=zs[:, 1, DV * h:DV * h + DV],
                                                       op0=ALU.mult, op1=ALU.mult)
                        if h % 4 == 3:
                            ins.then_inc(s_og1, 1)
                    for n, (m, t, eng) in enumerate(GTURNS):
                        if eng == "D":
                            dve.wait_ge(s_gturned, 1 + b * len(GTURNS) + n + 1)
                            dve.tensor_scalar(gT[:, 4 * m:4 * m + 4, P * t:P * t + P], four(g.bank[n % 2]), norm_w[:, 0:1], None, ALU.mult).then_inc(s_gbackD, 1)
                    for t in range(TPB):
                        dve.wait_ge(s_out, 1 + b * TPB + t + 1)
                        tile = g.X[:, bass.ds(b * TPB + t, 1), :]
                        dve.tensor_tensor(tile, g.bank[4 + t][:, 0:C].unsqueeze(1), tile, ALU.add).then_inc(s_added, 1)
                    own.end()


E1, TOP1, CAP = 32, 4, 32
F1, FS = 176, 704
GRP = P // CAP
NGRP = E1 // GRP
NFS = -(-FS // P)


def experts1(nc, g, a):
    HALF, FH = 512, F1 // 2
    NSLOT = E1 * CAP
    NB = 3
    with ExitStack() as ctx:
        def sb(n, shape, dt=F32):
            return ctx.enter_context(nc.sbuf_tensor(f"e1_{n}", shape, dt))

        def sem(n):
            return g.sem(f"e1_{n}")

        combine, chosen = sb("combine", [P, NT, E1]), sb("chosen", [P, NT, E1])
        combineP = sb("combineP", [P, NT, 2, E1], F16)
        before, before16, ones = sb("before", [P, P]), sb("before16", [P, P], F16), sb("ones", [P, P], F16)
        chosen16 = sb("chosen16", [P, NT, E1], F16)
        place = sb("place", [P, NT, E1])
        iota, sel = sb("iota", [P, CAP]), sb("sel", [P, NGRP, E1])
        ident16 = sb("ident16", [P, P], F16)
        wsgu, wsd, wse = sb("wsgu", [P, KC, 2 * FS]), sb("wsd", [P, NFS, C]), sb("wse", [P, KC, 1])
        share = sb("share", [P, NT])
        silu = sb("silu", [P, 2, HALF])
        act_ = sb("act", [P, 2, NFS, HALF])
        gate = sb("gate", [P, 2, NSLOT], F16)
        gateT = sb("gateT", [P, NGRP, NTOK], F16)
        xP = [sb(f"x{x}", [P, NT, C], F16) for x in "HL"]
        xeT = sb("xeT", [P, KC, NSLOT])
        picked, slotw = sb("picked", [P, NGRP, 2, E1]), sb("slotw", [P, NGRP])
        wgu = [sb(f"wgu{i}", [P, GRP, KC, 2 * F1]) for i in range(NB)]
        wd = [sb(f"wd{i}", [FH, GRP, 2, C]) for i in range(NB)]
        esilu, eact, eactT = sb("esilu", [P, F1]), sb("eact", [P, F1]), sb("eactT", [FH, 2, P])
        ye = sb("ye", [P, NGRP, C])
        yeP = [sb(f"ye{x}", [P, NGRP, C], F16) for x in "HL"]
        s_ones = sem("ones")
        s_w, s_ws, s_const, s_place, s_own, s_pos = sem("w"), sem("ws"), sem("const"), sem("place"), sem("own"), sem("pos")
        s_ew = [sem(f"ew{i}") for i in range(NB)]
        s_share, s_sgu, s_ssilu, s_sact, s_sdown, s_sadd = sem("share"), sem("sgu"), sem("ssilu"), sem("sact"), sem("sdown"), sem("sadd")
        s_hi, s_lo, s_gate, s_disp, s_turned, s_back = sem("hi"), sem("lo"), sem("gate"), sem("disp"), sem("turned"), sem("back")
        s_xe, s_slotw, s_egu, s_esilu, s_eact = sem("xe"), sem("slotw"), sem("egu"), sem("esilu"), sem("eact")
        s_eturned, s_eback, s_edown, s_ye = sem("eturned"), sem("eback"), sem("edown"), sem("ye")
        s_yehi, s_yelo, s_comb = sem("yehi"), sem("yelo"), sem("comb")
        widths = [min(P, FS - P * f) for f in range(NFS)]
        PIECES = [(0, f) for f in range(NFS)] + [(1, 0), (0, None, 0), (0, None, 1)] + [(1, f) for f in range(1, NFS)]
        PIECES += [(1, None, 0), (1, None, 1)]
        BY = len(PIECES) // NGRP

        def load(sp, k):
            i = k % NB
            sp.dma_start(wgu[i][:], a["L1_wgu"][k]).then_inc(s_ew[i], 16)
            sp.dma_start(wd[i][:], a["L1_wd"][k]).then_inc(s_ew[i], 16)

        def first_loads(sp):
            for tile, name in ((before, "before"), (wse, "L1_wse"), (sel, "sel")):
                sp.dma_start(tile[:], a[name]).then_inc(s_w, 16)
            load(sp, 0)
            for tile, name in ((wsgu, "L1_wsgu"), (wsd, "L1_wsd")):
                sp.dma_start(tile[:], a[name]).then_inc(s_ws, 16)
            for k in range(1, NB):
                load(sp, k)

        def highs(act):
            act.copy(xP[0][:], g.X[:]).then_inc(s_hi, 1)

        top_weights(nc, g, "r1", E1, TOP1, a["L1_wr"], combine[:], chosen[:], ahead=first_loads, split=highs)
        with nc.Block() as block:
            @block.sync
            def _(sp):
                for k in range(NB, NGRP):
                    sp.wait_ge(s_edown, 1 + k - NB + 1)
                    load(sp, k)

            @block.gpsimd
            def _(pool):
                pool.iota(iota[:], [[1, CAP]], base=0, channel_multiplier=0, allow_small_or_imprecise_dtypes=True).then_inc(s_const, 1)
                pool.memset(ones[:], 1.0).then_inc(s_const, 1)

            @block.tensor
            def _(pe):
                pe.wait_ge(s_const, 1 + 2)
                pe.wait_ge(s_w, 1 + 48)
                pe.wait_ge(s_ones, 1 + 2)
                for t in range(NT):
                    for i in range(t + 1):
                        mm = pe.matmul(g.bank[0][:, E1 * t:E1 * t + E1], before16[:] if i == t else ones[:], chosen16[:, i, :],
                                       start=(i == 0), stop=(i == t))
                mm.then_inc(s_pos, 1)

                for t in range(NT):
                    for j in range(KC):
                        mm = pe.matmul(g.bank[6][:, t:t + 1], g.XT[:, j, P * t:P * t + P], wse[:, j, :], start=(j == 0), stop=(j == KC - 1))
                mm.then_inc(s_share, 1)

                pe.wait_ge(s_place, 1 + 1)
                pe.wait_ge(s_lo, 1 + 3)
                for t in range(NT):
                    pe.wait_ge(s_gate, 1 + t + 1)
                    for n in range(2):
                        if t:
                            pe.wait_ge(s_back, 1 + 2 * t + n - 1)
                        for i in range(4):
                            mm = pe.matmul(g.bank[(0, 7)[n]][:, P * i:P * i + P], gate[:, t % 2, P * (4 * n + i):P * (4 * n + i) + P],
                                           ident16[:], start=True, stop=True)
                        mm.then_inc(s_turned, 1)
                    for k in range(NGRP):
                        pe.matmul(g.bank[5][:, 2 * E1 * k:2 * E1 * k + 2 * E1], gate[:, t % 2, P * k:P * k + P], combineP[:, t, :, :],
                                  start=(t == 0 and k == 0), stop=(t == NT - 1 and k == NGRP - 1))
                    for j in range(KC):
                        for n in range(2):
                            for part in range(2):
                                mm = pe.matmul(g.bank[1 + 2 * j + n][:], xP[part][:, t, P * j:P * j + P],
                                               gate[:, t % 2, HALF * n:HALF * n + HALF],
                                               start=(t == 0 and part == 0), stop=(t == NT - 1 and part == 1))
                            mm.then_inc(s_disp, 1)

                def shared(piece):
                    n = piece[0]
                    if len(piece) == 2:
                        u = n * NFS + piece[1]
                        f = piece[1]
                        if u >= 2:
                            pe.wait_ge(s_sact, 1 + u - 1)
                        for part in range(2):
                            for j in range(KC):
                                mm = pe.matmul(g.bank[1 + 2 * (u % 2) + part][0:widths[f], :],
                                               wsgu[:, j, FS * part + P * f:FS * part + P * f + widths[f]],
                                               g.XT[:, j, HALF * n:HALF * n + HALF], start=(j == 0), stop=(j == KC - 1))
                            mm.then_inc(s_sgu, 1)
                    else:
                        q = piece[2]
                        d = 2 * n + q
                        pe.wait_ge(s_sact, 1 + (n + 1) * NFS)
                        if d >= 2:
                            pe.wait_ge(s_sadd, 1 + d - 1)
                        for t in range(2):
                            for f in range(NFS):
                                mm = pe.matmul(g.bank[5 + d % 2][:, C * t:C * t + C],
                                               act_[0:widths[f], n, f, P * (2 * q + t):P * (2 * q + t) + P],
                                               wsd[0:widths[f], f, :], start=(f == 0), stop=(f == NFS - 1))
                        mm.then_inc(s_sdown, 1)

                pe.wait_ge(s_ws, 1 + 32)
                pe.wait_ge(s_xe, 1 + 4)
                pe.wait_ge(s_slotw, 1 + 1)
                pe.wait_ge(s_share, 1 + 2)
                pe.wait_ge(s_back, 1 + 2 * NT)
                for k in range(NGRP):
                    i = k % NB
                    pe.wait_ge(s_ew[i], 1 + 32 * (k // NB) + 32)
                    if k:
                        pe.wait_ge(s_eact, 1 + k)
                    for e in range(GRP):
                        for j in range(KC):
                            mm = pe.matmul(g.bank[0][CAP * e:CAP * e + CAP, 0:2 * F1], xeT[:, j, P * k + CAP * e:P * k + CAP * e + CAP],
                                           wgu[i][:, e, j, :], start=(j == 0), stop=(j == KC - 1), tile_position=(0, CAP * e))
                    mm.then_inc(s_egu, 1)
                    shared(PIECES[BY * k])
                    pe.wait_ge(s_eact, 1 + k + 1)
                    if k:
                        pe.wait_ge(s_ye, 1 + k)
                    for f in range(2):
                        mm = pe.transpose(g.bank[7][0:FH, P * f:P * f + P], eact[:, FH * f:FH * f + FH], g.ident[:])
                    mm.then_inc(s_eturned, 1)
                    shared(PIECES[BY * k + 1])
                    pe.wait_ge(s_eback, 1 + k + 1)
                    for e in range(GRP):
                        for f in range(2):
                            mm = pe.matmul(g.bank[7][CAP * e:CAP * e + CAP, 0:C], eactT[:, f, CAP * e:CAP * e + CAP],
                                           wd[i][:, e, f, :], start=(f == 0), stop=(f == 1), tile_position=(0, CAP * e))
                    mm.then_inc(s_edown, 1)

                pe.wait_ge(s_yelo, 1 + NGRP)
                for t in range(NT):
                    for part in range(2):
                        for k in range(NGRP):
                            mm = pe.matmul(g.bank[1 + t % 4][:, C * (t // 4):C * (t // 4) + C], gateT[:, k, P * t:P * t + P],
                                           yeP[part][:, k, :], start=(part == 0 and k == 0), stop=(part == 1 and k == NGRP - 1))
                    if t >= 4:
                        mm.then_inc(s_comb, 1)

            @block.scalar
            def _(act):
                act.wait_ge(s_w, 1 + 48)
                act.copy(before16[:], before[:]).then_inc(s_ones, 1)
                act.copy(combineP[:, :, 0, :], combine[:]).then_inc(s_hi, 1)
                act.copy(ident16[:], g.ident[:]).then_inc(s_lo, 1)
                act.wait_ge(s_share, 1 + 1)
                act.activation(share[:], g.bank[6][:, 0:NT], ACT.Sigmoid).then_inc(s_share, 1)
                for t in range(NT):
                    for n in range(2):
                        act.wait_ge(s_turned, 1 + 2 * t + n + 1)
                        act.copy(gateT[:, 4 * n:4 * n + 4, P * t:P * t + P],
                                 g.bank[(0, 7)[n]][:].rearrange("p (i t) -> p i t", i=4)).then_inc(s_back, 1)

                def shared(piece):
                    if len(piece) == 2:
                        u = piece[0] * NFS + piece[1]
                        w = widths[piece[1]]
                        act.wait_ge(s_sgu, 1 + 2 * u + 1)
                        if u >= 2:
                            act.wait_ge(s_sact, 1 + u - 1)
                        act.activation(silu[0:w, u % 2, :], g.bank[1 + 2 * (u % 2)][0:w, :], ACT.Silu).then_inc(s_ssilu, 1)

                for k in range(NGRP):
                    act.wait_ge(s_egu, 1 + k + 1)
                    if k:
                        act.wait_ge(s_eact, 1 + k)
                    act.activation(esilu[:], g.bank[0][:, 0:F1], ACT.Silu).then_inc(s_esilu, 1)
                    shared(PIECES[BY * k])
                    shared(PIECES[BY * k + 1])
                    act.wait_ge(s_slotw, 1 + 1)
                    act.wait_ge(s_edown, 1 + k + 1)
                    act.activation(ye[:, k, :], g.bank[7][:, 0:C], ACT.Copy, scale=slotw[:, k:k + 1]).then_inc(s_ye, 1)
                    act.wait_ge(s_ye, 1 + k + 1)
                    act.copy(yeP[0][:, k, :], ye[:, k, :]).then_inc(s_yehi, 1)

            @block.vector
            def _(dve):
                own = Steps(dve, s_own)
                dve.tensor_copy(chosen16[:], chosen[:]).then_inc(s_ones, 1)
                dve.wait_ge(s_hi, 1 + 2)
                dve.tensor_tensor(combineP[:, :, 1, :], combine[:], combineP[:, :, 0, :], ALU.subtract).then_inc(s_lo, 1)
                dve.wait_ge(s_pos, 1 + 1)
                own.then(dve.tensor_scalar(place[:], chosen[:], -1e4, 1e4, ALU.mult, ALU.add))
                own.wait()
                dve.tensor_tensor(place[:], place[:], g.bank[0][:, 0:NT * E1].rearrange("p (t e) -> p t e", t=NT),
                                  ALU.add).then_inc(s_place, 1)
                dve.wait_ge(s_place, 1 + 1)
                dve.wait_ge(s_const, 1 + 2)
                for t in range(NT):
                    if t >= 2:
                        dve.wait_ge(s_disp, 1 + 4 * (t - 1))
                    dve.tensor_tensor(gate[:, t % 2, :].rearrange("p (e s) -> p e s", e=E1),
                                      place[:, t, :].unsqueeze(2).to_broadcast([P, E1, CAP]),
                                      iota[:].unsqueeze(1).to_broadcast([P, E1, CAP]), ALU.is_equal).then_inc(s_gate, 1)
                    if t == 0:
                        dve.tensor_tensor(xP[1][:], g.X[:], xP[0][:], ALU.subtract).then_inc(s_lo, 1)
                for j in range(KC):
                    for n in range(2):
                        dve.wait_ge(s_disp, 1 + 4 * (NT - 1) + 2 * j + n + 1)
                        dve.tensor_copy(xeT[:, j, HALF * n:HALF * n + HALF], g.bank[1 + 2 * j + n][:]).then_inc(s_xe, 1)
                own.then(dve.tensor_tensor(picked[:], g.bank[5][:].rearrange("p (k a e) -> p k a e", k=NGRP, a=2),
                                           sel[:].unsqueeze(2).to_broadcast([P, NGRP, 2, E1]), ALU.mult))
                own.wait()
                dve.tensor_reduce(slotw[:], picked[:].rearrange("p k a e -> p k (a e)"), AX.X, ALU.add).then_inc(s_slotw, 1)
                dve.wait_ge(s_share, 1 + 2)

                def shared(piece):
                    n = piece[0]
                    if len(piece) == 2:
                        f = piece[1]
                        u = n * NFS + f
                        dve.wait_ge(s_sgu, 1 + 2 * u + 2)
                        dve.wait_ge(s_ssilu, 1 + u + 1)
                        dve.tensor_tensor(act_[0:widths[f], n, f, :], g.bank[2 + 2 * (u % 2)][0:widths[f], :],
                                          silu[0:widths[f], u % 2, :], ALU.mult).then_inc(s_sact, 1)
                    else:
                        d = 2 * n + piece[2]
                        dve.wait_ge(s_sdown, 1 + d + 1)
                        for t in range(2):
                            tt = 2 * d + t
                            ins = dve.scalar_tensor_tensor(out=g.X[:, tt, :], in0=g.bank[5 + d % 2][:, C * t:C * t + C],
                                                           scalar=share[:, tt:tt + 1], in1=g.X[:, tt, :], op0=ALU.mult, op1=ALU.add)
                        ins.then_inc(s_sadd, 1)

                def low(k):
                    dve.wait_ge(s_yehi, 1 + k + 1)
                    dve.tensor_tensor(yeP[1][:, k, :], ye[:, k, :], yeP[0][:, k, :], ALU.subtract).then_inc(s_yelo, 1)

                for k in range(NGRP):
                    dve.wait_ge(s_esilu, 1 + k + 1)
                    if k:
                        dve.wait_ge(s_eturned, 1 + k)
                    dve.tensor_tensor(eact[:], g.bank[0][:, F1:2 * F1], esilu[:], ALU.mult).then_inc(s_eact, 1)
                    if k:
                        low(k - 1)
                    shared(PIECES[BY * k])
                    dve.wait_ge(s_eturned, 1 + k + 1)
                    dve.tensor_copy(eactT[:], g.bank[7][0:FH, 0:2 * P].rearrange("p (f t) -> p f t", f=2)).then_inc(s_eback, 1)
                    shared(PIECES[BY * k + 1])
                low(NGRP - 1)
                for t in range(NT // 2):
                    dve.wait_ge(s_comb, 1 + t + 1)
                    for tt in (t, t + 4):
                        dve.tensor_tensor(g.X[:, tt, :], g.bank[1 + t][:, C * (tt // 4):C * (tt // 4) + C], g.X[:, tt, :], ALU.add)




SEMS = 80


def program(nc, a, out, first=0, last=6):
    with ExitStack() as ctx:
        def sb(name, shape, dt=F32):
            return ctx.enter_context(nc.sbuf_tensor(name, shape, dt))

        g = Shared(sb, lambda name, shape, dt: ctx.enter_context(nc.psum_tensor(name, shape, dt)),
                   lambda name: ctx.enter_context(nc.semaphore(name)))
        order = [("ident", g.ident), ("x", g.X), ("xT", g.XT), ("ctxT", g.ctxT)]
        s_load = g.sem("load")
        pool_of_sems = [g.sem(f"shared{n}") for n in range(SEMS)]
        with nc.Block() as block:
            @block.gpsimd
            def _(pool):
                for sem in pool_of_sems:
                    pool.sem_inc(sem, 1)

            @block.sync
            def _(sp):
                for n, (name, tile) in enumerate(order):
                    sp.dma_start(tile[:], a[name]).then_inc(s_load, 16)

            @block.vector
            def _(dve):
                dve.memset(g.eps_ln[:], LN_EPS)
                dve.memset(g.eps6[:], 1e-6)
                dve.wait_ge(s_load, 16 * len(order))
        subs = [
            lambda: attention(nc, g, "a0", True, a, "L0"),
            lambda: context_softmax(nc, g, a),
            lambda: experts0(nc, g, a),
            lambda: deltanet(nc, g, a),
            lambda: attention(nc, g, "a1", False, a, "L1"),
            lambda: experts1(nc, g, a),
        ]
        for n in range(first, last):
            used = []
            g.sem = lambda name: (used.append(pool_of_sems[len(used)]), used[-1])[1]
            subs[n]()
            layernorm(nc, g, n - first, used if n < last - 1 else [], out if n == last - 1 else None)


def arrays_of(i):
    import numpy as np

    def tiled(w):
        return np.ascontiguousarray(w.reshape(-1, P, w.shape[-1]).transpose(1, 0, 2))

    def rotated(wT):
        h = wT.reshape(-1, NH, 2, HD // 2)
        return h[:, :, ::-1, :].reshape(wT.shape)

    f = np.float32
    x = np.asarray(i["x"])
    a = {"x": tiled(x.reshape(NTOK, C)), "xT": tiled(x.reshape(NTOK, C).T), "ident": np.eye(P, dtype=f)}
    a["ctxT"] = np.ascontiguousarray(np.asarray(i["ctx_512"]).reshape(NTOK, CTX).T)
    wq, wk, wv, wo = (np.asarray(i["L0_attn_w_" + n]).T for n in "qkvo")
    a["L0_wq"], a["L0_wk"] = (tiled(np.concatenate([w, rotated(w)], axis=1)) for w in (wq, wk))
    a["L0_wv"], a["L0_wo"] = tiled(wv), tiled(wo)
    inv = (f(1.0) / f(10000.0) ** (np.arange(0, HD, 2, dtype=f) / f(HD))).astype(f)
    freq = np.outer(np.arange(T, dtype=f), inv).astype(f)
    cos, sin = np.cos(freq).T.astype(f), np.sin(freq).T.astype(f)
    rows = [np.tile(np.tile(np.concatenate(x), (P // HD, 1)), (1, 2)) for x in ([cos, cos], [-sin, sin])]
    a["rope"] = np.ascontiguousarray(np.stack(rows, axis=1))
    spread = np.zeros((P, 4, 4, P), f)
    for part, groups in enumerate(((0, 1), (2, 3), (0, 2), (1, 3))):
        for j in range(4):
            for e in range(2):
                for r in groups:
                    for d in range(HD):
                        spread[HD * (2 * j + e) + d, part, j, 64 * e + HD * r + d] = 1.0
    a["spread"] = spread
    qi, ki = np.arange(P)[:, None], np.arange(P)[None, :]
    zero = np.zeros((P, P), f)
    a["L0_mask"] = np.concatenate([zero, np.where(ki // 64 <= qi // 64, 0, MASKED).astype(f)], axis=1)
    a["L1_mask"] = np.concatenate([zero, np.where(ki <= qi, 0, MASKED).astype(f)], axis=1)
    a["L1_wq"] = tiled(np.asarray(i["L1_xattn_Wq"]).T)
    kv = np.asarray(i["L1_xattn_Wkv_expand"]).T
    a["L1_wk"] = np.ascontiguousarray(kv[:, :C])[:, None, :]
    a["L1_wv"] = np.ascontiguousarray(kv[:, C:])[:, None, :]
    a["L1_wo"] = tiled(np.asarray(i["L1_xattn_Wout"]).T)
    a["L0_Wk"] = np.ascontiguousarray(np.asarray(i["L0_xattn_W_k"]).T)
    a["L0_bk"], a["L0_gamma"], a["L0_beta"] = (np.asarray(i["L0_xattn_" + n]) for n in ("b_k", "ln_gamma", "ln_beta"))
    a["L0_gate"] = tiled(np.asarray(i["L0_ffn_gate_w"]))

    def experts(w, shared):
        w = np.concatenate([np.asarray(w), np.asarray(shared)[None]])
        return np.ascontiguousarray(w.reshape(w.shape[0], -1, P, w.shape[2]).transpose(0, 2, 1, 3))

    a["L0_wgu"] = experts(i["L0_ffn_w_gate_up"], i["L0_ffn_shared_gate_up"])
    a["L0_wd"] = experts(i["L0_ffn_w_down"], i["L0_ffn_shared_down"])
    a["L1_wr"] = tiled(np.asarray(i["L1_ffn_Wr"]))
    a["L1_wse"] = tiled(np.asarray(i["L1_ffn_Wse"]))
    a["L1_wsgu"] = tiled(np.concatenate([np.asarray(i["L1_ffn_Wsg"]), np.asarray(i["L1_ffn_Wsu"])], axis=1))
    wsd = np.asarray(i["L1_ffn_Wsd"])
    a["L1_wsd"] = tiled(np.concatenate([wsd, np.zeros((NFS * P - FS, C), f)]))
    gu = np.concatenate([np.asarray(i["L1_ffn_Wg"]), np.asarray(i["L1_ffn_Wu"])], axis=2)
    a["sel"] = (GRP * np.arange(NGRP)[None, :, None] + np.arange(P)[:, None, None] // CAP == np.arange(E1)).astype(f)
    a["L1_wgu"] = np.ascontiguousarray(gu.reshape(NGRP, GRP, KC, P, 2 * F1).transpose(0, 3, 1, 2, 4))
    a["L1_wd"] = np.ascontiguousarray(np.asarray(i["L1_ffn_Wd"]).reshape(NGRP, GRP, 2, F1 // 2, C).transpose(0, 3, 1, 2, 4))
    pw = np.asarray(i["L1_attn_in_proj_w"]).T
    n = NCT * P
    a["L1_w"], a["L1_wz"], a["L1_wba"] = tiled(pw[:, :n]), tiled(pw[:, n:n + VD]), tiled(pw[:, n + VD:])
    a["L1_taps"] = tiled(np.asarray(i["L1_attn_conv_w"]))
    a["L1_dt"], a["L1_alog"] = (np.asarray(i["L1_attn_" + n]) for n in ("dt_bias", "A_log"))
    a["L1_nw"] = np.asarray(i["L1_attn_norm_weight"]).reshape(P, 1)
    a["L1_wo2"] = tiled(np.asarray(i["L1_attn_out_proj_w"]).T)
    a["halves"] = (np.arange(P)[:, None] // DK == np.arange(2)[None, :]).astype(f)
    r, c = np.arange(P)[:, None], np.arange(P)[None, :]
    a["upto"], a["after"] = (r <= c).astype(f), (r > c).astype(f)
    fill = [(r // (2 * s) == c // (2 * s)) & (r % (2 * s) >= s) & (c % (2 * s) < s) for s in [1] + LEVELS]
    a["first"] = np.ascontiguousarray(fill[0].T).astype(f)
    a["lvl"] = np.stack([m | (r == c) for m in fill[1:]], axis=1).astype(f)
    a["before"] = (np.arange(P)[:, None] < np.arange(P)[None, :]).astype(f)
    return a


def kernel(**inputs):
    import numpy as _np
    import concourse.bacc as _bacc
    from concourse import mybir as _mybir
    from concourse.bass_utils import run_bass_kernel_spmd as _run

    nc = _bacc.Bacc("TRN2", target_bir_lowering=False, num_devices=1)
    arrays = arrays_of(inputs)
    aps = {n: nc.dram_tensor(f"in_{n}", a.shape, _mybir.dt.from_np(a.dtype), kind="ExternalInput").ap()
           for n, a in arrays.items()}
    out = nc.dram_tensor("out", (P, NT, C), F32, kind="ExternalOutput").ap()
    program(nc, aps, out)
    r = _run(nc, [{f"in_{n}": a for n, a in arrays.items()}], core_ids=[0])
    return r.results[0]["out"].transpose(1, 0, 2).reshape(B, T, C)
```
